# Optimizing a Trainium2 kernel written in Bass

```python
import numpy as np
import jax
import jax.numpy as jnp

def _softmax(x, axis=-1):
    return jax.nn.softmax(x, axis=axis)

def _gelu(x):
    return jax.nn.gelu(x, approximate=True)

def _silu(x):
    return jax.nn.silu(x)

def _sigmoid(x):
    return jax.nn.sigmoid(x)

def _layernorm(x, axis=-1, eps=1e-05):
    m = jnp.mean(x, axis=axis, keepdims=True)
    v = jnp.var(x, axis=axis, keepdims=True)
    return (x - m) / jnp.sqrt(v + eps)

def _scatter_add(tgt, idx, src, axis=0):
    return tgt.at[idx].add(src)

def _segment_sum(src, seg, n):
    return jax.ops.segment_sum(src, seg, n)
kernel_name = 'mk_xattn_ffn_d2_seqx_r8_a0d6be'

def setup_inputs(seed: int=0):
    np.random.seed(seed)
    _w = jnp.asarray

    def _rec_inputs():
        import jax
        import jax.numpy as jnp
        _rk = jax.random.key(seed)
        x = -0.0002928 + 1 * jax.random.normal(jax.random.fold_in(_rk, 1), (32, 64, 256), jnp.float32)
        _lenS = 64 - jax.random.randint(jax.random.fold_in(_rk, 7), (32,), 0, max(1, 64 // 4) + 1, jnp.int32)
        _lenS2 = 64 - jax.random.randint(jax.random.fold_in(_rk, 8), (32,), 0, max(1, 64 // 4) + 1, jnp.int32)
        _ctx_2048P = jax.random.normal(jax.random.fold_in(_rk, 11), (32, 16, 256), jnp.float32)
        _ctx_2048c = jax.random.dirichlet(jax.random.fold_in(_rk, 511), 0.3 * jnp.ones((16,), jnp.float32), (32, 64))
        _ctx_2048t = jnp.einsum('bsk,bkd->bsd', _ctx_2048c, _ctx_2048P)
        _ctx_2048t = _ctx_2048t * jax.lax.rsqrt(jnp.mean(jnp.square(_ctx_2048t)) + 1e-12) * 0.953939
        ctx_2048 = -1.39393e-06 + 0.999914 * (_ctx_2048t + 0.3 * jax.random.normal(jax.random.fold_in(_rk, 611), (32, 64, 256), jnp.float32))
        return (x, ctx_2048)
    x, ctx_2048 = _rec_inputs()

    def _L0_xattn_setup():
        import jax, jax.numpy as jnp
        import numpy as np
        DIM = 64
        CTX_DIM = 64
        NUM_HEADS = 8
        DIM_HEAD = 64
        INNER = NUM_HEADS * DIM_HEAD
        B, N, CTX_LEN = (4, 256, 256)
        key = jax.random.key(seed)
        ks = jax.random.split(key, 6)
        x = jax.random.normal(ks[0], (B, DIM, N), dtype=jnp.float32)
        context = jax.random.normal(ks[1], (B, CTX_DIM, CTX_LEN), dtype=jnp.float32)
        W_q = jax.random.normal(ks[2], (DIM, INNER), dtype=jnp.float32) / np.sqrt(DIM)
        W_kv = jax.random.normal(ks[3], (CTX_DIM, 2 * INNER), dtype=jnp.float32) / np.sqrt(CTX_DIM)
        W_out = jax.random.normal(ks[4], (INNER, DIM), dtype=jnp.float32) / np.sqrt(INNER)
        b_out = jax.random.normal(ks[5], (DIM,), dtype=jnp.float32) * 0.01
        return {'x': x, 'context': context, 'W_q': W_q, 'W_kv': W_kv, 'W_out': W_out, 'b_out': b_out}
    _L0_xattn_all = _L0_xattn_setup()
    _L0_xattn_in = {k: v for k, v in _L0_xattn_all.items() if k in ('W_q', 'W_kv', 'W_out', 'b_out')}
    del _L0_xattn_all

    def _L0_ffn_setup():
        import jax, jax.numpy as jnp
        import numpy as np
        B, S, D = (4, 256, 256)
        E = 8
        H = 352
        CAP_F = 1.0

        def _moe(x, Wg, W1, W3, W2, sw1, sw3, sw2):
            b, sl, d = x.shape
            T = b * sl
            C = int(CAP_F * T / E)
            xt = x.reshape(T, d)
            probs = jax.nn.softmax(xt @ Wg, axis=-1)
            eidx = jnp.argmax(probs, axis=-1)
            gate = jnp.take_along_axis(probs, eidx[:, None], 1)[:, 0]
            oh = jax.nn.one_hot(eidx, E, dtype=jnp.int32)
            pos = (jnp.cumsum(oh, axis=0) * oh).sum(-1) - 1
            keep = pos < C
            flat = jnp.where(keep, eidx * C + pos, E * C)
            xd = jnp.zeros((E * C, d), x.dtype).at[flat].set(xt, mode='drop')
            xd = xd.reshape(E, C, d)
            h = jax.nn.silu(jnp.einsum('ecd,edh->ech', xd, W1)) * jnp.einsum('ecd,edh->ech', xd, W3)
            oe = jnp.einsum('ech,ehd->ecd', h, W2).reshape(E * C, d)
            out = jnp.take(oe, jnp.minimum(flat, E * C - 1), axis=0)
            out = out * (gate * keep.astype(x.dtype))[:, None]
            shared = jax.nn.silu(xt @ sw1) * (xt @ sw3) @ sw2
            return (out + shared).reshape(b, sl, d)
        key = jax.random.key(seed)
        ks = jax.random.split(key, 8)
        s = lambda fan: 1.0 / np.sqrt(fan)
        return {'x': jax.random.normal(ks[0], (B, S, D), jnp.float32), 'Wg': jax.random.normal(ks[1], (D, E), jnp.float32) * s(D), 'W1': jax.random.normal(ks[2], (E, D, H), jnp.float32) * s(D), 'W3': jax.random.normal(ks[3], (E, D, H), jnp.float32) * s(D), 'W2': jax.random.normal(ks[4], (E, H, D), jnp.float32) * s(H), 'sw1': jax.random.normal(ks[5], (D, H), jnp.float32) * s(D), 'sw3': jax.random.normal(ks[6], (D, H), jnp.float32) * s(D), 'sw2': jax.random.normal(ks[7], (H, D), jnp.float32) * s(H)}
    _L0_ffn_all = _L0_ffn_setup()
    _L0_ffn_in = {k: v for k, v in _L0_ffn_all.items() if k in ('Wg', 'W1', 'W3', 'W2', 'sw1', 'sw3', 'sw2')}
    del _L0_ffn_all

    def _L1_xattn_setup():
        import jax, jax.numpy as jnp
        import numpy as np
        HIDDEN = 256
        NUM_HEADS = 16
        NUM_KV_HEADS = 4
        HEAD_DIM = 128
        ROPE_THETA = 10000.0
        EPS = 1e-06

        def rms_norm(x, w, eps=EPS):
            var = jnp.mean(jnp.square(x), axis=-1, keepdims=True)
            return x * jax.lax.rsqrt(var + eps) * w

        def rope_cache(L, head_dim, theta, dtype):
            inv_freq = 1.0 / theta ** (jnp.arange(0, head_dim, 2, dtype=jnp.float32) / head_dim)
            t = jnp.arange(L, dtype=jnp.float32)
            freqs = jnp.outer(t, inv_freq)
            emb = jnp.concatenate([freqs, freqs], -1)
            cos = jnp.cos(emb).astype(dtype)[None, :, None, :]
            sin = jnp.sin(emb).astype(dtype)[None, :, None, :]
            return (cos, sin)

        def rotate_half(x):
            x1, x2 = jnp.split(x, 2, axis=-1)
            return jnp.concatenate([-x2, x1], axis=-1)
        key = jax.random.key(seed)
        ks = jax.random.split(key, 10)
        B, L, T = (2, 256, 64)
        q_out = NUM_HEADS * HEAD_DIM
        kv_out = NUM_KV_HEADS * HEAD_DIM
        s = lambda fan_in: 1.0 / np.sqrt(fan_in)
        return {'x': jax.random.normal(ks[0], (B, L, HIDDEN), jnp.float32), 'h_ctx_kv': jax.random.normal(ks[1], (B, T, HIDDEN), jnp.float32), 'wq': jax.random.normal(ks[2], (HIDDEN, q_out), jnp.float32) * s(HIDDEN), 'wk': jax.random.normal(ks[3], (HIDDEN, kv_out), jnp.float32) * s(HIDDEN), 'wv': jax.random.normal(ks[4], (HIDDEN, kv_out), jnp.float32) * s(HIDDEN), 'wo': jax.random.normal(ks[5], (q_out, HIDDEN), jnp.float32) * s(q_out), 'wk_ctx': jax.random.normal(ks[6], (HIDDEN, kv_out), jnp.float32) * s(HIDDEN), 'wv_ctx': jax.random.normal(ks[7], (HIDDEN, kv_out), jnp.float32) * s(HIDDEN), 'q_norm_w': jnp.ones((HEAD_DIM,), jnp.float32), 'k_norm_w': jnp.ones((HEAD_DIM,), jnp.float32)}
    _L1_xattn_all = _L1_xattn_setup()
    _L1_xattn_in = {k: v for k, v in _L1_xattn_all.items() if k in ('wq', 'wk', 'wv', 'wo', 'wk_ctx', 'wv_ctx', 'q_norm_w', 'k_norm_w')}
    del _L1_xattn_all

    def _L1_ffn_setup():
        import jax, jax.numpy as jnp
        import numpy as np
        H = 256
        F = 176
        E = 8
        TOPK = 2
        key = jax.random.key(seed)
        ks = jax.random.split(key, 5)
        s = 1.0 / np.sqrt(H)
        hidden_states = jax.random.normal(ks[0], (1, 256, H), dtype=jnp.float32)
        gate_w = jax.random.uniform(ks[1], (H, E), jnp.float32, -s, s)
        w_gate = jax.random.uniform(ks[2], (E, H, F), jnp.float32, -s, s)
        w_up = jax.random.uniform(ks[3], (E, H, F), jnp.float32, -s, s)
        w_down = jax.random.uniform(ks[4], (E, F, H), jnp.float32, -1.0 / np.sqrt(F), 1.0 / np.sqrt(F))
        return {'hidden_states': hidden_states, 'gate_w': gate_w, 'w_gate': w_gate, 'w_up': w_up, 'w_down': w_down}
    _L1_ffn_all = _L1_ffn_setup()
    _L1_ffn_in = {k: v for k, v in _L1_ffn_all.items() if k in ('gate_w', 'w_gate', 'w_up', 'w_down')}
    del _L1_ffn_all
    return {'x': x, 'ctx_2048': ctx_2048, 'L0_xattn_W_q': _L0_xattn_in['W_q'], 'L0_xattn_W_kv': _L0_xattn_in['W_kv'], 'L0_xattn_W_out': _L0_xattn_in['W_out'], 'L0_xattn_b_out': _L0_xattn_in['b_out'], 'L0_ffn_Wg': _L0_ffn_in['Wg'], 'L0_ffn_W1': _L0_ffn_in['W1'], 'L0_ffn_W3': _L0_ffn_in['W3'], 'L0_ffn_W2': _L0_ffn_in['W2'], 'L0_ffn_sw1': _L0_ffn_in['sw1'], 'L0_ffn_sw3': _L0_ffn_in['sw3'], 'L0_ffn_sw2': _L0_ffn_in['sw2'], 'L1_xattn_wq': _L1_xattn_in['wq'], 'L1_xattn_wk': _L1_xattn_in['wk'], 'L1_xattn_wv': _L1_xattn_in['wv'], 'L1_xattn_wo': _L1_xattn_in['wo'], 'L1_xattn_wk_ctx': _L1_xattn_in['wk_ctx'], 'L1_xattn_wv_ctx': _L1_xattn_in['wv_ctx'], 'L1_xattn_q_norm_w': _L1_xattn_in['q_norm_w'], 'L1_xattn_k_norm_w': _L1_xattn_in['k_norm_w'], 'L1_ffn_gate_w': _L1_ffn_in['gate_w'], 'L1_ffn_w_gate': _L1_ffn_in['w_gate'], 'L1_ffn_w_up': _L1_ffn_in['w_up'], 'L1_ffn_w_down': _L1_ffn_in['w_down']}

def reference(x, ctx_2048, L0_xattn_W_q, L0_xattn_W_kv, L0_xattn_W_out, L0_xattn_b_out, L0_ffn_Wg, L0_ffn_W1, L0_ffn_W3, L0_ffn_W2, L0_ffn_sw1, L0_ffn_sw3, L0_ffn_sw2, L1_xattn_wq, L1_xattn_wk, L1_xattn_wv, L1_xattn_wo, L1_xattn_wk_ctx, L1_xattn_wv_ctx, L1_xattn_q_norm_w, L1_xattn_k_norm_w, L1_ffn_gate_w, L1_ffn_w_gate, L1_ffn_w_up, L1_ffn_w_down):
    import jax
    import jax.numpy as jnp

    def _L0_xattn_ref(x, context, W_q, W_kv, W_out, b_out):
        import jax, jax.numpy as jnp
        import numpy as np
        DIM = 64
        CTX_DIM = 64
        NUM_HEADS = 8
        DIM_HEAD = 64
        INNER = NUM_HEADS * DIM_HEAD
        B, N, CTX_LEN = (4, 256, 256)
        scale = DIM_HEAD ** (-0.5)
        xs = jnp.swapaxes(x, 1, 2)
        cs = jnp.swapaxes(context, 1, 2)
        b, n, _ = xs.shape
        m = cs.shape[1]
        q = xs @ W_q
        kv = cs @ W_kv
        k, v = jnp.split(kv, 2, axis=-1)
        q = q.reshape(b, n, NUM_HEADS, DIM_HEAD).transpose(0, 2, 1, 3)
        k = k.reshape(b, m, NUM_HEADS, DIM_HEAD).transpose(0, 2, 1, 3)
        v = v.reshape(b, m, NUM_HEADS, DIM_HEAD).transpose(0, 2, 1, 3)
        attn = jnp.einsum('bhqd,bhkd->bhqk', q * scale, k)
        attn = jax.nn.softmax(attn, axis=-1)
        out = jnp.einsum('bhqk,bhkd->bhqd', attn, v)
        out = out.transpose(0, 2, 1, 3).reshape(b, n, INNER)
        out = out @ W_out + b_out
        return jnp.swapaxes(out, 1, 2)

    def _L0_ffn_ref(x, Wg, W1, W3, W2, sw1, sw3, sw2):
        import jax, jax.numpy as jnp
        import numpy as np
        B, S, D = (4, 256, 256)
        E = 8
        H = 352
        CAP_F = 1.0

        def _moe(x, Wg, W1, W3, W2, sw1, sw3, sw2):
            b, sl, d = x.shape
            T = b * sl
            C = int(CAP_F * T / E)
            xt = x.reshape(T, d)
            probs = jax.nn.softmax(xt @ Wg, axis=-1)
            eidx = jnp.argmax(probs, axis=-1)
            gate = jnp.take_along_axis(probs, eidx[:, None], 1)[:, 0]
            oh = jax.nn.one_hot(eidx, E, dtype=jnp.int32)
            pos = (jnp.cumsum(oh, axis=0) * oh).sum(-1) - 1
            keep = pos < C
            flat = jnp.where(keep, eidx * C + pos, E * C)
            xd = jnp.zeros((E * C, d), x.dtype).at[flat].set(xt, mode='drop')
            xd = xd.reshape(E, C, d)
            h = jax.nn.silu(jnp.einsum('ecd,edh->ech', xd, W1)) * jnp.einsum('ecd,edh->ech', xd, W3)
            oe = jnp.einsum('ech,ehd->ecd', h, W2).reshape(E * C, d)
            out = jnp.take(oe, jnp.minimum(flat, E * C - 1), axis=0)
            out = out * (gate * keep.astype(x.dtype))[:, None]
            shared = jax.nn.silu(xt @ sw1) * (xt @ sw3) @ sw2
            return (out + shared).reshape(b, sl, d)
        return _moe(x, Wg, W1, W3, W2, sw1, sw3, sw2)

    def _L1_xattn_ref(x, h_ctx_kv, wq, wk, wv, wo, wk_ctx, wv_ctx, q_norm_w, k_norm_w):
        import jax, jax.numpy as jnp
        import numpy as np
        HIDDEN = 256
        NUM_HEADS = 16
        NUM_KV_HEADS = 4
        HEAD_DIM = 128
        ROPE_THETA = 10000.0
        EPS = 1e-06

        def rms_norm(x, w, eps=EPS):
            var = jnp.mean(jnp.square(x), axis=-1, keepdims=True)
            return x * jax.lax.rsqrt(var + eps) * w

        def rope_cache(L, head_dim, theta, dtype):
            inv_freq = 1.0 / theta ** (jnp.arange(0, head_dim, 2, dtype=jnp.float32) / head_dim)
            t = jnp.arange(L, dtype=jnp.float32)
            freqs = jnp.outer(t, inv_freq)
            emb = jnp.concatenate([freqs, freqs], -1)
            cos = jnp.cos(emb).astype(dtype)[None, :, None, :]
            sin = jnp.sin(emb).astype(dtype)[None, :, None, :]
            return (cos, sin)

        def rotate_half(x):
            x1, x2 = jnp.split(x, 2, axis=-1)
            return jnp.concatenate([-x2, x1], axis=-1)
        B, L, _ = x.shape
        T = h_ctx_kv.shape[1]
        rep = NUM_HEADS // NUM_KV_HEADS
        q = (x @ wq).reshape(B, L, NUM_HEADS, HEAD_DIM)
        k = (x @ wk).reshape(B, L, NUM_KV_HEADS, HEAD_DIM)
        v = (x @ wv).reshape(B, L, NUM_KV_HEADS, HEAD_DIM)
        q = rms_norm(q, q_norm_w)
        k = rms_norm(k, k_norm_w)
        k_ctx = (h_ctx_kv @ wk_ctx).reshape(B, T, NUM_KV_HEADS, HEAD_DIM)
        v_ctx = (h_ctx_kv @ wv_ctx).reshape(B, T, NUM_KV_HEADS, HEAD_DIM)
        k_ctx = rms_norm(k_ctx, k_norm_w)
        cos, sin = rope_cache(L, HEAD_DIM, ROPE_THETA, x.dtype)
        q = q * cos + rotate_half(q) * sin
        k = k * cos + rotate_half(k) * sin
        k_full = jnp.concatenate([k_ctx, k], axis=1)
        v_full = jnp.concatenate([v_ctx, v], axis=1)
        k_full = jnp.repeat(k_full, rep, axis=2)
        v_full = jnpp_repeat = jnp.repeat(v_full, rep, axis=2)
        i = jnp.arange(L)[:, None]
        j = jnp.arange(L)[None, :]
        causal = jnp.where(j > i, -jnp.inf, 0.0).astype(x.dtype)
        mask = jnp.concatenate([jnp.zeros((L, T), x.dtype), causal], axis=1)
        scale = 1.0 / np.sqrt(HEAD_DIM)
        scores = jnp.einsum('blhd,bmhd->bhlm', q, k_full) * scale + mask
        probs = jax.nn.softmax(scores, axis=-1)
        out = jnp.einsum('bhlm,bmhd->blhd', probs, v_full)
        out = out.reshape(B, L, NUM_HEADS * HEAD_DIM)
        return out @ wo

    def _L1_ffn_ref(hidden_states, gate_w, w_gate, w_up, w_down):
        import jax, jax.numpy as jnp
        import numpy as np
        H = 256
        F = 176
        E = 8
        TOPK = 2
        b, s, h = hidden_states.shape
        x = hidden_states.reshape(-1, h)
        logits = x @ gate_w
        probs = jax.nn.softmax(logits.astype(jnp.float32), axis=-1)
        topw, sel = jax.lax.top_k(probs, TOPK)
        topw = topw / jnp.sum(topw, axis=-1, keepdims=True)
        topw = topw.astype(hidden_states.dtype)
        combine = jnp.sum(jax.nn.one_hot(sel, E, dtype=topw.dtype) * topw[..., None], axis=1)
        g = jnp.einsum('th,ehf->etf', x, w_gate)
        u = jnp.einsum('th,ehf->etf', x, w_up)
        a = jax.nn.silu(g) * u
        y = jnp.einsum('etf,efh->eth', a, w_down)
        out = jnp.einsum('eth,te->th', y, combine)
        return out.reshape(b, s, h)
    x = x + _L0_xattn_ref(_layernorm(x, axis=-1), ctx_2048, L0_xattn_W_q, L0_xattn_W_kv, L0_xattn_W_out, L0_xattn_b_out)
    x = x + _L0_ffn_ref(_layernorm(x, axis=-1), L0_ffn_Wg, L0_ffn_W1, L0_ffn_W3, L0_ffn_W2, L0_ffn_sw1, L0_ffn_sw3, L0_ffn_sw2)
    x = x + _L1_xattn_ref(_layernorm(x, axis=-1), ctx_2048, L1_xattn_wq, L1_xattn_wk, L1_xattn_wv, L1_xattn_wo, L1_xattn_wk_ctx, L1_xattn_wv_ctx, L1_xattn_q_norm_w, L1_xattn_k_norm_w)
    x = x + _L1_ffn_ref(_layernorm(x, axis=-1), L1_ffn_gate_w, L1_ffn_w_gate, L1_ffn_w_up, L1_ffn_w_down)
    return x

_drawn_inputs = setup_inputs


def setup_inputs(seed=0):
    import zlib

    import numpy as np

    out = dict(_drawn_inputs(seed))
    spreads = {'L1_xattn_q_norm_w': (1.0, 0.2), 'L1_xattn_k_norm_w': (1.0, 0.2)}
    factors = {'L0_xattn_b_out': 6.543}
    for name, (base, spread) in spreads.items():
        noise = np.random.default_rng([zlib.crc32(name.encode()), seed]).standard_normal(out[name].shape)
        drawn = base * np.exp(spread * noise) if base else spread * noise
        out[name] = jnp.asarray(drawn.astype(out[name].dtype))
    for name, factor in factors.items():
        out[name] = (out[name] * factor).astype(out[name].dtype)
    return out
```

```python
from contextlib import ExitStack

import numpy as np
import concourse.bass as bass
from concourse import mybir

F32 = mybir.dt.float32
I32 = mybir.dt.int32
ALU = mybir.AluOpType
ACT = mybir.ActivationFunctionType
AX = mybir.AxisListType

P = 128
NB = 32
S = 64
D = 256
TILES = NB * S // P
LN_EPS = 1e-5


class Scope:

    def __init__(self, nc, ctx):
        self.nc, self.ctx = nc, ctx

    def sb(self, name, shape, dt=F32):
        return self.ctx.enter_context(self.nc.sbuf_tensor(name, shape, dt))

    def ps(self, name, shape, dt=F32):
        return self.ctx.enter_context(self.nc.psum_tensor(name, shape, dt))

    def sem(self, name):
        sem = self.ctx.enter_context(self.nc.semaphore(name))
        SPENT.append(sem)
        return sem


SPENT = []


def clear_spent(nc, live):
    with nc.Block() as block:

        @block.gpsimd
        def _(pool):
            for sem in SPENT:
                if not any(sem is other for other in live):
                    pool.sem_clear(sem)
    SPENT.clear()


def wait(eng, sem, value):
    if isinstance(value, int) and value <= 0:
        return
    eng.wait_ge(sem, value)


class Turns:

    def __init__(self, body, steps, lag, peeled=1):
        self.body, self.steps, self.lag, self.peeled = body, steps, lag, peeled

    def exists(self, i, j):
        return not isinstance(i, int) or 0 <= self.body * i + j < self.steps

    def at_most(self, value, limit):
        return min(value, limit) if isinstance(value, int) else value

    def run(self, eng, step):
        turns = self.steps // self.body
        for i in range(self.peeled):
            for j in range(self.body):
                step(i, j)
        with eng.Fori(self.peeled, turns - 1) as i:
            for j in range(self.body):
                step(i, j)
        for j in range(self.body):
            step(turns - 1, j)
        for j in range(self.lag):
            step(turns + j // self.body, j % self.body)


H0 = 8
E0 = 64


def first_weights(nc, W_q, W_kv, W_out, b_out, x, x_all, x_loaded, ident, score_w, out_w, bias0):
    scale = float(E0) ** -0.5
    with ExitStack() as ctx:
        s = Scope(nc, ctx)
        w_in = s.sb("w_in", [E0, 3 * H0 * E0])
        wo_in = s.sb("wo_in", [P, H0 // 2, E0])
        wT = s.sb("wT", [P, 12, E0])
        ps_t = s.ps("ps_t", [P, 16, E0])
        ps_a = s.ps("ps_a", [P, 2, 8, E0])
        ps_b = s.ps("ps_b", [P, 2, 8, E0])
        w_loaded = s.sem("w_loaded")
        zeroed = s.sem("zeroed")
        ident_ready = s.sem("ident_ready")
        turned = s.sem("turned")
        wT_ready = s.sem("wT_ready")
        products = s.sem("products")
        stored = s.sem("stored")
        with nc.Block() as block:

            @block.sync
            def _(sp):
                sp.dma_start(w_in[:, 0:512], W_q).then_inc(w_loaded, 16)
                sp.dma_start(w_in[:, 512:1536], W_kv).then_inc(w_loaded, 16)
                sp.dma_start(wo_in[:], W_out.rearrange("(p k) n -> k p n", k=P)).then_inc(w_loaded, 16)
                for b in range(2):
                    sp.dma_start(bias0[b * S:(b + 1) * S, :],
                                 b_out.rearrange("(d o) -> d o", o=1)).then_inc(w_loaded, 16)
                xt = x.rearrange("(t b) d n -> (b d) t n", b=2)
                for c in range(4):
                    sp.dma_start(x_all[:, 4 * c:4 * c + 4, :], xt[:, 4 * c:4 * c + 4, :]).then_inc(x_loaded, 16)

            @block.gpsimd
            def _(pool):
                nc.gpsimd.memset(ident[:], 0.0).then_inc(zeroed, 1)
                pool.wait_ge(zeroed, 1)
                nc.gpsimd.affine_select(out=ident[:], in_=ident[:], compare_op=ALU.not_equal, fill=1.0,
                                        base=0, pattern=[[-1, P]], channel_multiplier=1).then_inc(ident_ready, 1)
                nc.gpsimd.memset(score_w[:], 0.0).then_inc(zeroed, 1)

            @block.tensor
            def _(pe):
                pe.wait_ge(w_loaded, 80)
                pe.wait_ge(ident_ready, 1)
                for c in range(12):
                    last = nc.tensor.transpose(ps_t[:, c, :], w_in[:, c * P:(c + 1) * P], ident[0:E0, 0:E0])
                last.then_inc(turned, 1)
                pe.wait_ge(wT_ready, 1)
                for h in range(H0):
                    r, pair = E0 * (h % 2), h // 2
                    for b in range(2):
                        nc.tensor.matmul(ps_a[b * E0:(b + 1) * E0, h % 2, pair, :], wT[r:r + E0, pair, :],
                                         wT[r:r + E0, 4 + pair, :], start=True, stop=True)
                for h in range(H0):
                    r, pair = E0 * (h % 2), h // 2
                    last = nc.tensor.matmul(ps_b[r:r + E0, h % 2, pair, :], wT[r:r + E0, 8 + pair, :],
                                            wo_in[r:r + E0, pair, :], start=True, stop=True)
                last.then_inc(products, 1)

            @block.vector
            def _(dve):
                dve.wait_ge(turned, 1)
                nc.vector.tensor_copy(wT[:], ps_t[:, 0:12, :]).then_inc(wT_ready, 1)
                dve.wait_ge(products, 1)
                dve.wait_ge(zeroed, 2)
                for b in range(2):
                    r = slice(b * E0, (b + 1) * E0)
                    for odd in range(2):
                        nc.vector.tensor_scalar(score_w[r, odd::2, r], ps_a[r, odd, 0:4, :], scale, None,
                                                ALU.mult).then_inc(stored, 1)
                for odd in range(2):
                    r = slice(odd * E0, (odd + 1) * E0)
                    nc.vector.tensor_copy(out_w[r, :, :], ps_b[r, odd, 0:4, :]).then_inc(stored, 1)


def rows_rstd_stage(nc, x_all, x_loaded, mean_var, rstd, label):
    with ExitStack() as ctx:
        s = Scope(nc, ctx)
        stats = s.sb(f"stats_{label}", [P, TILES, 6])
        std = s.sb(f"std_{label}", [P, TILES])
        stats_done = s.sem(f"stats_done_{label}")
        var_done = s.sem(f"var_done_{label}")
        eps_done = s.sem(f"eps_done_{label}")
        sqrt_done = s.sem(f"sqrt_done_{label}")
        rstd_done = s.sem(f"rstd_done_{label}")
        with nc.Block() as block:

            @block.vector
            def _(dve):
                for t in range(TILES):
                    if x_loaded is not None and t == 0:
                        dve.wait_ge(x_loaded, 64)
                    nc.vector.bn_stats(stats[:, t, :], x_all[:, t, :]).then_inc(stats_done, 1)
                for t in range(TILES):
                    dve.wait_ge(stats_done, t + 1)
                    nc.vector.bn_aggr(mean_var[:, t, :], stats[:, t, :]).then_inc(var_done, 1)
                dve.wait_ge(var_done, TILES)
                nc.vector.tensor_scalar(std[:], mean_var[:, :, 1], LN_EPS, None, ALU.add).then_inc(eps_done, 1)
                dve.wait_ge(sqrt_done, 1)
                nc.vector.reciprocal(rstd[:], rstd[:]).then_inc(rstd_done, 1)

            @block.scalar
            def _(act):
                act.wait_ge(eps_done, 1)
                nc.scalar.activation(rstd[:], std[:], ACT.Sqrt).then_inc(sqrt_done, 1)


UNITS = H0 // 2 * 2
BODY0 = 2 * UNITS
STEPS0 = TILES * UNITS


def first_attention(nc, ctx_in, x_all, mean_var, rstd, ident, score_w, out_w, bias0, room, prefetch):
    with ExitStack() as ctx:
        s = Scope(nc, ctx)
        ctx_tile = s.sb("ctx_tile", [P, 2, D])
        ctx_pad = s.sb("ctx_pad", [P, 2, 2, D])
        ctx_T = s.sb("ctx_T", [P, 2, 2, P])
        xn = s.sb("xn", [P, 2, D])
        q_sb = s.sb("q_sb", [P, 2, 2, D])
        neg_max = s.sb("neg_max", [P, 4, 4])
        den = s.sb("den", [P, 4, 4])
        rden = s.sb("rden", [P, 4, 4])
        probs = s.sb("probs", [P, 4, 4, D])
        probs_T = room[:, 0:8, :].rearrange("p (u r k) n -> p u r k n", u=2, r=2)
        heads = room[:, 8:16, :].rearrange("p (b q) n -> p b q n", b=2)
        ps_s = s.ps("ps_s", [P, 2, 4, D])
        ps_pT = s.ps("ps_pT", [P, 2, 2, D])
        ps_q = s.ps("ps_q", [P, 2, D])
        ps_o = s.ps("ps_o", [P, 2, D])

        ctx_loaded = [s.sem(f"ctx_loaded{k}") for k in range(2)]
        pads_zero = s.sem("pads_zero")
        xn_ready = s.sem("xn_ready")
        q_done = s.sem("q_done")
        q_ready = s.sem("q_ready")
        ctxT_done = s.sem("ctxT_done")
        ctxT_ready = s.sem("ctxT_ready")
        scores_done = s.sem("scores_done")
        max_ready = s.sem("max_ready")
        exp_ready = s.sem("exp_ready")
        rden_ready = s.sem("rden_ready")
        probs_ready = s.sem("probs_ready")
        turned = s.sem("probs_turned")
        turned_a = s.sem("turned_copied_by_act")
        turned_d = s.sem("turned_copied_by_dve")
        pv_done = s.sem("pv_done")
        heads_ready = s.sem("heads_ready")
        out_done = s.sem("out_done")
        x_updated = s.sem("x_updated")

        src_tile = ctx_in.rearrange("(t b) d n -> (b d) t n", b=2)
        src_batch = ctx_in.rearrange("(t b) d n -> b d t n", b=2)

        turn = Turns(BODY0, STEPS0, 4)
        exists = turn.exists

        def tile_of(i, j):
            return 2 * i + j // UNITS

        with nc.Block() as block:

            @block.sync
            def _(sp):
                def load(t, k, i):
                    wait(sp, scores_done, UNITS * (t - 1))
                    sp.dma_start(ctx_tile[:, k, :], src_tile[:, t, :]).then_inc(ctx_loaded[k], 16)
                    for b in range(2):
                        sp.dma_start(ctx_pad[b * S:(b + 1) * S, k, b, :], src_batch[b, :, t, :]).then_inc(ctx_loaded[k], 16)

                for k in range(2):
                    load(k, k, 0)
                prefetch(sp)
                with sp.Fori(1, TILES // 2) as i:
                    for k in range(2):
                        load(2 * i + k, k, i)

            @block.gpsimd
            def _(pool):
                for b in range(2):
                    nc.gpsimd.memset(ctx_pad[(1 - b) * S:(2 - b) * S, :, b, :], 0.0).then_inc(pads_zero, 1)

                def normalise(i, j):
                    pool.wait_ge(rden_ready, BODY0 * i + j + 1)
                    p3 = probs[:, j % 4]
                    nc.gpsimd.tensor_tensor(p3, p3, rden[:, j % 4, :].unsqueeze(2).to_broadcast([P, 4, D]),
                                            ALU.mult).then_inc(probs_ready, 1)

                def step(i, j):
                    if exists(i, j):
                        normalise(i, j)

                turn.run(pool, step)

            @block.tensor
            def _(pe):
                def project(i, j):
                    t, pair = tile_of(i, j), BODY0 // 2 * i + j // 2
                    pe.wait_ge(xn_ready, t + 1)
                    wait(pe, q_ready, pair)
                    for r in range(2):
                        last = nc.tensor.matmul(ps_q[:, r, :], score_w[:, (j + r) % H0, :], xn[:, j // UNITS % 2, :],
                                                start=True, stop=True)
                    last.then_inc(q_done, 1)

                def turn_context(i, j):
                    t, k = tile_of(i, j), j // UNITS % 2
                    pe.wait_ge(ctx_loaded[k], 48 * (i + (j // BODY0) + 1))
                    wait(pe, x_updated, 2 * (t - 1))
                    wait(pe, heads_ready, BODY0 * i + j - UNITS - 3)
                    for c in range(2):
                        last = nc.tensor.transpose(ps_o[:, 1, c * P:(c + 1) * P],
                                                   ctx_tile[:, k, c * P:(c + 1) * P], ident[:])
                    last.then_inc(ctxT_done, 1)

                def score(i, j):
                    g, k, b = BODY0 * i + j, j // UNITS, j % 2
                    pe.wait_ge(q_ready, BODY0 // 2 * i + j // 2 + 1)
                    pe.wait_ge(ctx_loaded[k], 48 * (i + 1))
                    wait(pe, exp_ready, g - 1)
                    for r in range(2):
                        for qb in range(2):
                            last = nc.tensor.matmul(ps_s[:, j % 2, 2 * r + qb, :],
                                                    q_sb[:, j // 2 % 2, r, qb * P:(qb + 1) * P],
                                                    ctx_pad[:, k, b, :], start=True, stop=True)
                    last.then_inc(scores_done, 1)

                def turn_probs(i, j):
                    g = BODY0 * i + j
                    pe.wait_ge(probs_ready, g + 1)
                    wait(pe, turned_a, g)
                    wait(pe, turned_d, g)
                    for r in range(2):
                        for kb in range(2):
                            for qb in range(2):
                                last = nc.tensor.transpose(ps_pT[:, r, kb, qb * P:(qb + 1) * P],
                                                           probs[:, j % 4, 2 * r + qb, kb * P:(kb + 1) * P], ident[:])
                    last.then_inc(turned, 1)

                def values(i, j):
                    g, k, b = BODY0 * i + j, j // UNITS % 2, j % 2
                    pe.wait_ge(turned_a, g + 1)
                    pe.wait_ge(turned_d, g + 1)
                    pe.wait_ge(ctxT_ready, tile_of(i, j) + 1)
                    wait(pe, heads_ready, g)
                    if (j - 1) % UNITS >= UNITS - 2:
                        wait(pe, x_updated, 2 * tile_of(i, j - 1) + (j - 1) % 2 + 1)
                    if j % UNITS == 2:
                        pe.wait_ge(ctxT_ready, turn.at_most(tile_of(i, j) + 2, TILES))
                    for kb in range(2):
                        for r in range(2):
                            last = nc.tensor.matmul(ps_o[r * E0:(r + 1) * E0, 0, :],
                                                    ctx_T[:, k, kb, b * E0:(b + 1) * E0],
                                                    probs_T[:, j % 2, r, kb, :], start=(kb == 0), stop=(kb == 1),
                                                    skip_group_check=True)
                    last.then_inc(pv_done, 1)

                def output(i, j):
                    t, b = tile_of(i, j), j % 2
                    pe.wait_ge(heads_ready, BODY0 * i + j + 1)
                    wait(pe, x_updated, 2 * t + b)
                    for pr in range(4):
                        last = nc.tensor.matmul(ps_o[b * E0:(b + 1) * E0, 1, :], out_w[:, pr, :],
                                                heads[:, b, pr, :], start=(pr == 0), stop=(pr == 3),
                                                skip_group_check=True)
                    last.then_inc(out_done, 1)

                def step(i, j):
                    if exists(i, j):
                        score(i, j)
                    if j % UNITS == 5 and exists(i, j + UNITS):
                        turn_context(i, j + UNITS)
                    if j % 2 == 1 and exists(i, j + 1):
                        project(i, j + 1)
                    if (j - 4) % UNITS >= UNITS - 2 and exists(i, j - 4):
                        output(i, j - 4)
                    if exists(i, j - 2):
                        turn_probs(i, j - 2)
                    if exists(i, j - 3):
                        values(i, j - 3)

                turn_context(0, 0)
                project(0, 0)
                pe.wait_ge(pads_zero, 2)
                turn.run(pe, step)

            @block.scalar
            def _(act):
                def copy_context(i, j):
                    t = tile_of(i, j)
                    act.wait_ge(ctxT_done, t + 1)
                    wait(act, pv_done, UNITS * (t - 1))
                    nc.scalar.copy(ctx_T[:, j // UNITS % 2].rearrange("p k c -> p (k c)"), ps_o[:, 1, :]).then_inc(ctxT_ready, 1)

                def exponents(i, j):
                    g = BODY0 * i + j
                    act.wait_ge(max_ready, g + 1)
                    wait(act, turned, g - 3)
                    for c in range(4):
                        last = nc.scalar.activation(probs[:, j % 4, c, :], ps_s[:, j % 2, c, :], ACT.Exp,
                                                    bias=neg_max[:, j % 4, c:c + 1], scale=1.0,
                                                    accum_out=den[:, j % 4, c:c + 1])
                    last.then_inc(exp_ready, 1)

                def copy_turned(i, j):
                    g = BODY0 * i + j
                    act.wait_ge(turned, g + 1)
                    wait(act, pv_done, g - 1)
                    nc.scalar.copy(probs_T[:, j % 2, 0], ps_pT[:, 0]).then_inc(turned_a, 1)

                def copy_heads(i, j):
                    t, b = tile_of(i, j), j % 2
                    act.wait_ge(pv_done, BODY0 * i + j + 1)
                    wait(act, out_done, 2 * (t - 1) + b + 1)
                    nc.scalar.copy(heads[:, b, j // 2 % 4, :], ps_o[:, 0, :]).then_inc(heads_ready, 1)

                def step(i, j):
                    if j % UNITS == 5 and exists(i, j + UNITS):
                        copy_context(i, j + UNITS)
                    if exists(i, j):
                        exponents(i, j)
                    if exists(i, j - 2):
                        copy_turned(i, j - 2)
                    if exists(i, j - 3):
                        copy_heads(i, j - 3)

                copy_context(0, 0)
                turn.run(act, step)

            @block.vector
            def _(dve):
                def normalise_rows(i, j):
                    t = tile_of(i, j)
                    wait(dve, q_done, 4 * (t - 1))
                    nc.vector.tensor_scalar(xn[:, j // UNITS % 2, :], x_all[:, t, :], mean_var[:, t, 0:1],
                                            rstd[:, t:t + 1] if isinstance(t, int) else rstd[:, bass.ds(t, 1)],
                                            ALU.subtract, ALU.mult).then_inc(xn_ready, 1)

                def copy_q(i, j):
                    pair = BODY0 // 2 * i + j // 2
                    dve.wait_ge(q_done, pair + 1)
                    wait(dve, scores_done, 2 * (pair - 1))
                    nc.vector.tensor_copy(q_sb[:, j // 2 % 2], ps_q[:]).then_inc(q_ready, 1)

                def maxima(i, j):
                    g = BODY0 * i + j
                    dve.wait_ge(scores_done, g + 1)
                    wait(dve, exp_ready, g - 3)
                    nc.vector.tensor_reduce(neg_max[:, j % 4, :], ps_s[:, j % 2], AX.X, ALU.max,
                                            negate=True).then_inc(max_ready, 1)

                def copy_turned(i, j):
                    g = BODY0 * i + j
                    dve.wait_ge(turned, g + 1)
                    wait(dve, pv_done, g - 1)
                    nc.vector.tensor_copy(probs_T[:, j % 2, 1], ps_pT[:, 1]).then_inc(turned_d, 1)

                def denominators(i, j):
                    g = BODY0 * i + j
                    dve.wait_ge(exp_ready, g + 1)
                    wait(dve, probs_ready, g - 3)
                    nc.vector.reciprocal(rden[:, j % 4, :], den[:, j % 4, :]).then_inc(rden_ready, 1)

                def update(i, j):
                    t, b = tile_of(i, j), j % 2
                    r = slice(b * S, (b + 1) * S)
                    dve.wait_ge(out_done, 2 * t + b + 1)
                    nc.vector.scalar_tensor_tensor(x_all[r, t, :], ps_o[r, 1, :], bias0[r, 0:1], x_all[r, t, :],
                                                   ALU.add, ALU.add).then_inc(x_updated, 1)

                def step(i, j):
                    if exists(i, j):
                        maxima(i, j)
                    if j % 2 == 1 and exists(i, j + 1):
                        copy_q(i, j + 1)
                    if (j - 4) % UNITS >= UNITS - 2 and exists(i, j - 4):
                        update(i, j - 4)
                    if j % UNITS == 3 and exists(i, j + UNITS):
                        normalise_rows(i, j + UNITS)
                    if exists(i, j - 2):
                        copy_turned(i, j - 2)
                    if exists(i, j):
                        denominators(i, j)

                normalise_rows(0, 0)
                copy_q(0, 0)
                turn.run(dve, step)
E = 8
HID0 = 352
CHUNKS0 = [(0, 128), (128, 128), (256, 96)]
CAP = NB * S // E
SLOTS = E * CAP
FAR = 2 * SLOTS


def load_first_experts(eng, W1, W3, W2, w13, w2, loaded):
    for k in range(2):
        rows = slice(k * P, (k + 1) * P)
        for h, w in enumerate((W1, W3)):
            eng.dma_start(w13[:, k, :, h * HID0:(h + 1) * HID0],
                          w[:, rows, :].rearrange("e p h -> p e h")).then_inc(loaded, 16)
    for c, (r0, n) in enumerate(CHUNKS0):
        eng.dma_start(w2[0:n, c, :, :], W2[:, r0:r0 + n, :].rearrange("e p d -> p e d")).then_inc(loaded, 16)


FIRST_EXPERTS_LOADED = 16 * 7


def load_shared_expert(eng, sw1, sw3, sw2, s13, s2, loaded):
    for k in range(2):
        for h, w in enumerate((sw1, sw3)):
            eng.dma_start(s13[:, k, h * HID0:(h + 1) * HID0], w[k * P:(k + 1) * P, :]).then_inc(loaded, 16)
    for c, (r0, n) in enumerate(CHUNKS0):
        eng.dma_start(s2[0:n, c, :], sw2[r0:r0 + n, :]).then_inc(loaded, 16)


SHARED_EXPERT_LOADED = 16 * 7


def logits_stage(nc, label, x_all, mean_var, rstd, ident, gate_w, gate_loaded, xn_all, logits):
    with ExitStack() as ctx:
        s = Scope(nc, ctx)
        rows = s.sb(f"rows_{label}", [P, 2, D])
        xT = s.sb(f"xT_{label}", [P, 2, D])
        ps_x = s.ps(f"ps_x_{label}", [P, 2, 512])
        ps_l = s.ps(f"ps_l_{label}", [P, 512])
        rows_ready = s.sem(f"rows_ready_{label}")
        kept = s.sem(f"kept_{label}")
        turned = s.sem(f"rows_turned_{label}")
        xT_ready = s.sem(f"xT_ready_{label}")
        logits_done = s.sem(f"logits_done_{label}")
        logits_kept = s.sem(f"logits_kept_{label}")
        turn = Turns(2, TILES, 1, 2)
        exists = turn.exists
        with nc.Block() as block:

            @block.vector
            def _(dve):
                def step(i, j):
                    if exists(i, j):
                        t = 2 * i + j
                        wait(dve, turned, t - 1)
                        nc.vector.tensor_scalar(rows[:, j, :], x_all[:, t, :], mean_var[:, t, 0:1],
                                                column(rstd, t), ALU.subtract, ALU.mult).then_inc(rows_ready, 1)
                        dve.wait_ge(rows_ready, t + 1)
                        nc.vector.tensor_copy(xn_all[:, t, :], rows[:, j, :]).then_inc(kept, 1)

                turn.run(dve, step)
                dve.wait_ge(logits_done, TILES)
                nc.vector.tensor_copy(logits[:].rearrange("p t e -> p (t e)"), ps_l[:, 0:TILES * E]).then_inc(logits_kept, 1)

            @block.tensor
            def _(pe):
                pe.wait_ge(gate_loaded, 16)

                def step(i, j):
                    if exists(i, j):
                        t = 2 * i + j
                        pe.wait_ge(rows_ready, t + 1)
                        wait(pe, xT_ready, t - 1)
                        for k in range(2):
                            last = nc.tensor.transpose(ps_x[:, j, k * P:(k + 1) * P], rows[:, j, k * P:(k + 1) * P], ident[:])
                        last.then_inc(turned, 1)
                    if exists(i, j - 1):
                        t, m = 2 * i + j - 1, (j - 1) % 2
                        pe.wait_ge(xT_ready, t + 1)
                        for k in range(2):
                            last = nc.tensor.matmul(ps_l[:, E * t:E * t + E] if isinstance(t, int) else ps_l[:, bass.ds(E * t, E)],
                                                    xT[:, m, k * P:(k + 1) * P], gate_w[:, k, :],
                                                    start=(k == 0), stop=(k == 1))
                        last.then_inc(logits_done, 1)

                turn.run(pe, step)

            @block.scalar
            def _(act):
                def step(i, j):
                    if exists(i, j):
                        t = 2 * i + j
                        act.wait_ge(turned, t + 1)
                        wait(act, logits_done, t - 1)
                        nc.scalar.copy(xT[:, j, :], ps_x[:, j, 0:D]).then_inc(xT_ready, 1)

                turn.run(act, step)


def column(a, t):
    return a[:, t:t + 1] if isinstance(t, int) else a[:, bass.ds(t, 1)]


class Chain:

    def __init__(self, eng, sem):
        self.eng, self.sem, self.n = eng, sem, 0

    def __call__(self, instruction):
        self.n += 1
        instruction.then_inc(self.sem, 1)
        self.eng.wait_ge(self.sem, self.n)


def pick_first(link, nc, from_eight, values, best, ranked, rank, one_hot):
    wide = lambda a: a.unsqueeze(2).to_broadcast([P, TILES, E])
    per_expert = from_eight[:].unsqueeze(1).to_broadcast([P, TILES, E])
    link(nc.vector.tensor_reduce(best[:], values[:], AX.X, ALU.max))
    link(nc.vector.tensor_tensor(ranked[:], values[:], wide(best[:]), ALU.is_equal))
    link(nc.vector.tensor_tensor(ranked[:], ranked[:], per_expert, ALU.mult))
    link(nc.vector.tensor_reduce(rank[:], ranked[:], AX.X, ALU.min))
    link(nc.vector.tensor_tensor(one_hot[:], per_expert, wide(rank[:]), ALU.is_equal))


def first_routing(nc, logits, scatter_at, gather_at, gate):
    with ExitStack() as ctx:
        s = Scope(nc, ctx)
        BF = mybir.dt.bfloat16
        wide = lambda a: a.unsqueeze(2).to_broadcast([P, TILES, E])
        from_eight = s.sb("r_from_eight", [P, E])
        best = s.sb("r_best", [P, TILES])
        ranked = s.sb("r_ranked", [P, TILES, E])
        rank = s.sb("r_rank", [P, TILES])
        one_hot = s.sb("r_one_hot", [P, TILES, E])
        one_hot_b = s.sb("r_one_hot_b", [P, TILES, E], BF)
        shifted = s.sb("r_shifted", [P, TILES, E])
        total = s.sb("r_total", [P, TILES])
        pos = s.sb("r_pos", [P, TILES])
        keep = s.sb("r_keep", [P, TILES])
        slot = s.sb("r_slot", [P, TILES])
        far = s.sb("r_far", [P, TILES])
        idx = s.sb("r_idx", [P, 2, TILES])
        ones = s.sb("r_ones", [P, P], BF)
        upto = s.sb("r_upto", [P, P], BF)
        ps_c = s.ps("r_ps_c", [P, 512])
        made = s.sem("r_made")
        consts = s.sem("r_consts")
        chain = s.sem("r_chain")
        hot_ready = s.sem("r_hot_ready")
        shift_ready = s.sem("r_shift_ready")
        exp_done = s.sem("r_exp_done")
        counted = s.sem("r_counted")
        with nc.Block() as block:

            @block.gpsimd
            def _(pool):
                nc.gpsimd.iota(from_eight[:], [[1, E]], base=-E, channel_multiplier=0,
                               allow_small_or_imprecise_dtypes=True).then_inc(consts, 1)
                nc.gpsimd.iota(far[:], [[P, TILES]], base=FAR, channel_multiplier=1,
                               allow_small_or_imprecise_dtypes=True).then_inc(consts, 1)
                nc.gpsimd.memset(ones[:], 1.0).then_inc(made, 1)
                pool.wait_ge(made, 1)
                nc.gpsimd.affine_select(out=upto[:], in_=ones[:], compare_op=ALU.is_ge, fill=0.0, base=0,
                                        pattern=[[1, P]], channel_multiplier=-1).then_inc(consts, 1)

            @block.vector
            def _(dve):
                link = Chain(dve, chain)
                dve.wait_ge(consts, 3)
                pick_first(link, nc, from_eight, logits, best, ranked, rank, one_hot)
                nc.vector.tensor_copy(one_hot_b[:], one_hot[:]).then_inc(hot_ready, 1)
                nc.vector.tensor_tensor(shifted[:], logits[:], wide(best[:]), ALU.subtract).then_inc(shift_ready, 1)
                dve.wait_ge(exp_done, 1)
                link(nc.vector.tensor_reduce(total[:], shifted[:], AX.X, ALU.add))
                link(nc.vector.reciprocal(gate[:], total[:]))
                dve.wait_ge(counted, 1)
                link(nc.vector.tensor_tensor(ranked[:], one_hot[:], ps_c[:, 0:TILES * E].rearrange("p (t e) -> p t e", e=E),
                                             ALU.mult))
                link(nc.vector.tensor_reduce(pos[:], ranked[:], AX.X, ALU.add))
                link(nc.vector.tensor_scalar(keep[:], pos[:], float(CAP), None, ALU.is_le))
                link(nc.vector.tensor_tensor(gate[:], gate[:], keep[:], ALU.mult))
                link(nc.vector.tensor_scalar(slot[:], rank[:], float(CAP), float(E * CAP - 1), ALU.mult, ALU.add))
                link(nc.vector.tensor_tensor(slot[:], slot[:], pos[:], ALU.add))
                link(nc.vector.tensor_tensor(idx[:, 0, :], slot[:], far[:], ALU.subtract))
                link(nc.vector.tensor_tensor(idx[:, 0, :], idx[:, 0, :], keep[:], ALU.mult))
                link(nc.vector.tensor_tensor(idx[:, 0, :], idx[:, 0, :], far[:], ALU.add))
                link(nc.vector.tensor_scalar(idx[:, 1, :], slot[:], float(-(SLOTS - 1)), None, ALU.add))
                link(nc.vector.tensor_tensor(idx[:, 1, :], idx[:, 1, :], keep[:], ALU.mult))
                link(nc.vector.tensor_scalar(idx[:, 1, :], idx[:, 1, :], float(SLOTS - 1), None, ALU.add))
                link(nc.vector.tensor_copy(scatter_at[:], idx[:, 0, :]))
                link(nc.vector.tensor_copy(gather_at[:], idx[:, 1, :]))

            @block.scalar
            def _(act):
                act.wait_ge(shift_ready, 1)
                nc.scalar.activation(shifted[:], shifted[:], ACT.Exp).then_inc(exp_done, 1)

            @block.tensor
            def _(pe):
                pe.wait_ge(hot_ready, 1)
                pe.wait_ge(consts, 3)
                hot = one_hot_b[:].rearrange("p t e -> p (t e)")
                last = nc.tensor.matmul(ps_c[:, 0:TILES * E], upto[:], hot, start=True, stop=False)
                for back in range(1, TILES):
                    last = nc.tensor.matmul(ps_c[:, back * E:TILES * E], ones[:], hot[:, 0:(TILES - back) * E],
                                            start=False, stop=(back == TILES - 1))
                last.then_inc(counted, 1)


def first_ffn(nc, label, ident, weights, weights_loaded, x_all=None, xn_all=None, table=None, results=None, extra_pool=None):
    w13_of, w2_of = weights
    with ExitStack() as ctx:
        s = Scope(nc, ctx)
        rows = s.sb(f"rows_{label}", [P, 2, D])
        xT = s.sb(f"xT_{label}", [P, 2, D])
        hid = s.sb(f"hid_{label}", [P, 2, HID0])
        hT = s.sb(f"hT_{label}", [P, 2, 3, P])
        y = s.sb(f"y_{label}", [P, 2, D])
        ps_x = s.ps(f"ps_x_{label}", [P, 512])
        ps_h = s.ps(f"ps_h_{label}", [P, 2, 2, 512])
        ps_hT = s.ps(f"ps_hT_{label}", [P, 512])
        ps_y = s.ps(f"ps_y_{label}", [P, 512])
        rows_ready = [s.sem(f"rows_ready{k}_{label}") for k in range(2)]
        rows_turned = s.sem(f"rows_turned_{label}")
        xT_ready = s.sem(f"xT_ready_{label}")
        h_done = s.sem(f"h_done_{label}")
        silu_ready = s.sem(f"silu_ready_{label}")
        hid_ready = s.sem(f"hid_ready_{label}")
        hid_turned = s.sem(f"hid_turned_{label}")
        hT_ready = s.sem(f"hT_ready_{label}")
        y_done = s.sem(f"y_done_{label}")
        y_used = s.sem(f"y_used_{label}")
        stored = [s.sem(f"stored{k}_{label}") for k in range(2)]
        each = 16 if table is not None else 1
        turn = Turns(2, TILES, 4, 2)
        exists = turn.exists
        with nc.Block() as block:
            if extra_pool is not None:
                block.gpsimd(extra_pool)

            @block.sync
            def _(sp):
                if table is None:
                    return

                def step(i, j):
                    if exists(i, j):
                        n = 2 * i + j
                        wait(sp, rows_turned, n - 1)
                        sp.dma_start(rows[:, j, :], table[n]).then_inc(rows_ready[j], 16)
                    if exists(i, j - 3):
                        n = 2 * i + j - 3
                        sp.wait_ge(y_used, n + 1)
                        sp.dma_start(results[n], y[:, (j - 3) % 2, :]).then_inc(stored[(j - 3) % 2], 16)

                for j in range(2):
                    step(0, j)
                for i in range(1, TILES // 2 + 2):
                    for j in range(2):
                        step(i, j)
                for k in range(2):
                    sp.wait_ge(stored[k], 16 * TILES // 2)

            @block.tensor
            def _(pe):
                def turn_rows(i, j):
                    n = 2 * i + j
                    pe.wait_ge(rows_ready[j % 2], each * (i + 1))
                    wait(pe, xT_ready, n)
                    for k in range(2):
                        last = nc.tensor.transpose(ps_x[:, k * P:(k + 1) * P], rows[:, j % 2, k * P:(k + 1) * P], ident[:])
                    last.then_inc(rows_turned, 1)

                def hidden(i, j):
                    n, m = 2 * i + j, j % 2
                    pe.wait_ge(xT_ready, n + 1)
                    wait(pe, hid_ready, n - 1)
                    for h in range(2):
                        for k in range(2):
                            last = nc.tensor.matmul(ps_h[:, m, h, 0:HID0], xT[:, m, k * P:(k + 1) * P],
                                                    w13_of(i + j // 2, k)[:, h * HID0:(h + 1) * HID0],
                                                    start=(k == 0), stop=(k == 1))
                    last.then_inc(h_done, 1)

                def turn_hidden(i, j):
                    n, m = 2 * i + j, j % 2
                    pe.wait_ge(hid_ready, n + 1)
                    wait(pe, hT_ready, n)
                    for c, (r0, w) in enumerate(CHUNKS0):
                        last = nc.tensor.transpose(ps_hT[0:w, c * P:(c + 1) * P], hid[:, m, r0:r0 + w], ident[:])
                    last.then_inc(hid_turned, 1)

                def down(i, j):
                    n, m = 2 * i + j, j % 2
                    pe.wait_ge(hT_ready, n + 1)
                    wait(pe, y_used, n)
                    for c, (r0, w) in enumerate(CHUNKS0):
                        last = nc.tensor.matmul(ps_y[:, 0:D], hT[0:w, m, c, :], w2_of(i + j // 2, c)[0:w, :],
                                                start=(c == 0), stop=(c == 2))
                    last.then_inc(y_done, 1)

                def step(i, j):
                    if exists(i, j):
                        turn_rows(i, j)
                    if exists(i, j - 2):
                        turn_hidden(i, j - 2)
                    if exists(i, j - 1):
                        hidden(i, j - 1)
                    if exists(i, j - 2):
                        down(i, j - 2)

                pe.wait_ge(*weights_loaded)
                turn.run(pe, step)

            @block.scalar
            def _(act):
                def step(i, j):
                    if exists(i, j):
                        n = 2 * i + j
                        act.wait_ge(rows_turned, n + 1)
                        wait(act, h_done, n - 1)
                        nc.scalar.copy(xT[:, j, :], ps_x[:, 0:D]).then_inc(xT_ready, 1)
                    if exists(i, j - 2):
                        n = 2 * i + j - 2
                        act.wait_ge(hid_turned, n + 1)
                        wait(act, y_done, n - 1)
                        w = CHUNKS0[2][1]
                        nc.scalar.copy(hT[0:w, j, 2, :], ps_hT[0:w, 2 * P:3 * P])
                        nc.scalar.copy(hT[:, j, 0:2, :], ps_hT[:, 0:2 * P].rearrange("p (c n) -> p c n", c=2)).then_inc(hT_ready, 1)
                    if exists(i, j - 1):
                        n = 2 * i + j - 1
                        act.wait_ge(h_done, n + 1)
                        wait(act, hid_turned, n - 1)
                        nc.scalar.activation(hid[:, (j - 1) % 2, :], ps_h[:, (j - 1) % 2, 0, 0:HID0],
                                             ACT.Silu).then_inc(silu_ready, 1)

                turn.run(act, step)

            @block.vector
            def _(dve):
                def step(i, j):
                    if table is None and exists(i, j):
                        n = 2 * i + j
                        wait(dve, rows_turned, n - 1)
                        nc.vector.tensor_copy(rows[:, j, :], xn_all[:, n, :]).then_inc(rows_ready[j], 1)
                    if exists(i, j - 1):
                        n, m = 2 * i + j - 1, (j - 1) % 2
                        dve.wait_ge(silu_ready, n + 1)
                        nc.vector.tensor_tensor(hid[:, m, :], hid[:, m, :], ps_h[:, m, 1, 0:HID0], ALU.mult).then_inc(hid_ready, 1)
                    if exists(i, j - 2):
                        n = 2 * i + j - 2
                        dve.wait_ge(y_done, n + 1)
                        if table is None:
                            nc.vector.tensor_tensor(x_all[:, n, :], x_all[:, n, :], ps_y[:, 0:D], ALU.add).then_inc(y_used, 1)
                        else:
                            wait(dve, stored[j], 16 * (i - 1))
                            nc.vector.tensor_copy(y[:, j, :], ps_y[:, 0:D]).then_inc(y_used, 1)

                turn.run(dve, step)


def first_experts(nc, x_all, mean_var, rstd, ident, Wg, shared_weights, w13, w2, loaded, table, results, table_zeroed,
                  prefetch):
    with ExitStack() as ctx:
        s = Scope(nc, ctx)
        xn_all = s.sb("xn_all_f", [P, TILES, D])
        logits = s.sb("logits_f", [P, TILES, E])
        gate_w = s.sb("gate_w_f", [P, 2, E])
        scatter_at = s.sb("scatter_at", [P, TILES], I32)
        gather_at = s.sb("gather_at", [P, TILES], I32)
        gate = s.sb("gate_f", [P, TILES])
        s13 = s.sb("s13", [P, 2, 2 * HID0])
        s2 = s.sb("s2", [P, 3, D])
        gate_loaded = s.sem("gate_loaded_f")
        shared_loaded = s.sem("shared_loaded")
        scattered = s.sem("scattered")
        gathered = [s.sem(f"gathered{t}") for t in range(TILES)]
        added = s.sem("experts_added")
        with nc.Block() as block:

            @block.sync
            def _(sp):
                sp.dma_start(gate_w[:], Wg.rearrange("(k p) e -> p k e", p=P)).then_inc(gate_loaded, 16)
                load_shared_expert(sp, *shared_weights, s13, s2, shared_loaded)
                prefetch(sp)

        logits_stage(nc, "f", x_all, mean_var, rstd, ident, gate_w, gate_loaded, xn_all, logits)
        first_routing(nc, logits, scatter_at, gather_at, gate)

        def scatter(pool):
            pool.wait_ge(table_zeroed, 16 * TILES)
            for t in range(TILES):
                nc.gpsimd.indirect_dma_start(out=table, out_offset=bass.IndirectOffsetOnAxis(ap=scatter_at[:, t:t + 1], axis=0),
                                             in_=xn_all[:, t, :], in_offset=None,
                                             bounds_check=SLOTS - 1, oob_is_err=False).then_inc(scattered, 16)
            pool.wait_ge(scattered, 16 * TILES)

        first_ffn(nc, "shared", ident, (lambda e, k: s13[:, k, :], lambda e, c: s2[:, c, :]),
                  (shared_loaded, SHARED_EXPERT_LOADED), x_all=x_all, xn_all=xn_all, extra_pool=scatter)
        first_ffn(nc, "experts", ident, (lambda e, k: w13[:, k, e, :], lambda e, c: w2[:, c, e, :]),
                  (loaded, FIRST_EXPERTS_LOADED), table=table.rearrange("(n p) d -> n p d", p=P), results=results.rearrange("(n p) d -> n p d", p=P))
        with nc.Block() as block:

            @block.gpsimd
            def _(pool):
                for t in range(TILES):
                    nc.gpsimd.indirect_dma_start(out=xn_all[:, t, :], out_offset=None, in_=results,
                                                 in_offset=bass.IndirectOffsetOnAxis(ap=gather_at[:, t:t + 1], axis=0),
                                                 bounds_check=SLOTS - 1, oob_is_err=False).then_inc(gathered[t], 16)

            @block.vector
            def _(dve):
                for t in range(TILES):
                    dve.wait_ge(gathered[t], 16)
                    nc.vector.scalar_tensor_tensor(x_all[:, t, :], xn_all[:, t, :], gate[:, t:t + 1], x_all[:, t, :],
                                                   ALU.mult, ALU.add).then_inc(added, 1)
H1 = 16
GROUPS = 4
DH = 128
HG = H1 // GROUPS
KEYS = 2 * S
BODY1 = 2 * GROUPS
STEPS1 = TILES * GROUPS
RMS_EPS = 1e-6
MASKED = -1e30


def load_second_projections(eng, wq, wk, wv, wk_ctx, wv_ctx, q_w, kv_w, loaded):
    eng.dma_start(q_w[:], wq.rearrange("(k p) n -> p k n", p=P)).then_inc(loaded, 16)
    for n, w in enumerate((wk_ctx, wk, wv_ctx, wv)):
        eng.dma_start(kv_w[:, n], w.rearrange("(k p) n -> p k n", p=P)).then_inc(loaded, 16)


def load_second_output(eng, wo, o_w, loaded):
    for n in range(2):
        eng.dma_start(o_w[:, 8 * n:8 * n + 8], wo[n * 1024:(n + 1) * 1024].rearrange("(h p) n -> p h n", p=P)).then_inc(loaded, 16)


SECOND_ATTENTION_LOADED = 16 * 7


def rope_stage(nc, rope, q_norm, k_norm, tables, mask):
    with ExitStack() as ctx:
        s = Scope(nc, ctx)
        angle = s.sb("rope_angle", [P, 2, DH])
        w = s.sb("rope_w", [P, 2, DH])
        angle_loaded = s.sem("angle_loaded")
        zeros = s.sem("mask_zero")
        steps = s.sem("rope_steps")
        masked = s.sem("mask_made")
        with nc.Block() as block:

            @block.sync
            def _(sp):
                for b in range(2):
                    sp.dma_start(angle[b * S:(b + 1) * S], rope.rearrange("c s d -> s c d")).then_inc(angle_loaded, 16)
                for n, v in enumerate((q_norm, k_norm)):
                    sp.dma_start(w[:, n, :], v.rearrange("(o d) -> o d", o=1).to_broadcast([P, DH])).then_inc(angle_loaded, 16)

            @block.vector
            def _(dve):
                dve.wait_ge(angle_loaded, 64)
                half = DH // 2
                link = Chain(dve, steps)
                link(nc.vector.tensor_scalar(w[:, 0, :], w[:, 0, :], float(DH) ** -0.5, None, ALU.mult))
                for n in range(2):
                    link(nc.vector.tensor_tensor(tables[:, n, 0, :], w[:, n, :], angle[:, 0, :], ALU.mult))
                    for a in range(2):
                        o = 1 - a
                        link(nc.vector.tensor_tensor(tables[:, n, 1, a * half:(a + 1) * half], w[:, n, o * half:(o + 1) * half],
                                                     angle[:, 1, a * half:(a + 1) * half], ALU.mult))
                link(nc.vector.tensor_copy(tables[0:S, 1, 0, :], w[0:S, 1, :]))
                link(nc.vector.memset(tables[0:S, 1, 1, :], 0.0))

            @block.gpsimd
            def _(pool):
                nc.gpsimd.memset(mask[:], 0.0).then_inc(zeros, 1)
                pool.wait_ge(zeros, 1)
                for h in range(2):
                    own = mask[h * S:(h + 1) * S, :, S:KEYS]
                    nc.gpsimd.affine_select(out=own, in_=own, compare_op=ALU.is_ge, fill=MASKED, base=0,
                                            pattern=[[0, 4], [-1, S]], channel_multiplier=1).then_inc(masked, 1)


def second_attention(nc, ctx_in, x_all, mean_var, rstd, ident, q_w, kv_w, o_w, loaded, tables, mask, prefetch):
    with ExitStack() as ctx:
        s = Scope(nc, ctx)
        BF = mybir.dt.bfloat16
        ident_b = s.sb("ident_b", [P, P], BF)
        eps = s.sb("rms_eps", [P, 1])
        rows = s.sb("a_rows", [P, 2, 2, D])
        rowsT = s.sb("a_rowsT", [P, 2, 2, 2, P])
        square = s.sb("a_square", [P, 2, 512])
        mean_sq = s.sb("a_mean_sq", [P, 4, 4])
        log_sq = s.sb("a_log_sq", [P, 4, 4])
        inv_rms = s.sb("a_inv_rms", [P, 4, 4])
        turned_cos = s.sb("a_cos", [P, 2, HG, DH])
        turned_sin = s.sb("a_sin", [P, 2, HG, DH])
        kT = s.sb("a_kT", [P, 2, 2, GROUPS, KEYS])
        v = s.sb("a_v", [P, 2, 2, 512])
        qT = s.sb("a_qT", [P, 2, GROUPS, 2, HG, S])
        neg_max = s.sb("a_neg_max", [P, 2, 4])
        den = s.sb("a_den", [P, 2, 4])
        rden = s.sb("a_rden", [P, 2, 4])
        probs = s.sb("a_probs", [P, 2, 4, KEYS])
        probs_T = s.sb("a_probs_T", [P, 2, 4, P])
        heads = s.sb("a_heads", [P, 2, HG, 2, S])
        ps_p = [s.ps(f"a_ps_p{n}", [P, 512]) for n in range(2)]
        ps_r = s.ps("a_ps_r", [P, 512])
        ps_s = s.ps("a_ps_s", [P, 4, KEYS])
        ps_pT = s.ps("a_ps_pT", [P, 4, P])
        ps_o = s.ps("a_ps_o", [P, 2, HG, S])
        ps_y = s.ps("a_ps_y", [P, 512])
        ps_x = s.ps("a_ps_x", [P, 512])

        ident_cast = s.sem("ident_cast")
        ctx_loaded = [s.sem(f"a_ctx_loaded{k}") for k in range(2)]
        xn_ready = s.sem("a_xn_ready")
        rows_turned = s.sem("a_rows_turned")
        rowsT_ready = s.sem("a_rowsT_ready")
        projected = [s.sem(f"a_projected{n}") for n in range(2)]
        v_kept = [s.sem(f"a_v_kept{n}") for n in range(2)]
        squared = [s.sem(f"a_squared{n}") for n in range(2)]
        summed = [s.sem(f"a_summed{n}") for n in range(2)]
        log_done = s.sem("a_log_done")
        inv_ready = [s.sem(f"a_inv_ready{n}") for n in range(2)]
        rotated = [s.sem(f"a_rotated{n}") for n in range(2)]
        summed_up = s.sem("a_summed_up")
        roped = [s.sem(f"a_roped{n}") for n in range(2)]
        rope_turned = [s.sem(f"a_rope_turned{n}") for n in range(2)]
        rope_kept = [s.sem(f"a_rope_kept{n}") for n in range(2)]
        scores_done = s.sem("a_scores_done")
        max_ready = s.sem("a_max_ready")
        exp_ready = s.sem("a_exp_ready")
        rden_ready = s.sem("a_rden_ready")
        probs_ready = s.sem("a_probs_ready")
        probs_turned = s.sem("a_probs_turned")
        probsT_ready = s.sem("a_probsT_ready")
        pv_done = s.sem("a_pv_done")
        heads_ready = s.sem("a_heads_ready")
        out_done = s.sem("a_out_done")
        x_updated = s.sem("a_x_updated")

        turn = Turns(BODY1, STEPS1, GROUPS + 2)
        exists = turn.exists
        src_tile = ctx_in.rearrange("(t b) d n -> (b d) t n", b=2)

        def is_v(j):
            return j % GROUPS == 1

        def rope_steps(i, j):
            return 3 * (2 * i + j // GROUPS) + (0, 1, 1, 2)[j % GROUPS]

        with nc.Block() as block:

            @block.sync
            def _(sp):
                for k in range(2):
                    sp.dma_start(rows[:, k, 1, :], src_tile[:, k, :]).then_inc(ctx_loaded[k], 16)
                prefetch(sp)
                with sp.Fori(1, TILES // 2) as i:
                    for k in range(2):
                        sp.wait_ge(rows_turned, 2 * i + k - 1)
                        sp.dma_start(rows[:, k, 1, :], src_tile[:, 2 * i + k, :]).then_inc(ctx_loaded[k], 16)

            @block.gpsimd
            def _(pool):
                nc.gpsimd.memset(eps[:], RMS_EPS)
                nc.gpsimd.tensor_copy(ident_b[:], ident[:]).then_inc(ident_cast, 1)

                def rope(i, j, n):
                    r = rope_steps(i, j)
                    pool.wait_ge(rotated[n], r + 1)
                    nc.gpsimd.tensor_tensor(turned_cos[:, n], turned_cos[:, n], turned_sin[:, n], ALU.add).then_inc(summed_up, 1)
                    pool.wait_ge(summed_up, 2 * r + n + 1)
                    pool.wait_ge(inv_ready[n], r + 1)
                    nc.gpsimd.tensor_tensor(turned_cos[:, n], turned_cos[:, n],
                                            inv_rms[:, 2 * (j % 2) + n, :].unsqueeze(2).to_broadcast([P, HG, DH]),
                                            ALU.mult).then_inc(roped[n], 1)

                def normalise(i, j):
                    u, m = BODY1 * i + j, j % 2
                    pool.wait_ge(rden_ready, u + 1)
                    nc.gpsimd.tensor_tensor(probs[:, m], probs[:, m], rden[:, m, :].unsqueeze(2).to_broadcast([P, 4, KEYS]),
                                            ALU.mult).then_inc(probs_ready, 1)

                def step(i, j):
                    if exists(i, j) and not is_v(j):
                        rope(i, j, 0)
                    if exists(i, j - 4):
                        normalise(i, j - 4)
                    if exists(i, j) and not is_v(j):
                        rope(i, j, 1)

                turn.run(pool, step)

            @block.tensor
            def _(pe):
                def turn_rows(i, j):
                    t, k = 2 * i + j // GROUPS, j // GROUPS % 2
                    pe.wait_ge(xn_ready, t + 1)
                    pe.wait_ge(ctx_loaded[k], 16 * (i + j // BODY1 + 1))
                    wait(pe, rowsT_ready, t)
                    for a in range(2):
                        for c in range(2):
                            last = nc.tensor.transpose(ps_x[:, (2 * a + c) * P:(2 * a + c + 1) * P],
                                                       rows[:, k, a, c * P:(c + 1) * P], ident[:])
                    last.then_inc(rows_turned, 1)

                def project(i, j, n):
                    t, k = 2 * i + j // GROUPS, j // GROUPS
                    u = BODY1 * i + j
                    if n == 0:
                        pe.wait_ge(rowsT_ready, t + 1)
                    wait(pe, v_kept[n], 2 * i + (j + 2) // GROUPS)
                    wait(pe, rotated[n], rope_steps(i, j))
                    if j % GROUPS < 2:
                        kind = 2 * (j % GROUPS)
                        for part in range(2):
                            for c in range(2):
                                last = nc.tensor.matmul(ps_p[n][part * S:(part + 1) * S, :],
                                                        rowsT[:, k, 1 - part, c, n * S:(n + 1) * S],
                                                        kv_w[:, kind + part, c, :], start=(c == 0), stop=(c == 1),
                                                        skip_group_check=True)
                    else:
                        g = 2 * (j % GROUPS - 2) + n
                        for c in range(2):
                            last = nc.tensor.matmul(ps_p[n][:], rowsT[:, k, 0, c, :], q_w[:, c, g * 512:(g + 1) * 512],
                                                    start=(c == 0), stop=(c == 1))
                    last.then_inc(projected[n], 1)

                def turn_rope(i, j, n):
                    r = rope_steps(i, j)
                    pe.wait_ge(roped[n], r + 1)
                    wait(pe, rope_kept[1 - n], r + n)
                    for h in range(HG):
                        last = nc.tensor.transpose(ps_r[:, h * P:(h + 1) * P], turned_cos[:, n, h, :], ident[:])
                    last.then_inc(rope_turned[n], 1)

                def score(i, j):
                    u, k, g = BODY1 * i + j, j // GROUPS % 2, j % GROUPS
                    pe.wait_ge(rope_kept[g % 2], 3 * (2 * i + j // GROUPS) + 2 + g // 2)
                    pe.wait_ge(rope_kept[1], 3 * (2 * i + j // GROUPS) + 1)
                    wait(pe, exp_ready, u)
                    nc.tensor.matmul(ps_s[:].rearrange("p a b -> p (a b)"), ident_b[:], mask[:].rearrange("p a b -> p (a b)"),
                                     start=True, stop=False)
                    for b in range(2):
                        for m in range(2):
                            last = nc.tensor.matmul(ps_s[:, 2 * b + m, :],
                                                    qT[:, k, g, b, 2 * m:2 * m + 2, :].rearrange("p h s -> p (h s)"),
                                                    kT[:, k, b, g, :], start=False, stop=(b == 1 and m == 1))
                    last.then_inc(scores_done, 1)

                def turn_probs(i, j):
                    u, m = BODY1 * i + j, j % 2
                    pe.wait_ge(probs_ready, u + 1)
                    wait(pe, probsT_ready, u)
                    for a in range(4):
                        last = nc.tensor.transpose(ps_pT[:, a, :], probs[:, m, a, :], ident[:])
                    last.then_inc(probs_turned, 1)

                def values(i, j):
                    u, k, g = BODY1 * i + j, j // GROUPS % 2, j % GROUPS
                    pe.wait_ge(probsT_ready, u + 1)
                    for n in range(2):
                        pe.wait_ge(v_kept[n], 2 * i + j // GROUPS + 1)
                    wait(pe, heads_ready, u)
                    for b in range(2):
                        last = nc.tensor.matmul(ps_o[:, b].rearrange("p h s -> p (h s)"), v[:, k, b, g * DH:(g + 1) * DH],
                                                probs_T[:, j % 2, 2 * b:2 * b + 2, :].rearrange("p a n -> p (a n)"),
                                                start=True, stop=True)
                    last.then_inc(pv_done, 1)

                def output(i, j):
                    u, g = BODY1 * i + j, j % GROUPS
                    pe.wait_ge(heads_ready, u + 1)
                    if g == 0:
                        wait(pe, x_updated, 2 * i + j // GROUPS)
                    for h in range(HG):
                        last = nc.tensor.matmul(ps_y[:, 0:D], heads[:, j % 2, h].rearrange("p b s -> p (b s)"),
                                                o_w[:, HG * g + h, :], start=(g == 0 and h == 0),
                                                stop=(g == GROUPS - 1 and h == HG - 1))
                    last.then_inc(out_done, 1)

                def step(i, j):
                    if exists(i, j - 4):
                        score(i, j - 4)
                    if exists(i, j - 5):
                        turn_probs(i, j - 5)
                    if exists(i, j):
                        project(i, j, 0)
                    if exists(i, j - 5):
                        values(i, j - 5)
                    if exists(i, j - 1) and not is_v(j - 1):
                        turn_rope(i, j - 1, 0)
                    if j % GROUPS == 3 and exists(i, j + 1):
                        turn_rows(i, j + 1)
                    if exists(i, j):
                        project(i, j, 1)
                    if exists(i, j - 5):
                        output(i, j - 5)
                    if exists(i, j - 1) and not is_v(j - 1):
                        turn_rope(i, j - 1, 1)

                pe.wait_ge(ident_cast, 1)
                pe.wait_ge(loaded, SECOND_ATTENTION_LOADED)
                turn_rows(0, 0)
                turn.run(pe, step)

            @block.scalar
            def _(act):
                def copy_rows(i, j):
                    t, k = 2 * i + j // GROUPS, j // GROUPS % 2
                    act.wait_ge(rows_turned, t + 1)
                    wait(act, projected[1], GROUPS * (t - 1))
                    nc.scalar.copy(rowsT[:, k].rearrange("p a c n -> p (a c n)"), ps_x[:]).then_inc(rowsT_ready, 1)

                def keep_values(i, j, n):
                    u, k = BODY1 * i + j, j // GROUPS
                    act.wait_ge(projected[n], u + 1)
                    wait(act, pv_done, u - 1 - GROUPS)
                    nc.scalar.copy(v[:, k, n, :], ps_p[n][:]).then_inc(v_kept[n], 1)

                def squares(i, j, n):
                    r = rope_steps(i, j)
                    act.wait_ge(projected[n], BODY1 * i + j + 1)
                    wait(act, summed[n], r)
                    nc.scalar.activation(square[:, n, :], ps_p[n][:], ACT.Square).then_inc(squared[n], 1)

                def inverse(i, j, n):
                    r, c = rope_steps(i, j), 2 * (j % 2) + n
                    act.wait_ge(summed[n], r + 1)
                    nc.scalar.activation(log_sq[:, c, :], mean_sq[:, c, :], ACT.Ln, bias=eps[:, 0:1],
                                         scale=1.0 / DH).then_inc(log_done, 1)
                    act.wait_ge(log_done, 2 * r + n + 1)
                    wait(act, roped[n], r - 1)
                    nc.scalar.activation(inv_rms[:, c, :], log_sq[:, c, :], ACT.Exp, scale=-0.5).then_inc(inv_ready[n], 1)

                def keep_rope(i, j, n):
                    k, r = j // GROUPS % 2, rope_steps(i, j)
                    act.wait_ge(rope_turned[n], r + 1)
                    if j % GROUPS == 0:
                        nc.scalar.copy(kT[:, k, n].rearrange("p g n -> p (g n)"), ps_r[:]).then_inc(rope_kept[n], 1)
                    else:
                        g = 2 * (j % GROUPS - 2) + n
                        nc.scalar.copy(qT[:, k, g].rearrange("p b h s -> p h b s"),
                                       ps_r[:].rearrange("p (h b s) -> p h b s", h=HG, b=2)).then_inc(rope_kept[n], 1)

                def exponents(i, j):
                    u, m = BODY1 * i + j, j % 2
                    act.wait_ge(max_ready, u + 1)
                    wait(act, probs_turned, u - 1)
                    for a in range(4):
                        last = nc.scalar.activation(probs[:, m, a, :], ps_s[:, a, :], ACT.Exp, bias=neg_max[:, m, a:a + 1],
                                                    scale=1.0, accum_out=den[:, m, a:a + 1])
                    last.then_inc(exp_ready, 1)

                def keep_heads(i, j):
                    u, m = BODY1 * i + j, j % 2
                    act.wait_ge(pv_done, u + 1)
                    wait(act, out_done, u - 1)
                    nc.scalar.copy(heads[:, m].rearrange("p h b s -> p b h s"), ps_o[:]).then_inc(heads_ready, 1)

                def step(i, j):
                    if exists(i, j - 4):
                        exponents(i, j - 4)
                    rope = exists(i, j) and not is_v(j)
                    if rope:
                        squares(i, j, 0)
                    elif exists(i, j):
                        keep_values(i, j, 0)
                    if exists(i, j - 5):
                        keep_heads(i, j - 5)
                    if exists(i, j - 1) and not is_v(j - 1):
                        keep_rope(i, j - 1, 0)
                    if rope:
                        inverse(i, j, 0)
                    if j % GROUPS == 3 and exists(i, j + 1):
                        copy_rows(i, j + 1)
                    if rope:
                        squares(i, j, 1)
                    elif exists(i, j):
                        keep_values(i, j, 1)
                    if exists(i, j - 1) and not is_v(j - 1):
                        keep_rope(i, j - 1, 1)
                    if rope:
                        inverse(i, j, 1)

                nc.scalar.preload_act_table_set("natural_log_exp_and_others")
                act.wait_ge(ident_cast, 1)
                copy_rows(0, 0)
                turn.run(act, step)

            @block.vector
            def _(dve):
                def normalise_rows(i, j):
                    t, k = 2 * i + j // GROUPS, j // GROUPS % 2
                    wait(dve, rows_turned, t - 1)
                    nc.vector.tensor_scalar(rows[:, k, 0, :], x_all[:, t, :], mean_var[:, t, 0:1], column(rstd, t),
                                            ALU.subtract, ALU.mult).then_inc(xn_ready, 1)

                def rotate(i, j, n):
                    r, c = rope_steps(i, j), 2 * (j % 2) + n
                    q_or_k = 1 if j % GROUPS == 0 else 0
                    half = DH // 2
                    dve.wait_ge(squared[n], r + 1)
                    nc.vector.tensor_reduce(mean_sq[:, c, :], square[:, n, :].rearrange("p (h d) -> p h d", h=HG),
                                            AX.X, ALU.add).then_inc(summed[n], 1)
                    wait(dve, rope_turned[n], r)
                    job = ps_p[n][:].rearrange("p (h d) -> p h d", h=HG)

                    def table(which, lo, hi):
                        return tables[:, q_or_k, which, lo:hi].unsqueeze(1).to_broadcast([P, HG, hi - lo])

                    nc.vector.tensor_tensor(turned_cos[:, n], job, table(0, 0, DH), ALU.mult)
                    nc.vector.tensor_tensor(turned_sin[:, n, :, 0:half], job[:, :, half:DH], table(1, 0, half), ALU.mult)
                    nc.vector.tensor_tensor(turned_sin[:, n, :, half:DH], job[:, :, 0:half], table(1, half, DH),
                                            ALU.mult).then_inc(rotated[n], 1)

                def maxima(i, j):
                    u, m = BODY1 * i + j, j % 2
                    dve.wait_ge(scores_done, u + 1)
                    wait(dve, exp_ready, u - 1)
                    nc.vector.tensor_reduce(neg_max[:, m, :], ps_s[:], AX.X, ALU.max, negate=True).then_inc(max_ready, 1)

                def denominators(i, j):
                    u, m = BODY1 * i + j, j % 2
                    dve.wait_ge(exp_ready, u + 1)
                    wait(dve, probs_ready, u - 1)
                    nc.vector.reciprocal(rden[:, m, :], den[:, m, :]).then_inc(rden_ready, 1)

                def copy_probs(i, j):
                    u, m = BODY1 * i + j, j % 2
                    dve.wait_ge(probs_turned, u + 1)
                    wait(dve, pv_done, u - 1)
                    nc.vector.tensor_copy(probs_T[:, m], ps_pT[:]).then_inc(probsT_ready, 1)

                def update(i, j):
                    t = 2 * i + j // GROUPS
                    dve.wait_ge(out_done, BODY1 * i + j + 1)
                    nc.vector.tensor_tensor(x_all[:, t, :], x_all[:, t, :], ps_y[:, 0:D], ALU.add).then_inc(x_updated, 1)

                def step(i, j):
                    if exists(i, j - 4):
                        maxima(i, j - 4)
                    if exists(i, j - 5):
                        copy_probs(i, j - 5)
                    if exists(i, j - 4):
                        denominators(i, j - 4)
                    if exists(i, j) and not is_v(j):
                        rotate(i, j, 0)
                    if j % GROUPS == 2 and exists(i, j + 2):
                        normalise_rows(i, j + 2)
                    if exists(i, j) and not is_v(j):
                        rotate(i, j, 1)
                    if (j - 5) % GROUPS == GROUPS - 1 and exists(i, j - 5):
                        update(i, j - 5)

                normalise_rows(0, 0)
                turn.run(dve, step)
HID1 = 176
BLOCKS1 = E * HID1 // P
GROUP_BLOCKS = [(0, 4), (4, 8), (8, 11)]
GROUP_LAST = [-(-hi * P // HID1) - 1 for _, hi in GROUP_BLOCKS]
BODY2 = 2 * E


def load_second_experts(eng, w_gate, w_up, w_down, w_gu, w_d, loaded):
    for k in range(2):
        for h, w in enumerate((w_gate, w_up)):
            eng.dma_start(w_gu[:, k, :, h * HID1:(h + 1) * HID1],
                          w[:, k * P:(k + 1) * P, :].rearrange("e p f -> p e f")).then_inc(loaded, 16)
    eng.dma_start(w_d[:], w_down.rearrange("e f d -> (e f) d").rearrange("(c p) d -> p c d", p=P)).then_inc(loaded, 16)


SECOND_EXPERTS_LOADED = 16 * 5


def second_routing(nc, logits, combine):
    with ExitStack() as ctx:
        s = Scope(nc, ctx)
        from_eight = s.sb("t_from_eight", [P, E])
        best = [s.sb(f"t_best{n}", [P, TILES]) for n in range(2)]
        hot = [s.sb(f"t_hot{n}", [P, TILES, E]) for n in range(2)]
        ranked = s.sb("t_ranked", [P, TILES, E])
        rank = s.sb("t_rank", [P, TILES])
        rest = s.sb("t_rest", [P, TILES, E])
        ratio = s.sb("t_ratio", [P, TILES])
        total = s.sb("t_total", [P, TILES])
        weight = [s.sb(f"t_weight{n}", [P, TILES]) for n in range(2)]
        consts = s.sem("t_consts")
        chain = s.sem("t_chain")
        diff_ready = s.sem("t_diff_ready")
        exp_done = s.sem("t_exp_done")
        wide = lambda a: a.unsqueeze(2).to_broadcast([P, TILES, E])
        with nc.Block() as block:

            @block.gpsimd
            def _(pool):
                nc.gpsimd.iota(from_eight[:], [[1, E]], base=-E, channel_multiplier=0,
                               allow_small_or_imprecise_dtypes=True).then_inc(consts, 1)

            @block.vector
            def _(dve):
                link = Chain(dve, chain)
                dve.wait_ge(consts, 1)
                pick_first(link, nc, from_eight, logits, best[0], ranked, rank, hot[0])
                link(nc.vector.tensor_scalar(ranked[:], hot[0][:], -3e38, None, ALU.mult))
                link(nc.vector.tensor_tensor(rest[:], logits[:], ranked[:], ALU.add))
                pick_first(link, nc, from_eight, rest, best[1], ranked, rank, hot[1])
                nc.vector.tensor_tensor(ratio[:], best[1][:], best[0][:], ALU.subtract).then_inc(diff_ready, 1)
                dve.wait_ge(exp_done, 1)
                link(nc.vector.tensor_scalar(total[:], ratio[:], 1.0, None, ALU.add))
                link(nc.vector.reciprocal(weight[0][:], total[:]))
                link(nc.vector.tensor_tensor(weight[1][:], weight[0][:], ratio[:], ALU.mult))
                link(nc.vector.tensor_tensor(hot[0][:], hot[0][:], wide(weight[0][:]), ALU.mult))
                link(nc.vector.tensor_tensor(hot[1][:], hot[1][:], wide(weight[1][:]), ALU.mult))
                link(nc.vector.tensor_tensor(combine[:], hot[0][:], hot[1][:], ALU.add))

            @block.scalar
            def _(act):
                act.wait_ge(diff_ready, 1)
                nc.scalar.activation(ratio[:], ratio[:], ACT.Exp).then_inc(exp_done, 1)


def second_ffn(nc, x_all, xn_all, ident, w_gu, w_d, loaded, combine, out):
    with ExitStack() as ctx:
        s = Scope(nc, ctx)
        rows = s.sb("e_rows", [P, 2, D])
        xT = s.sb("e_xT", [P, 2, 2, P])
        act_g = s.sb("e_act_g", [P, 4, HID1])
        hid = s.sb("e_hid", [P, 2, E * HID1])
        hT = s.sb("e_hT", [P, 2, BLOCKS1, P])
        ps_h = [s.ps(f"e_ps_h{n}", [P, 512]) for n in range(4)]
        ps_t = [s.ps(f"e_ps_t{n}", [P, 4, P]) for n in range(2)]
        ps_x = s.ps("e_ps_x", [P, 512])
        ps_y = s.ps("e_ps_y", [P, 512])
        rows_ready = s.sem("e_rows_ready")
        rows_turned = s.sem("e_rows_turned")
        xT_ready = s.sem("e_xT_ready")
        h_done = s.sem("e_h_done")
        silu_ready = s.sem("e_silu_ready")
        hid_ready = s.sem("e_hid_ready")
        turned = s.sem("e_turned")
        hT_ready = s.sem("e_hT_ready")
        y_done = s.sem("e_y_done")
        x_ready = s.sem("e_x_ready")
        stored = s.sem("e_stored")
        turn = Turns(BODY2, TILES * E, E + 3)
        exists = turn.exists
        out_tile = out.rearrange("(t b) d n -> (b d) t n", b=2)
        turn_at = [last + 2 for last in GROUP_LAST]
        down_at = turn_at[2] + 1

        def tile_of(i, j):
            return 2 * i + j // E

        def groups_due(j):
            return [(n, j - at) for n, at in enumerate(turn_at) if (j - at) % E == 0]

        with nc.Block() as block:

            @block.sync
            def _(sp):
                for t in range(TILES):
                    sp.wait_ge(x_ready, t + 1)
                    sp.dma_start(out_tile[:, t, :], x_all[:, t, :]).then_inc(stored, 16)
                sp.wait_ge(stored, 16 * TILES)

            @block.tensor
            def _(pe):
                def turn_rows(i, j):
                    t, k = tile_of(i, j), j // E % 2
                    pe.wait_ge(rows_ready, t + 1)
                    wait(pe, xT_ready, t)
                    for c in range(2):
                        last = nc.tensor.transpose(ps_x[:, c * P:(c + 1) * P], rows[:, k, c * P:(c + 1) * P], ident[:])
                    last.then_inc(rows_turned, 1)

                def hidden(i, j):
                    u, k = BODY2 * i + j, j // E
                    pe.wait_ge(xT_ready, tile_of(i, j) + 1)
                    wait(pe, hid_ready, u - 3)
                    for c in range(2):
                        last = nc.tensor.matmul(ps_h[j % 4][:, 0:2 * HID1], xT[:, k, c, :], w_gu[:, c, j % E, :],
                                                start=(c == 0), stop=(c == 1))
                    last.then_inc(h_done, 1)

                def turn_group(i, j, n):
                    t, k = tile_of(i, j), j // E % 2
                    c = 3 * t + n
                    b = (3 * (j // E) + n) % 2
                    lo, hi = GROUP_BLOCKS[n]
                    pe.wait_ge(hid_ready, BODY2 * i + j + GROUP_LAST[n] + 1)
                    wait(pe, hT_ready, c - 1)
                    for m in range(lo, hi):
                        last = nc.tensor.transpose(ps_t[b][:, m - lo, :], hid[:, k, m * P:(m + 1) * P], ident[:])
                    last.then_inc(turned, 1)

                def down(i, j):
                    t, k = tile_of(i, j), j // E % 2
                    pe.wait_ge(hT_ready, 3 * t + 3)
                    wait(pe, x_ready, t)
                    for m in range(BLOCKS1):
                        last = nc.tensor.matmul(ps_y[:, 0:D], hT[:, k, m, :], w_d[:, m, :],
                                                start=(m == 0), stop=(m == BLOCKS1 - 1))
                    last.then_inc(y_done, 1)

                def step(i, j):
                    if exists(i, j):
                        hidden(i, j)
                    if j % E == 4 and exists(i, j + 4):
                        turn_rows(i, j + 4)
                    for n, j0 in groups_due(j):
                        if exists(i, j0):
                            turn_group(i, j0, n)
                    if (j - down_at) % E == 0 and exists(i, j - down_at):
                        down(i, j - down_at)

                pe.wait_ge(loaded, SECOND_EXPERTS_LOADED)
                turn_rows(0, 0)
                turn.run(pe, step)

            @block.scalar
            def _(act):
                def copy_rows(i, j):
                    t, k = tile_of(i, j), j // E % 2
                    act.wait_ge(rows_turned, t + 1)
                    wait(act, h_done, E * (t - 1))
                    nc.scalar.copy(xT[:, k].rearrange("p c n -> p (c n)"), ps_x[:, 0:D]).then_inc(xT_ready, 1)

                def silu(i, j):
                    u = BODY2 * i + j
                    act.wait_ge(h_done, u + 1)
                    wait(act, hid_ready, u - 3)
                    nc.scalar.activation(act_g[:, j % 4, :], ps_h[j % 4][:, 0:HID1], ACT.Silu).then_inc(silu_ready, 1)

                def copy_group(i, j, n):
                    t, k = tile_of(i, j), j // E % 2
                    lo, hi = GROUP_BLOCKS[n]
                    act.wait_ge(turned, 3 * t + n + 1)
                    wait(act, y_done, t - 1)
                    nc.scalar.copy(hT[:, k, lo:hi, :], ps_t[(3 * (j // E) + n) % 2][:, 0:hi - lo, :]).then_inc(hT_ready, 1)

                def step(i, j):
                    if j % E == 4 and exists(i, j + 4):
                        copy_rows(i, j + 4)
                    if exists(i, j):
                        silu(i, j)
                    for n, j0 in groups_due(j):
                        if exists(i, j0):
                            copy_group(i, j0, n)

                copy_rows(0, 0)
                turn.run(act, step)

            @block.vector
            def _(dve):
                def stage_rows(i, j):
                    t = tile_of(i, j)
                    wait(dve, rows_turned, t - 1)
                    nc.vector.tensor_copy(rows[:, j // E % 2, :], xn_all[:, t, :]).then_inc(rows_ready, 1)

                def gated(i, j):
                    u, t, k, e = BODY2 * i + j, tile_of(i, j), j // E, j % E
                    dve.wait_ge(silu_ready, u + 1)
                    wait(dve, turned, 3 * (t - 1))
                    w = combine[:].rearrange("p t e -> p (t e)")
                    w = w[:, E * t + e:E * t + e + 1] if isinstance(t, int) else w[:, bass.ds(E * t + e, 1)]
                    nc.vector.scalar_tensor_tensor(hid[:, k, e * HID1:(e + 1) * HID1], act_g[:, j % 4, :], w,
                                                   ps_h[j % 4][:, HID1:2 * HID1], ALU.mult, ALU.mult).then_inc(hid_ready, 1)

                def update(i, j):
                    t = tile_of(i, j)
                    dve.wait_ge(y_done, t + 1)
                    nc.vector.tensor_tensor(x_all[:, t, :], x_all[:, t, :], ps_y[:, 0:D], ALU.add).then_inc(x_ready, 1)

                def step(i, j):
                    if exists(i, j):
                        gated(i, j)
                    if j % E == 2 and exists(i, j + 6):
                        stage_rows(i, j + 6)
                    if (j - down_at) % E == 0 and exists(i, j - down_at):
                        update(i, j - down_at)

                stage_rows(0, 0)
                turn.run(dve, step)


def second_experts(nc, x_all, mean_var, rstd, ident, gate_w_in, w_gu, w_d, loaded, out):
    with ExitStack() as ctx:
        s = Scope(nc, ctx)
        xn_all = s.sb("xn_all_e", [P, TILES, D])
        logits = s.sb("logits_e", [P, TILES, E])
        gate_w = s.sb("gate_w_e", [P, 2, E])
        combine = s.sb("combine", [P, TILES, E])
        gate_loaded = s.sem("gate_loaded_e")
        with nc.Block() as block:

            @block.sync
            def _(sp):
                sp.dma_start(gate_w[:], gate_w_in.rearrange("(k p) e -> p k e", p=P)).then_inc(gate_loaded, 16)

        logits_stage(nc, "e", x_all, mean_var, rstd, ident, gate_w, gate_loaded, xn_all, logits)
        second_routing(nc, logits, combine)
        second_ffn(nc, x_all, xn_all, ident, w_gu, w_d, loaded, combine, out)


def build(nc, a, out):
    SPENT.clear()
    table = nc.dram_tensor("expert_rows", [SLOTS, D], F32, kind="Internal").ap()
    results = nc.dram_tensor("expert_results", [SLOTS, D], F32, kind="Internal").ap()
    with ExitStack() as ctx:
        s = Scope(nc, ctx)
        x_all = s.sb("x_all", [P, TILES, D])
        ident = s.sb("ident", [P, P])
        mean_var = s.sb("mean_var", [P, TILES, 2])
        rstd = s.sb("rstd", [P, TILES])
        q_w = s.sb("q_w", [P, 2, H1 * DH])
        kv_w = s.sb("kv_w", [P, 4, 2, GROUPS * DH])
        o_w = s.sb("o_w", [P, H1, D])
        x_loaded = s.sem("x_loaded")
        second_loaded = s.sem("second_attention_loaded")
        with ExitStack() as first:
            f = Scope(nc, first)
            w13 = f.sb("w13", [P, 2, E, 2 * HID0])
            w2 = f.sb("w2", [P, 3, E, D])
            first_loaded = f.sem("first_experts_loaded")
            table_zeroed = f.sem("table_zeroed")
            with ExitStack() as attention:
                t = Scope(nc, attention)
                score_w = t.sb("score_w", [P, H0, P])
                out_w = t.sb("out_w", [P, H0 // 2, E0])
                bias0 = t.sb("bias0", [P, 1])
                zero = t.sb("zero", [P, D])
                zero_made = t.sem("zero_made")
                with nc.Block() as block:

                    @block.gpsimd
                    def _(pool):
                        nc.gpsimd.memset(zero[:], 0.0).then_inc(zero_made, 1)

                first_weights(nc, a["L0_xattn_W_q"], a["L0_xattn_W_kv"], a["L0_xattn_W_out"], a["L0_xattn_b_out"],
                              a["x"], x_all, x_loaded, ident, score_w, out_w, bias0)
                rows_rstd_stage(nc, x_all, x_loaded, mean_var, rstd, "a")

                def prefetch_experts(sp):
                    load_first_experts(sp, a["L0_ffn_W1"], a["L0_ffn_W3"], a["L0_ffn_W2"], w13, w2, first_loaded)
                    load_second_projections(sp, a["L1_xattn_wq"], a["L1_xattn_wk"], a["L1_xattn_wv"], a["L1_xattn_wk_ctx"],
                                            a["L1_xattn_wv_ctx"], q_w, kv_w, second_loaded)
                    sp.wait_ge(zero_made, 1)
                    for n in range(TILES):
                        sp.dma_start(table[n * P:(n + 1) * P, :], zero[:]).then_inc(table_zeroed, 16)
                    sp.wait_ge(table_zeroed, 16 * TILES)

                first_attention(nc, a["ctx_2048"], x_all, mean_var, rstd, ident, score_w, out_w, bias0, o_w,
                                prefetch_experts)
            rows_rstd_stage(nc, x_all, None, mean_var, rstd, "b")
            first_experts(nc, x_all, mean_var, rstd, ident, a["L0_ffn_Wg"],
                          (a["L0_ffn_sw1"], a["L0_ffn_sw3"], a["L0_ffn_sw2"]), w13, w2, first_loaded,
                          table, results, table_zeroed,
                          lambda sp: load_second_output(sp, a["L1_xattn_wo"], o_w, second_loaded))
        clear_spent(nc, (x_loaded, second_loaded))
        w_gu = s.sb("w_gu", [P, 2, E, 2 * HID1])
        w_d = s.sb("w_d", [P, BLOCKS1, D])
        experts_loaded = s.sem("second_experts_loaded")
        with ExitStack() as attention:
            t = Scope(nc, attention)
            tables = t.sb("rope_tables", [P, 2, 2, DH])
            mask = t.sb("mask", [P, 4, KEYS], mybir.dt.bfloat16)
            rows_rstd_stage(nc, x_all, None, mean_var, rstd, "c")
            rope_stage(nc, a["rope"], a["L1_xattn_q_norm_w"], a["L1_xattn_k_norm_w"], tables, mask)
            second_attention(nc, a["ctx_2048"], x_all, mean_var, rstd, ident, q_w, kv_w, o_w, second_loaded, tables, mask,
                             lambda sp: load_second_experts(sp, a["L1_ffn_w_gate"], a["L1_ffn_w_up"], a["L1_ffn_w_down"],
                                                            w_gu, w_d, experts_loaded))
        rows_rstd_stage(nc, x_all, None, mean_var, rstd, "d")
        second_experts(nc, x_all, mean_var, rstd, ident, a["L1_ffn_gate_w"], w_gu, w_d, experts_loaded, out)


def rope_angles():
    half = np.arange(0, DH, 2, dtype=np.float64) / DH
    angle = np.outer(np.arange(S, dtype=np.float64), 1.0 / 10000.0 ** half)
    cos, sin = np.cos(angle), np.sin(angle)
    return np.stack([np.concatenate([cos, cos], -1), np.concatenate([-sin, sin], -1)]).astype(np.float32)


def kernel(**inputs):
    import concourse.bacc as bacc
    from concourse.bass_utils import run_bass_kernel_spmd

    nc = bacc.Bacc("TRN2", target_bir_lowering=False, num_devices=1)
    arrays = {name: np.ascontiguousarray(a) for name, a in inputs.items()}
    arrays["rope"] = rope_angles()
    args = {name: nc.dram_tensor(name, a.shape, mybir.dt.from_np(a.dtype), kind="ExternalInput").ap()
            for name, a in arrays.items()}
    out = nc.dram_tensor("out", (NB, S, D), F32, kind="ExternalOutput").ap()
    build(nc, args, out)
    r = run_bass_kernel_spmd(nc, [arrays], core_ids=[0])
    return r.results[0]["out"]
```

```python
from contextlib import ExitStack

import numpy as np
import concourse.bass as bass
from concourse import mybir

F32 = mybir.dt.float32
F32R = mybir.dt.float32r
I32 = mybir.dt.int32
ALU = mybir.AluOpType
ACT = mybir.ActivationFunctionType
AX = mybir.AxisListType

P = 128
NB = 32
S = 64
D = 256
TILES = NB * S // P
LN_EPS = 1e-5


class Scope:

    def __init__(self, nc, ctx):
        self.nc, self.ctx = nc, ctx

    def sb(self, name, shape, dt=F32):
        return self.ctx.enter_context(self.nc.sbuf_tensor(name, shape, dt))

    def ps(self, name, shape, dt=F32):
        return self.ctx.enter_context(self.nc.psum_tensor(name, shape, dt))

    def sem(self, name):
        sem = self.ctx.enter_context(self.nc.semaphore(name))
        SPENT.append(sem)
        return sem


SPENT = []


def clear_spent(nc, live):
    with nc.Block() as block:

        @block.gpsimd
        def _(pool):
            for sem in SPENT:
                if not any(sem is other for other in live):
                    pool.sem_clear(sem)
    SPENT.clear()


def wait(eng, sem, value):
    if isinstance(value, int) and value <= 0:
        return
    eng.wait_ge(sem, value)


class Turns:

    def __init__(self, body, steps, lag, peeled=1):
        self.body, self.steps, self.lag, self.peeled = body, steps, lag, peeled

    def exists(self, i, j):
        return not isinstance(i, int) or 0 <= self.body * i + j < self.steps

    def at_most(self, value, limit):
        return min(value, limit) if isinstance(value, int) else value

    def run(self, eng, step):
        turns = self.steps // self.body
        for i in range(self.peeled):
            for j in range(self.body):
                step(i, j)
        with eng.Fori(self.peeled, turns - 1) as i:
            for j in range(self.body):
                step(i, j)
        for j in range(self.body):
            step(turns - 1, j)
        for j in range(self.lag):
            step(turns + j // self.body, j % self.body)


H0 = 8
E0 = 64


def first_weights(nc, W_q, W_kv, W_out, b_out, x, x_all, x_loaded, ident, score_w, out_w, bias0):
    scale = float(E0) ** -0.5
    with ExitStack() as ctx:
        s = Scope(nc, ctx)
        w_in = s.sb("w_in", [E0, 3 * H0 * E0])
        wo_in = s.sb("wo_in", [P, H0 // 2, E0])
        wT = s.sb("wT", [P, 12, E0])
        a_w = s.sb("a_w", [P, H0 // 2, P])
        ps_t = s.ps("ps_t", [P, 16, E0])
        ps_a = s.ps("ps_a", [P, 2, 8, E0])
        ps_b = s.ps("ps_b", [P, 2, 8, E0])
        w_loaded = s.sem("w_loaded")
        zeroed = s.sem("zeroed")
        ident_ready = s.sem("ident_ready")
        turned = s.sem("turned")
        wT_ready = s.sem("wT_ready")
        products = s.sem("products")
        stored = s.sem("stored")
        with nc.Block() as block:

            @block.sync
            def _(sp):
                sp.dma_start(w_in[:, 0:512], W_q).then_inc(w_loaded, 16)
                sp.dma_start(w_in[:, 512:1536], W_kv).then_inc(w_loaded, 16)
                sp.dma_start(wo_in[:], W_out.rearrange("(p k) n -> k p n", k=P)).then_inc(w_loaded, 16)
                for b in range(2):
                    sp.dma_start(bias0[b * S:(b + 1) * S, :],
                                 b_out.rearrange("(d o) -> d o", o=1)).then_inc(w_loaded, 16)
                xt = x.rearrange("(t b) d n -> (b d) t n", b=2)
                for c in range(4):
                    sp.dma_start(x_all[:, 4 * c:4 * c + 4, :], xt[:, 4 * c:4 * c + 4, :]).then_inc(x_loaded, 16)

            @block.gpsimd
            def _(pool):
                nc.gpsimd.memset(ident[:], 0.0).then_inc(zeroed, 1)
                pool.wait_ge(zeroed, 1)
                nc.gpsimd.affine_select(out=ident[:], in_=ident[:], compare_op=ALU.not_equal, fill=1.0,
                                        base=0, pattern=[[-1, P]], channel_multiplier=1).then_inc(ident_ready, 1)

            @block.tensor
            def _(pe):
                pe.wait_ge(w_loaded, 80)
                pe.wait_ge(ident_ready, 1)
                for c in range(12):
                    last = nc.tensor.transpose(ps_t[:, c, :], w_in[:, c * P:(c + 1) * P], ident[0:E0, 0:E0])
                last.then_inc(turned, 1)
                pe.wait_ge(wT_ready, 1)
                for h in range(H0):
                    r, pair = E0 * (h % 2), h // 2
                    for b in range(2):
                        nc.tensor.matmul(ps_a[b * E0:(b + 1) * E0, h % 2, pair, :], wT[r:r + E0, pair, :],
                                         wT[r:r + E0, 4 + pair, :], start=True, stop=True)
                for h in range(H0):
                    r, pair = E0 * (h % 2), h // 2
                    last = nc.tensor.matmul(ps_b[r:r + E0, h % 2, pair, :], wT[r:r + E0, 8 + pair, :],
                                            wo_in[r:r + E0, pair, :], start=True, stop=True)
                last.then_inc(products, 1)

            @block.vector
            def _(dve):
                dve.wait_ge(turned, 1)
                nc.vector.tensor_copy(wT[:], ps_t[:, 0:12, :]).then_inc(wT_ready, 1)
                dve.wait_ge(products, 1)
                for odd in range(2):
                    nc.vector.tensor_scalar(a_w[:, :, odd * E0:(odd + 1) * E0], ps_a[:, odd, 0:4, :], scale, None,
                                            ALU.mult).then_inc(stored, 1)
                dve.wait_ge(stored, 2)
                nc.vector.tensor_copy(score_w[:, :, 0, :], a_w[:]).then_inc(stored, 1)
                dve.wait_ge(stored, 3)
                nc.vector.tensor_tensor(score_w[:, :, 1, :], a_w[:], score_w[:, :, 0, :], ALU.subtract).then_inc(stored, 1)
                for odd in range(2):
                    r = slice(odd * E0, (odd + 1) * E0)
                    nc.vector.tensor_copy(out_w[r, :, :], ps_b[r, odd, 0:4, :]).then_inc(stored, 1)


def rows_rstd_stage(nc, x_all, x_loaded, mean_var, rstd, label, loads=None):
    with ExitStack() as ctx:
        s = Scope(nc, ctx)
        stats = s.sb(f"stats_{label}", [P, TILES, 6])
        std = s.sb(f"std_{label}", [P, TILES])
        stats_done = s.sem(f"stats_done_{label}")
        var_done = s.sem(f"var_done_{label}")
        eps_done = s.sem(f"eps_done_{label}")
        sqrt_done = s.sem(f"sqrt_done_{label}")
        rstd_done = s.sem(f"rstd_done_{label}")
        with nc.Block() as block:
            if loads is not None:
                block.sync(loads)

            @block.vector
            def _(dve):
                for t in range(TILES):
                    if x_loaded is not None and t == 0:
                        dve.wait_ge(x_loaded, 64)
                    nc.vector.bn_stats(stats[:, t, :], x_all[:, t, :]).then_inc(stats_done, 1)
                for t in range(TILES):
                    dve.wait_ge(stats_done, t + 1)
                    nc.vector.bn_aggr(mean_var[:, t, :], stats[:, t, :]).then_inc(var_done, 1)
                dve.wait_ge(var_done, TILES)
                nc.vector.tensor_scalar(std[:], mean_var[:, :, 1], LN_EPS, None, ALU.add).then_inc(eps_done, 1)
                dve.wait_ge(sqrt_done, 1)
                nc.vector.reciprocal(rstd[:], rstd[:]).then_inc(rstd_done, 1)

            @block.scalar
            def _(act):
                act.wait_ge(eps_done, 1)
                nc.scalar.activation(rstd[:], std[:], ACT.Sqrt).then_inc(sqrt_done, 1)


UNITS = H0 // 2 * 2
BODY0 = 2 * UNITS
STEPS0 = TILES * UNITS
CTX_AT = 4


def first_attention(nc, ctx_in, x_all, mean_var, rstd, ident, score_w, out_w, bias0, room, prefetch):
    with ExitStack() as ctx:
        s = Scope(nc, ctx)
        ctx_tile = s.sb("ctx_tile", [P, 2, D])
        ctx_twice = s.sb("ctx_twice", [P, 2, 2, D])
        ctx_split = s.sb("ctx_split", [P, 2, 2, 2, D], F32R)
        one = s.sb("one", [P, 1])
        ctx_T = s.sb("ctx_T", [P, 2, 2, P])
        xn = s.sb("xn", [P, 2, D])
        x_split = s.sb("x_split", [P, 2, 2, D], F32R)
        q_split = s.sb("q_split", [P, 4, 2, D], F32R)
        neg_max = s.sb("neg_max", [P, 4, 4])
        den = s.sb("den", [P, 4, 4])
        rden = s.sb("rden", [P, 4, 4])
        probs = s.sb("probs", [P, 4, 4, D])
        probs_T = room[:, 0:8, :].rearrange("p (u r k) n -> p u r k n", u=2, r=2)
        heads = room[:, 8:16, :].rearrange("p (b q) n -> p b q n", b=2)
        ps_s = s.ps("ps_s", [P, 2, 4, D])
        ps_pT = s.ps("ps_pT", [P, 2, 2, D])
        ps_q = s.ps("ps_q", [P, 2, D])
        ps_o = s.ps("ps_o", [P, D])

        ctx_loaded = [s.sem(f"ctx_loaded{k}") for k in range(2)]
        one_made = s.sem("one_made")
        ctx_high = s.sem("ctx_high")
        ctx_parted = s.sem("ctx_parted")
        xn_ready = s.sem("xn_ready")
        x_high = s.sem("x_high")
        x_parted = s.sem("x_parted")
        q_done = s.sem("q_done")
        q_high_a = s.sem("q_high_by_act")
        q_high_d = s.sem("q_high_by_dve")
        q_ready = s.sem("q_ready")
        ctxT_done = s.sem("ctxT_done")
        ctxT_ready = s.sem("ctxT_ready")
        scores_done = s.sem("scores_done")
        max_ready = s.sem("max_ready")
        exp_ready = s.sem("exp_ready")
        rden_ready = s.sem("rden_ready")
        probs_ready = s.sem("probs_ready")
        turned = s.sem("probs_turned")
        turned_a = s.sem("turned_copied_by_act")
        turned_d = s.sem("turned_copied_by_dve")
        pv_done = s.sem("pv_done")
        heads_ready = s.sem("heads_ready")
        out_done = s.sem("out_done")
        x_updated = s.sem("x_updated")

        src_tile = ctx_in.rearrange("(t b) d n -> (b d) t n", b=2)
        src_batch = ctx_in.rearrange("(t b) d n -> d t b n", b=2)

        turn = Turns(BODY0, STEPS0, 6)
        exists = turn.exists

        def tile_of(i, j):
            return 2 * i + j // UNITS

        with nc.Block() as block:

            @block.sync
            def _(sp):
                def load(t, k, i):
                    wait(sp, scores_done, UNITS * (t - 1))
                    sp.dma_start(ctx_tile[:, k, :], src_tile[:, t, :]).then_inc(ctx_loaded[k], 16)
                    for half in range(2):
                        sp.dma_start(ctx_twice[half * S:(half + 1) * S, k], src_batch[:, t]).then_inc(ctx_loaded[k], 16)

                for k in range(2):
                    load(k, k, 0)
                prefetch(sp)
                with sp.Fori(1, TILES // 2) as i:
                    for k in range(2):
                        load(2 * i + k, k, i)

            @block.gpsimd
            def _(pool):
                def part_context(i, j, b):
                    t, k = tile_of(i, j), j // UNITS % 2
                    pool.wait_ge(ctx_loaded[k], 48 * (i + j // BODY0 + 1))
                    wait(pool, scores_done, UNITS * (t - 1))
                    nc.gpsimd.tensor_tensor(ctx_split[:, k, b, 0, :], ctx_twice[:, k, b, :], one[:].to_broadcast([P, D]),
                                            ALU.mult).then_inc(ctx_high, 1)
                    pool.wait_ge(ctx_high, 2 * t + b + 1)
                    nc.gpsimd.tensor_tensor(ctx_split[:, k, b, 1, :], ctx_twice[:, k, b, :], ctx_split[:, k, b, 0, :],
                                            ALU.subtract).then_inc(ctx_parted, 1)

                def normalise(i, j):
                    pool.wait_ge(rden_ready, BODY0 * i + j + 1)
                    p3 = probs[:, j % 4]
                    nc.gpsimd.tensor_tensor(p3, p3, rden[:, j % 4, :].unsqueeze(2).to_broadcast([P, 4, D]),
                                            ALU.mult).then_inc(probs_ready, 1)

                def step(i, j):
                    if exists(i, j):
                        normalise(i, j)
                    b = j % UNITS - CTX_AT
                    if b in (0, 1) and exists(i, j - b + UNITS - CTX_AT):
                        part_context(i, j - b + UNITS - CTX_AT, b)

                nc.gpsimd.memset(one[:], 1.0).then_inc(one_made, 1)
                pool.wait_ge(one_made, 1)
                for b in range(2):
                    part_context(0, 0, b)
                turn.run(pool, step)

            @block.tensor
            def _(pe):
                def project(i, j):
                    t, g, k, b = tile_of(i, j), BODY0 * i + j, j // UNITS % 2, j % 2
                    pe.wait_ge(x_parted, 2 * t + b + 1)
                    wait(pe, q_ready, 2 * g)
                    if (j - 3) % UNITS == 7:
                        wait(pe, ctxT_ready, turn.at_most(tile_of(i, j - 3) + 2, TILES))
                    if (j - 9) % UNITS >= UNITS - 2:
                        wait(pe, x_updated, 2 * tile_of(i, j - 9) + (j - 9) % 2 + 1)
                    for part in range(2):
                        last = nc.tensor.matmul(ps_q[:, 0, :], score_w[:, j // 2 % 4, part, :], x_split[:, k, b, :],
                                                start=(part == 0), stop=(part == 1))
                    last.then_inc(q_done, 1)

                def turn_context(i, j):
                    t, k = tile_of(i, j), j // UNITS % 2
                    pe.wait_ge(ctx_loaded[k], 48 * (i + (j // BODY0) + 1))
                    wait(pe, q_ready, 2 * (BODY0 * i + j - UNITS + 3))
                    wait(pe, x_updated, 2 * (t - 1))
                    for c in range(2):
                        last = nc.tensor.transpose(ps_q[:, 1, c * P:(c + 1) * P],
                                                   ctx_tile[:, k, c * P:(c + 1) * P], ident[:])
                    last.then_inc(ctxT_done, 1)

                def score(i, j):
                    g, k, b = BODY0 * i + j, j // UNITS, j % 2
                    pe.wait_ge(q_ready, 2 * (g + 1))
                    pe.wait_ge(ctx_parted, 2 * tile_of(i, j) + b + 1)
                    wait(pe, exp_ready, g - 1)
                    for r in range(2):
                        for qb in range(2):
                            for part in range(2):
                                last = nc.tensor.matmul(ps_s[:, j % 2, 2 * r + qb, :],
                                                        q_split[:, j % 4, r, qb * P:(qb + 1) * P],
                                                        ctx_split[:, k, b, part, :], start=(part == 0), stop=(part == 1))
                    last.then_inc(scores_done, 1)

                def turn_probs(i, j):
                    g = BODY0 * i + j
                    pe.wait_ge(probs_ready, g + 1)
                    wait(pe, turned_a, g)
                    wait(pe, turned_d, g)
                    for r in range(2):
                        for kb in range(2):
                            for qb in range(2):
                                last = nc.tensor.transpose(ps_pT[:, r, kb, qb * P:(qb + 1) * P],
                                                           probs[:, j % 4, 2 * r + qb, kb * P:(kb + 1) * P], ident[:])
                    last.then_inc(turned, 1)

                def values(i, j):
                    g, k, b = BODY0 * i + j, j // UNITS % 2, j % 2
                    pe.wait_ge(turned_a, g + 1)
                    pe.wait_ge(turned_d, g + 1)
                    pe.wait_ge(ctxT_ready, tile_of(i, j) + 1)
                    wait(pe, heads_ready, g)
                    for kb in range(2):
                        for r in range(2):
                            last = nc.tensor.matmul(ps_o[r * E0:(r + 1) * E0, :],
                                                    ctx_T[:, k, kb, b * E0:(b + 1) * E0],
                                                    probs_T[:, j % 2, r, kb, :], start=(kb == 0), stop=(kb == 1),
                                                    skip_group_check=True)
                    last.then_inc(pv_done, 1)

                def output(i, j):
                    t, b = tile_of(i, j), j % 2
                    pe.wait_ge(heads_ready, BODY0 * i + j + 1)
                    wait(pe, x_updated, 2 * t + b)
                    pe.wait_ge(q_ready, turn.at_most(2 * (BODY0 * i + j + 8), 2 * STEPS0))
                    for pr in range(4):
                        last = nc.tensor.matmul(ps_q[b * E0:(b + 1) * E0, 1, :], out_w[:, pr, :],
                                                heads[:, b, pr, :], start=(pr == 0), stop=(pr == 3),
                                                skip_group_check=True)
                    last.then_inc(out_done, 1)

                def step(i, j):
                    if exists(i, j):
                        score(i, j)
                    if exists(i, j - 3):
                        turn_probs(i, j - 3)
                    if exists(i, j - 4):
                        values(i, j - 4)
                    if (j - 5) % UNITS >= UNITS - 2 and exists(i, j - 5):
                        output(i, j - 5)
                    if j % UNITS == 6 and exists(i, j + UNITS):
                        turn_context(i, j + UNITS)
                    if exists(i, j + 3):
                        project(i, j + 3)

                turn_context(0, 0)
                for j in range(3):
                    project(0, j)
                turn.run(pe, step)

            @block.scalar
            def _(act):
                def copy_context(i, j):
                    t = tile_of(i, j)
                    act.wait_ge(ctxT_done, t + 1)
                    act.wait_ge(q_done, 1 if isinstance(t, int) and t == 0 else BODY0 * i + j - UNITS + 3)
                    wait(act, pv_done, UNITS * (t - 1))
                    nc.scalar.copy(ctx_T[:, j // UNITS % 2].rearrange("p k c -> p (k c)"), ps_q[:, 1, :]).then_inc(ctxT_ready, 1)

                def keep_x_high(i, j):
                    t, k = tile_of(i, j), j // UNITS % 2
                    act.wait_ge(xn_ready, t + 1)
                    wait(act, q_done, UNITS * (t - 1))
                    for b in range(2):
                        r = slice(b * S, (b + 1) * S)
                        nc.scalar.copy(x_split[r, k, b, :], xn[r, k, :]).then_inc(x_high, 1)

                def keep_q_high(i, j):
                    g = BODY0 * i + j
                    act.wait_ge(q_done, g + 1)
                    wait(act, scores_done, g - 3)
                    nc.scalar.copy(q_split[0:E0, j % 4, 0, :], ps_q[0:E0, 0, :]).then_inc(q_high_a, 1)

                def exponents(i, j):
                    g = BODY0 * i + j
                    act.wait_ge(max_ready, g + 1)
                    wait(act, turned, g - 3)
                    for c in range(4):
                        last = nc.scalar.activation(probs[:, j % 4, c, :], ps_s[:, j % 2, c, :], ACT.Exp,
                                                    bias=neg_max[:, j % 4, c:c + 1], scale=1.0,
                                                    accum_out=den[:, j % 4, c:c + 1])
                    last.then_inc(exp_ready, 1)

                def copy_turned(i, j):
                    g = BODY0 * i + j
                    act.wait_ge(turned, g + 1)
                    wait(act, pv_done, g - 1)
                    nc.scalar.copy(probs_T[:, j % 2, 0], ps_pT[:, 0]).then_inc(turned_a, 1)

                def copy_heads(i, j):
                    t, b = tile_of(i, j), j % 2
                    act.wait_ge(pv_done, BODY0 * i + j + 1)
                    wait(act, out_done, 2 * (t - 1) + b + 1)
                    nc.scalar.copy(heads[:, b, j // 2 % 4, :], ps_o[:]).then_inc(heads_ready, 1)

                def step(i, j):
                    if j % UNITS == 7 and exists(i, j + UNITS):
                        copy_context(i, j + UNITS)
                    if exists(i, j + 2):
                        keep_q_high(i, j + 2)
                    if exists(i, j - 1):
                        exponents(i, j - 1)
                    if exists(i, j - 3):
                        copy_turned(i, j - 3)
                    if exists(i, j - 4):
                        copy_heads(i, j - 4)
                    if j % UNITS == 1 and exists(i, j + UNITS):
                        keep_x_high(i, j + UNITS)

                keep_x_high(0, 0)
                copy_context(0, 0)
                for j in range(2):
                    keep_q_high(0, j)
                turn.run(act, step)

            @block.vector
            def _(dve):
                def normalise_rows(i, j):
                    t = tile_of(i, j)
                    wait(dve, x_parted, 2 * (t - 1))
                    nc.vector.tensor_scalar(xn[:, j // UNITS % 2, :], x_all[:, t, :], mean_var[:, t, 0:1],
                                            rstd[:, t:t + 1] if isinstance(t, int) else rstd[:, bass.ds(t, 1)],
                                            ALU.subtract, ALU.mult).then_inc(xn_ready, 1)

                def part_rows(i, j):
                    t, k = tile_of(i, j), j // UNITS % 2
                    dve.wait_ge(x_high, 2 * t + 2)
                    wait(dve, q_done, UNITS * (t - 1))
                    for b in range(2):
                        own, other = slice(b * S, (b + 1) * S), slice((1 - b) * S, (2 - b) * S)
                        nc.vector.tensor_tensor(x_split[other, k, b, :], xn[own, k, :], x_split[own, k, b, :],
                                                ALU.subtract).then_inc(x_parted, 1)

                def part_q(i, j):
                    g = BODY0 * i + j
                    dve.wait_ge(q_high_a, g + 1)
                    wait(dve, scores_done, g - 3)
                    nc.vector.tensor_copy(q_split[E0:P, j % 4, 1, :], ps_q[E0:P, 0, :]).then_inc(q_high_d, 1)
                    nc.vector.tensor_tensor(q_split[E0:P, j % 4, 0, :], ps_q[0:E0, 0, :], q_split[0:E0, j % 4, 0, :],
                                            ALU.subtract).then_inc(q_ready, 1)
                    dve.wait_ge(q_high_d, g + 1)
                    nc.vector.tensor_tensor(q_split[0:E0, j % 4, 1, :], ps_q[E0:P, 0, :], q_split[E0:P, j % 4, 1, :],
                                            ALU.subtract).then_inc(q_ready, 1)

                def maxima(i, j):
                    g = BODY0 * i + j
                    dve.wait_ge(scores_done, g + 1)
                    wait(dve, exp_ready, g - 3)
                    nc.vector.tensor_reduce(neg_max[:, j % 4, :], ps_s[:, j % 2], AX.X, ALU.max,
                                            negate=True).then_inc(max_ready, 1)

                def copy_turned(i, j):
                    g = BODY0 * i + j
                    dve.wait_ge(turned, g + 1)
                    wait(dve, pv_done, g - 1)
                    nc.vector.tensor_copy(probs_T[:, j % 2, 1], ps_pT[:, 1]).then_inc(turned_d, 1)

                def denominators(i, j):
                    g = BODY0 * i + j
                    dve.wait_ge(exp_ready, g + 1)
                    wait(dve, probs_ready, g - 3)
                    nc.vector.reciprocal(rden[:, j % 4, :], den[:, j % 4, :]).then_inc(rden_ready, 1)

                def update(i, j):
                    t, b = tile_of(i, j), j % 2
                    r = slice(b * S, (b + 1) * S)
                    dve.wait_ge(out_done, 2 * t + b + 1)
                    dve.wait_ge(q_high_a, turn.at_most(BODY0 * i + j + 9, STEPS0))
                    nc.vector.scalar_tensor_tensor(x_all[r, t, :], ps_q[r, 1, :], bias0[r, 0:1], x_all[r, t, :],
                                                   ALU.add, ALU.add).then_inc(x_updated, 1)

                def step(i, j):
                    if (j - 6) % UNITS >= UNITS - 2 and exists(i, j - 6):
                        update(i, j - 6)
                    if exists(i, j + 2):
                        part_q(i, j + 2)
                    if exists(i, j):
                        maxima(i, j)
                    if exists(i, j - 1):
                        denominators(i, j - 1)
                    if exists(i, j - 3):
                        copy_turned(i, j - 3)
                    if j % UNITS == 0 and exists(i, j + UNITS):
                        normalise_rows(i, j + UNITS)
                    if j % UNITS == 2 and exists(i, j + UNITS):
                        part_rows(i, j + UNITS)

                normalise_rows(0, 0)
                part_rows(0, 0)
                for j in range(2):
                    part_q(0, j)
                turn.run(dve, step)
E = 8
HID0 = 352
CHUNKS0 = [(0, 128), (128, 128), (256, 96)]
CAP = NB * S // E
SLOTS = E * CAP
FAR = 2 * SLOTS


def load_first_experts(eng, W1, W3, W2, w13, w2, loaded):
    for k in range(2):
        rows = slice(k * P, (k + 1) * P)
        for h, w in enumerate((W1, W3)):
            eng.dma_start(w13[:, k, :, h * HID0:(h + 1) * HID0],
                          w[:, rows, :].rearrange("e p h -> p e h")).then_inc(loaded, 16)
    for c, (r0, n) in enumerate(CHUNKS0):
        eng.dma_start(w2[0:n, c, :, :], W2[:, r0:r0 + n, :].rearrange("e p d -> p e d")).then_inc(loaded, 16)


FIRST_EXPERTS_LOADED = 16 * 7


def load_shared_expert(eng, sw1, sw3, sw2, s13, s2, loaded):
    for k in range(2):
        for h, w in enumerate((sw1, sw3)):
            eng.dma_start(s13[:, k, h * HID0:(h + 1) * HID0], w[k * P:(k + 1) * P, :]).then_inc(loaded, 16)
    for c, (r0, n) in enumerate(CHUNKS0):
        eng.dma_start(s2[0:n, c, :], sw2[r0:r0 + n, :]).then_inc(loaded, 16)


SHARED_EXPERT_LOADED = 16 * 7


def logits_stage(nc, label, x_all, mean_var, rstd, ident, gate_w, gate_loaded, xn_all, logits):
    with ExitStack() as ctx:
        s = Scope(nc, ctx)
        rows = s.sb(f"rows_{label}", [P, 2, D])
        xT = s.sb(f"xT_{label}", [P, 2, D])
        ps_x = s.ps(f"ps_x_{label}", [P, 2, 512])
        ps_l = s.ps(f"ps_l_{label}", [P, 512])
        rows_ready = s.sem(f"rows_ready_{label}")
        kept = s.sem(f"kept_{label}")
        turned = s.sem(f"rows_turned_{label}")
        xT_ready = s.sem(f"xT_ready_{label}")
        logits_done = s.sem(f"logits_done_{label}")
        logits_kept = s.sem(f"logits_kept_{label}")
        turn = Turns(2, TILES, 1, 2)
        exists = turn.exists
        with nc.Block() as block:

            @block.vector
            def _(dve):
                def step(i, j):
                    if exists(i, j):
                        t = 2 * i + j
                        wait(dve, turned, t - 1)
                        nc.vector.tensor_scalar(rows[:, j, :], x_all[:, t, :], mean_var[:, t, 0:1],
                                                column(rstd, t), ALU.subtract, ALU.mult).then_inc(rows_ready, 1)
                        dve.wait_ge(rows_ready, t + 1)
                        nc.vector.tensor_copy(xn_all[:, t, :], rows[:, j, :]).then_inc(kept, 1)

                turn.run(dve, step)
                dve.wait_ge(logits_done, TILES)
                nc.vector.tensor_copy(logits[:].rearrange("p t e -> p (t e)"), ps_l[:, 0:TILES * E]).then_inc(logits_kept, 1)

            @block.tensor
            def _(pe):
                pe.wait_ge(gate_loaded, 16)

                def step(i, j):
                    if exists(i, j):
                        t = 2 * i + j
                        pe.wait_ge(rows_ready, t + 1)
                        wait(pe, xT_ready, t - 1)
                        for k in range(2):
                            last = nc.tensor.transpose(ps_x[:, j, k * P:(k + 1) * P], rows[:, j, k * P:(k + 1) * P], ident[:])
                        last.then_inc(turned, 1)
                    if exists(i, j - 1):
                        t, m = 2 * i + j - 1, (j - 1) % 2
                        pe.wait_ge(xT_ready, t + 1)
                        for k in range(2):
                            last = nc.tensor.matmul(ps_l[:, E * t:E * t + E] if isinstance(t, int) else ps_l[:, bass.ds(E * t, E)],
                                                    xT[:, m, k * P:(k + 1) * P], gate_w[:, k, :],
                                                    start=(k == 0), stop=(k == 1))
                        last.then_inc(logits_done, 1)

                turn.run(pe, step)

            @block.scalar
            def _(act):
                def step(i, j):
                    if exists(i, j):
                        t = 2 * i + j
                        act.wait_ge(turned, t + 1)
                        wait(act, logits_done, t - 1)
                        nc.scalar.copy(xT[:, j, :], ps_x[:, j, 0:D]).then_inc(xT_ready, 1)

                turn.run(act, step)


def column(a, t):
    return a[:, t:t + 1] if isinstance(t, int) else a[:, bass.ds(t, 1)]


class Chain:

    def __init__(self, eng, sem):
        self.eng, self.sem, self.n = eng, sem, 0

    def __call__(self, instruction):
        self.n += 1
        instruction.then_inc(self.sem, 1)
        self.eng.wait_ge(self.sem, self.n)


def pick_first(link, nc, from_eight, values, best, ranked, rank, one_hot):
    wide = lambda a: a.unsqueeze(2).to_broadcast([P, TILES, E])
    per_expert = from_eight[:].unsqueeze(1).to_broadcast([P, TILES, E])
    link(nc.vector.tensor_reduce(best[:], values[:], AX.X, ALU.max))
    link(nc.vector.tensor_tensor(ranked[:], values[:], wide(best[:]), ALU.is_equal))
    link(nc.vector.tensor_tensor(ranked[:], ranked[:], per_expert, ALU.mult))
    link(nc.vector.tensor_reduce(rank[:], ranked[:], AX.X, ALU.min))
    link(nc.vector.tensor_tensor(one_hot[:], per_expert, wide(rank[:]), ALU.is_equal))


def first_routing(nc, logits, scatter_at, gather_at, gate):
    with ExitStack() as ctx:
        s = Scope(nc, ctx)
        BF = mybir.dt.bfloat16
        wide = lambda a: a.unsqueeze(2).to_broadcast([P, TILES, E])
        from_eight = s.sb("r_from_eight", [P, E])
        best = s.sb("r_best", [P, TILES])
        ranked = s.sb("r_ranked", [P, TILES, E])
        rank = s.sb("r_rank", [P, TILES])
        one_hot = s.sb("r_one_hot", [P, TILES, E])
        one_hot_b = s.sb("r_one_hot_b", [P, TILES, E], BF)
        shifted = s.sb("r_shifted", [P, TILES, E])
        total = s.sb("r_total", [P, TILES])
        pos = s.sb("r_pos", [P, TILES])
        keep = s.sb("r_keep", [P, TILES])
        slot = s.sb("r_slot", [P, TILES])
        far = s.sb("r_far", [P, TILES])
        idx = s.sb("r_idx", [P, 2, TILES])
        ones = s.sb("r_ones", [P, P], BF)
        upto = s.sb("r_upto", [P, P], BF)
        ps_c = s.ps("r_ps_c", [P, 512])
        made = s.sem("r_made")
        consts = s.sem("r_consts")
        chain = s.sem("r_chain")
        hot_ready = s.sem("r_hot_ready")
        shift_ready = s.sem("r_shift_ready")
        exp_done = s.sem("r_exp_done")
        counted = s.sem("r_counted")
        with nc.Block() as block:

            @block.gpsimd
            def _(pool):
                nc.gpsimd.iota(from_eight[:], [[1, E]], base=-E, channel_multiplier=0,
                               allow_small_or_imprecise_dtypes=True).then_inc(consts, 1)
                nc.gpsimd.iota(far[:], [[P, TILES]], base=FAR, channel_multiplier=1,
                               allow_small_or_imprecise_dtypes=True).then_inc(consts, 1)
                nc.gpsimd.memset(ones[:], 1.0).then_inc(made, 1)
                pool.wait_ge(made, 1)
                nc.gpsimd.affine_select(out=upto[:], in_=ones[:], compare_op=ALU.is_ge, fill=0.0, base=0,
                                        pattern=[[1, P]], channel_multiplier=-1).then_inc(consts, 1)

            @block.vector
            def _(dve):
                link = Chain(dve, chain)
                dve.wait_ge(consts, 3)
                pick_first(link, nc, from_eight, logits, best, ranked, rank, one_hot)
                nc.vector.tensor_copy(one_hot_b[:], one_hot[:]).then_inc(hot_ready, 1)
                nc.vector.tensor_tensor(shifted[:], logits[:], wide(best[:]), ALU.subtract).then_inc(shift_ready, 1)
                dve.wait_ge(exp_done, 1)
                link(nc.vector.tensor_reduce(total[:], shifted[:], AX.X, ALU.add))
                link(nc.vector.reciprocal(gate[:], total[:]))
                dve.wait_ge(counted, 1)
                link(nc.vector.tensor_tensor(ranked[:], one_hot[:], ps_c[:, 0:TILES * E].rearrange("p (t e) -> p t e", e=E),
                                             ALU.mult))
                link(nc.vector.tensor_reduce(pos[:], ranked[:], AX.X, ALU.add))
                link(nc.vector.tensor_scalar(keep[:], pos[:], float(CAP), None, ALU.is_le))
                link(nc.vector.tensor_tensor(gate[:], gate[:], keep[:], ALU.mult))
                link(nc.vector.tensor_scalar(slot[:], rank[:], float(CAP), float(E * CAP - 1), ALU.mult, ALU.add))
                link(nc.vector.tensor_tensor(slot[:], slot[:], pos[:], ALU.add))
                link(nc.vector.tensor_tensor(idx[:, 0, :], slot[:], far[:], ALU.subtract))
                link(nc.vector.tensor_tensor(idx[:, 0, :], idx[:, 0, :], keep[:], ALU.mult))
                link(nc.vector.tensor_tensor(idx[:, 0, :], idx[:, 0, :], far[:], ALU.add))
                link(nc.vector.tensor_scalar(idx[:, 1, :], slot[:], float(-(SLOTS - 1)), None, ALU.add))
                link(nc.vector.tensor_tensor(idx[:, 1, :], idx[:, 1, :], keep[:], ALU.mult))
                link(nc.vector.tensor_scalar(idx[:, 1, :], idx[:, 1, :], float(SLOTS - 1), None, ALU.add))
                link(nc.vector.tensor_copy(scatter_at[:], idx[:, 0, :]))
                link(nc.vector.tensor_copy(gather_at[:], idx[:, 1, :]))

            @block.scalar
            def _(act):
                act.wait_ge(shift_ready, 1)
                nc.scalar.activation(shifted[:], shifted[:], ACT.Exp).then_inc(exp_done, 1)

            @block.tensor
            def _(pe):
                pe.wait_ge(hot_ready, 1)
                pe.wait_ge(consts, 3)
                hot = one_hot_b[:].rearrange("p t e -> p (t e)")
                last = nc.tensor.matmul(ps_c[:, 0:TILES * E], upto[:], hot, start=True, stop=False)
                for back in range(1, TILES):
                    last = nc.tensor.matmul(ps_c[:, back * E:TILES * E], ones[:], hot[:, 0:(TILES - back) * E],
                                            start=False, stop=(back == TILES - 1))
                last.then_inc(counted, 1)


def first_ffn(nc, label, ident, weights, weights_loaded, x_all=None, xn_all=None, table=None, results=None, extra_pool=None):
    w13_of, w2_of = weights
    with ExitStack() as ctx:
        s = Scope(nc, ctx)
        rows = s.sb(f"rows_{label}", [P, 2, D])
        xT = s.sb(f"xT_{label}", [P, 2, D])
        hid = s.sb(f"hid_{label}", [P, 2, HID0])
        hT = s.sb(f"hT_{label}", [P, 2, 3, P])
        y = s.sb(f"y_{label}", [P, 2, D])
        ps_x = s.ps(f"ps_x_{label}", [P, 512])
        ps_h = s.ps(f"ps_h_{label}", [P, 2, 2, 512])
        ps_hT = s.ps(f"ps_hT_{label}", [P, 512])
        ps_y = s.ps(f"ps_y_{label}", [P, 512])
        rows_ready = [s.sem(f"rows_ready{k}_{label}") for k in range(2)]
        rows_turned = s.sem(f"rows_turned_{label}")
        xT_ready = s.sem(f"xT_ready_{label}")
        h_done = s.sem(f"h_done_{label}")
        silu_ready = s.sem(f"silu_ready_{label}")
        hid_ready = s.sem(f"hid_ready_{label}")
        hid_turned = s.sem(f"hid_turned_{label}")
        hT_ready = s.sem(f"hT_ready_{label}")
        y_done = s.sem(f"y_done_{label}")
        y_used = s.sem(f"y_used_{label}")
        stored = [s.sem(f"stored{k}_{label}") for k in range(2)]
        each = 16 if table is not None else 1
        turn = Turns(2, TILES, 4, 2)
        exists = turn.exists
        with nc.Block() as block:
            if extra_pool is not None:
                block.gpsimd(extra_pool)

            @block.sync
            def _(sp):
                if table is None:
                    return

                def step(i, j):
                    if exists(i, j):
                        n = 2 * i + j
                        wait(sp, rows_turned, n - 1)
                        sp.dma_start(rows[:, j, :], table[n]).then_inc(rows_ready[j], 16)
                    if exists(i, j - 3):
                        n = 2 * i + j - 3
                        sp.wait_ge(y_used, n + 1)
                        sp.dma_start(results[n], y[:, (j - 3) % 2, :]).then_inc(stored[(j - 3) % 2], 16)

                for j in range(2):
                    step(0, j)
                for i in range(1, TILES // 2 + 2):
                    for j in range(2):
                        step(i, j)
                for k in range(2):
                    sp.wait_ge(stored[k], 16 * TILES // 2)

            @block.tensor
            def _(pe):
                def turn_rows(i, j):
                    n = 2 * i + j
                    pe.wait_ge(rows_ready[j % 2], each * (i + 1))
                    wait(pe, xT_ready, n)
                    for k in range(2):
                        last = nc.tensor.transpose(ps_x[:, k * P:(k + 1) * P], rows[:, j % 2, k * P:(k + 1) * P], ident[:])
                    last.then_inc(rows_turned, 1)

                def hidden(i, j):
                    n, m = 2 * i + j, j % 2
                    pe.wait_ge(xT_ready, n + 1)
                    wait(pe, hid_ready, n - 1)
                    for h in range(2):
                        for k in range(2):
                            last = nc.tensor.matmul(ps_h[:, m, h, 0:HID0], xT[:, m, k * P:(k + 1) * P],
                                                    w13_of(i + j // 2, k)[:, h * HID0:(h + 1) * HID0],
                                                    start=(k == 0), stop=(k == 1))
                    last.then_inc(h_done, 1)

                def turn_hidden(i, j):
                    n, m = 2 * i + j, j % 2
                    pe.wait_ge(hid_ready, n + 1)
                    wait(pe, hT_ready, n)
                    for c, (r0, w) in enumerate(CHUNKS0):
                        last = nc.tensor.transpose(ps_hT[0:w, c * P:(c + 1) * P], hid[:, m, r0:r0 + w], ident[:])
                    last.then_inc(hid_turned, 1)

                def down(i, j):
                    n, m = 2 * i + j, j % 2
                    pe.wait_ge(hT_ready, n + 1)
                    wait(pe, y_used, n)
                    for c, (r0, w) in enumerate(CHUNKS0):
                        last = nc.tensor.matmul(ps_y[:, 0:D], hT[0:w, m, c, :], w2_of(i + j // 2, c)[0:w, :],
                                                start=(c == 0), stop=(c == 2))
                    last.then_inc(y_done, 1)

                def step(i, j):
                    if exists(i, j):
                        turn_rows(i, j)
                    if exists(i, j - 2):
                        turn_hidden(i, j - 2)
                    if exists(i, j - 1):
                        hidden(i, j - 1)
                    if exists(i, j - 2):
                        down(i, j - 2)

                pe.wait_ge(*weights_loaded)
                turn.run(pe, step)

            @block.scalar
            def _(act):
                def step(i, j):
                    if exists(i, j):
                        n = 2 * i + j
                        act.wait_ge(rows_turned, n + 1)
                        wait(act, h_done, n - 1)
                        nc.scalar.copy(xT[:, j, :], ps_x[:, 0:D]).then_inc(xT_ready, 1)
                    if exists(i, j - 2):
                        n = 2 * i + j - 2
                        act.wait_ge(hid_turned, n + 1)
                        wait(act, y_done, n - 1)
                        w = CHUNKS0[2][1]
                        nc.scalar.copy(hT[0:w, j, 2, :], ps_hT[0:w, 2 * P:3 * P])
                        nc.scalar.copy(hT[:, j, 0:2, :], ps_hT[:, 0:2 * P].rearrange("p (c n) -> p c n", c=2)).then_inc(hT_ready, 1)
                    if exists(i, j - 1):
                        n = 2 * i + j - 1
                        act.wait_ge(h_done, n + 1)
                        wait(act, hid_turned, n - 1)
                        nc.scalar.activation(hid[:, (j - 1) % 2, :], ps_h[:, (j - 1) % 2, 0, 0:HID0],
                                             ACT.Silu).then_inc(silu_ready, 1)

                turn.run(act, step)

            @block.vector
            def _(dve):
                def step(i, j):
                    if table is None and exists(i, j):
                        n = 2 * i + j
                        wait(dve, rows_turned, n - 1)
                        nc.vector.tensor_copy(rows[:, j, :], xn_all[:, n, :]).then_inc(rows_ready[j], 1)
                    if exists(i, j - 1):
                        n, m = 2 * i + j - 1, (j - 1) % 2
                        dve.wait_ge(silu_ready, n + 1)
                        nc.vector.tensor_tensor(hid[:, m, :], hid[:, m, :], ps_h[:, m, 1, 0:HID0], ALU.mult).then_inc(hid_ready, 1)
                    if exists(i, j - 2):
                        n = 2 * i + j - 2
                        dve.wait_ge(y_done, n + 1)
                        if table is None:
                            nc.vector.tensor_tensor(x_all[:, n, :], x_all[:, n, :], ps_y[:, 0:D], ALU.add).then_inc(y_used, 1)
                        else:
                            wait(dve, stored[j], 16 * (i - 1))
                            nc.vector.tensor_copy(y[:, j, :], ps_y[:, 0:D]).then_inc(y_used, 1)

                turn.run(dve, step)


def first_experts(nc, x_all, mean_var, rstd, ident, Wg, shared_weights, w13, w2, loaded, table, results, table_zeroed,
                  gather_at, gate, prefetch):
    with ExitStack() as ctx:
        s = Scope(nc, ctx)
        xn_all = s.sb("xn_all_f", [P, TILES, D])
        logits = s.sb("logits_f", [P, TILES, E])
        gate_w = s.sb("gate_w_f", [P, 2, E])
        scatter_at = s.sb("scatter_at", [P, TILES], I32)
        s13 = s.sb("s13", [P, 2, 2 * HID0])
        s2 = s.sb("s2", [P, 3, D])
        gate_loaded = s.sem("gate_loaded_f")
        shared_loaded = s.sem("shared_loaded")
        scattered = s.sem("scattered")
        with nc.Block() as block:

            @block.sync
            def _(sp):
                sp.dma_start(gate_w[:], Wg.rearrange("(k p) e -> p k e", p=P)).then_inc(gate_loaded, 16)
                load_shared_expert(sp, *shared_weights, s13, s2, shared_loaded)
                prefetch(sp)

        logits_stage(nc, "f", x_all, mean_var, rstd, ident, gate_w, gate_loaded, xn_all, logits)
        first_routing(nc, logits, scatter_at, gather_at, gate)

        def scatter(pool):
            pool.wait_ge(table_zeroed, 16 * TILES)
            for t in range(TILES):
                nc.gpsimd.indirect_dma_start(out=table, out_offset=bass.IndirectOffsetOnAxis(ap=scatter_at[:, t:t + 1], axis=0),
                                             in_=xn_all[:, t, :], in_offset=None,
                                             bounds_check=SLOTS - 1, oob_is_err=False).then_inc(scattered, 16)
            pool.wait_ge(scattered, 16 * TILES)

        first_ffn(nc, "shared", ident, (lambda e, k: s13[:, k, :], lambda e, c: s2[:, c, :]),
                  (shared_loaded, SHARED_EXPERT_LOADED), x_all=x_all, xn_all=xn_all, extra_pool=scatter)
        first_ffn(nc, "experts", ident, (lambda e, k: w13[:, k, e, :], lambda e, c: w2[:, c, e, :]),
                  (loaded, FIRST_EXPERTS_LOADED), table=table.rearrange("(n p) d -> n p d", p=P), results=results.rearrange("(n p) d -> n p d", p=P))
H1 = 16
GROUPS = 4
DH = 128
HG = H1 // GROUPS
KEYS = 2 * S
BODY1 = 2 * GROUPS
STEPS1 = TILES * GROUPS
RMS_EPS = 1e-6
MASKED = -1e30


def load_second_projections(eng, wq, wk, wv, wk_ctx, wv_ctx, q_w, kv_w, loaded):
    eng.dma_start(q_w[:], wq.rearrange("(k p) n -> p k n", p=P)).then_inc(loaded, 16)
    for n, w in enumerate((wk_ctx, wk, wv_ctx, wv)):
        eng.dma_start(kv_w[:, n], w.rearrange("(k p) n -> p k n", p=P)).then_inc(loaded, 16)


def load_second_output(eng, wo, o_w, loaded):
    for n in range(2):
        eng.dma_start(o_w[:, 8 * n:8 * n + 8], wo[n * 1024:(n + 1) * 1024].rearrange("(h p) n -> p h n", p=P)).then_inc(loaded, 16)


SECOND_ATTENTION_LOADED = 16 * 7


def between_layers(nc, x_all, mean_var, rstd, results, gather_at, gate, rope, q_norm, k_norm, tables, mask,
                   q_w, kv_w, loaded, q_parts, kv_parts):
    with ExitStack() as ctx:
        s = Scope(nc, ctx)
        results_got = s.sb("results_got", [P, TILES, D])
        stats = s.sb("stats_c", [P, TILES, 6])
        std = s.sb("std_c", [P, TILES])
        angle = s.sb("rope_angle", [P, 2, DH])
        w = s.sb("rope_w", [P, 2, DH])
        gathered = [s.sem(f"gathered{t}") for t in range(TILES)]
        added = s.sem("experts_added")
        stats_done = s.sem("stats_done_c")
        var_done = s.sem("var_done_c")
        eps_done = s.sem("eps_done_c")
        sqrt_done = s.sem("sqrt_done_c")
        angle_loaded = s.sem("angle_loaded")
        zeros = s.sem("mask_zero")
        steps = s.sem("rope_steps")
        masked = s.sem("mask_made")
        high_made = s.sem("weights_high")
        low_made = s.sem("weights_low")
        pieces = [[a[:, 1024 * n:1024 * (n + 1)] for a in group]
                  for group in ([a[:].rearrange("p k n -> p (k n)") for a in (q_w, *q_parts)],
                                [a[:].rearrange("p w k n -> p (w k n)") for a in (kv_w, *kv_parts)])
                  for n in range(4)]
        with nc.Block() as block:

            @block.sync
            def _(sp):
                for b in range(2):
                    sp.dma_start(angle[b * S:(b + 1) * S], rope.rearrange("c s d -> s c d")).then_inc(angle_loaded, 16)
                for n, v in enumerate((q_norm, k_norm)):
                    sp.dma_start(w[:, n, :], v.rearrange("(o d) -> o d", o=1).to_broadcast([P, DH])).then_inc(angle_loaded, 16)

            @block.gpsimd
            def _(pool):
                nc.gpsimd.memset(mask[:], 0.0).then_inc(zeros, 1)
                pool.wait_ge(zeros, 1)
                for h in range(2):
                    own = mask[h * S:(h + 1) * S, :, S:KEYS]
                    nc.gpsimd.affine_select(out=own, in_=own, compare_op=ALU.is_ge, fill=MASKED, base=0,
                                            pattern=[[0, 4], [-1, S]], channel_multiplier=1).then_inc(masked, 1)
                pool.wait_ge(masked, 2)
                for t in range(TILES):
                    nc.gpsimd.indirect_dma_start(out=results_got[:, t, :], out_offset=None, in_=results,
                                                 in_offset=bass.IndirectOffsetOnAxis(ap=gather_at[:, t:t + 1], axis=0),
                                                 bounds_check=SLOTS - 1, oob_is_err=False).then_inc(gathered[t], 16)

            @block.scalar
            def _(act):
                act.wait_ge(loaded, SECOND_ATTENTION_LOADED)
                for whole, high, _ in pieces:
                    nc.scalar.copy(high, whole).then_inc(high_made, 1)
                act.wait_ge(eps_done, 1)
                nc.scalar.activation(rstd[:], std[:], ACT.Sqrt).then_inc(sqrt_done, 1)

            @block.vector
            def _(dve):
                def low(n):
                    whole, high, rest = pieces[n]
                    dve.wait_ge(high_made, n + 1)
                    nc.vector.tensor_tensor(rest, whole, high, ALU.subtract).then_inc(low_made, 1)

                for n in range(2):
                    low(n)
                dve.wait_ge(angle_loaded, 64)
                half = DH // 2
                link = Chain(dve, steps)
                link(nc.vector.tensor_scalar(w[:, 0, :], w[:, 0, :], float(DH) ** -0.5, None, ALU.mult))
                for n, row in ((0, 0), (1, 2)):
                    nc.vector.tensor_tensor(tables[:, row, 0, :], w[:, n, :], angle[:, 0, :], ALU.mult)
                    for a in range(2):
                        o = 1 - a
                        nc.vector.tensor_tensor(tables[:, row, 1, a * half:(a + 1) * half], w[:, n, o * half:(o + 1) * half],
                                                angle[:, 1, a * half:(a + 1) * half], ALU.mult)
                nc.vector.tensor_copy(tables[:, 1, 0, :], w[:, 1, :])
                nc.vector.memset(tables[:, 1, 1, :], 0.0)
                for n in range(2, 8):
                    low(n)
                for t in range(TILES):
                    dve.wait_ge(gathered[t], 16)
                    nc.vector.scalar_tensor_tensor(x_all[:, t, :], results_got[:, t, :], gate[:, t:t + 1], x_all[:, t, :],
                                                   ALU.mult, ALU.add).then_inc(added, 1)
                    if t > 0:
                        dve.wait_ge(added, t)
                        nc.vector.bn_stats(stats[:, t - 1, :], x_all[:, t - 1, :]).then_inc(stats_done, 1)
                dve.wait_ge(added, TILES)
                nc.vector.bn_stats(stats[:, TILES - 1, :], x_all[:, TILES - 1, :]).then_inc(stats_done, 1)
                for t in range(TILES):
                    dve.wait_ge(stats_done, t + 1)
                    nc.vector.bn_aggr(mean_var[:, t, :], stats[:, t, :]).then_inc(var_done, 1)
                dve.wait_ge(var_done, TILES)
                nc.vector.tensor_scalar(std[:], mean_var[:, :, 1], LN_EPS, None, ALU.add).then_inc(eps_done, 1)
                dve.wait_ge(sqrt_done, 1)
                nc.vector.reciprocal(rstd[:], rstd[:])


def second_attention(nc, ctx_in, x_all, mean_var, rstd, ident, q_parts, kv_parts, q_w, kv_w, o_w, tables, mask):
    with ExitStack() as ctx:
        s = Scope(nc, ctx)
        BF = mybir.dt.bfloat16
        ident_b = s.sb("ident_b", [P, P], BF)
        eps = s.sb("rms_eps", [P, 1])
        rows = s.sb("a_rows", [P, 2, 2, D])
        rowsT = [s.sb(f"a_rowsT_{n}", [P, 2, 2, 2, P], F32R) for n in ("high", "low")]
        square = s.sb("a_square", [P, 2, 512])
        mean_sq = s.sb("a_mean_sq", [P, 4, 4])
        log_sq = s.sb("a_log_sq", [P, 4, 4])
        inv_rms = s.sb("a_inv_rms", [P, 4, 4])
        turned_cos = s.sb("a_cos", [P, 2, HG, DH])
        turned_sin = s.sb("a_sin", [P, 2, HG, DH])
        qT = q_w[:].rearrange("p k n -> p (k n)").rearrange("p (t g b h s) -> p t g b h s", t=2, g=GROUPS, b=2, h=HG)
        kT = kv_w[:, 0:2].rearrange("p w k n -> p (w k n)").rearrange("p (t b g n) -> p t b g n", t=2, b=2, g=GROUPS)
        v = kv_w[:, 2:4]
        neg_max = s.sb("a_neg_max", [P, 2, 4])
        den = s.sb("a_den", [P, 2, 4])
        rden = s.sb("a_rden", [P, 2, 4])
        probs = s.sb("a_probs", [P, 2, 4, KEYS])
        probs_T = s.sb("a_probs_T", [P, 2, 4, P])
        heads = s.sb("a_heads", [P, 2, HG, 2, S])
        ps_p = [s.ps(f"a_ps_p{n}", [P, 512]) for n in range(2)]
        ps_r = s.ps("a_ps_r", [P, 512])
        ps_s = s.ps("a_ps_s", [P, 4, KEYS])
        ps_pT = s.ps("a_ps_pT", [P, 4, P])
        ps_o = s.ps("a_ps_o", [P, 2, HG, S])
        ps_y = s.ps("a_ps_y", [P, 512])
        ps_x = s.ps("a_ps_x", [P, 512])

        ident_cast = s.sem("ident_cast")
        ctx_loaded = [s.sem(f"a_ctx_loaded{k}") for k in range(2)]
        xn_ready = s.sem("a_xn_ready")
        rows_turned = s.sem("a_rows_turned")
        rows_high = s.sem("a_rows_high")
        rowsT_ready = s.sem("a_rowsT_ready")
        projected = [s.sem(f"a_projected{n}") for n in range(2)]
        v_kept = [s.sem(f"a_v_kept{n}") for n in range(2)]
        squared = [s.sem(f"a_squared{n}") for n in range(2)]
        summed = [s.sem(f"a_summed{n}") for n in range(2)]
        log_done = s.sem("a_log_done")
        inv_ready = [s.sem(f"a_inv_ready{n}") for n in range(2)]
        rotated = [s.sem(f"a_rotated{n}") for n in range(2)]
        summed_up = s.sem("a_summed_up")
        roped = [s.sem(f"a_roped{n}") for n in range(2)]
        rope_turned = [s.sem(f"a_rope_turned{n}") for n in range(2)]
        rope_kept = [s.sem(f"a_rope_kept{n}") for n in range(2)]
        scores_done = s.sem("a_scores_done")
        max_ready = s.sem("a_max_ready")
        exp_ready = s.sem("a_exp_ready")
        rden_ready = s.sem("a_rden_ready")
        probs_ready = s.sem("a_probs_ready")
        probs_turned = s.sem("a_probs_turned")
        probsT_ready = s.sem("a_probsT_ready")
        pv_done = s.sem("a_pv_done")
        heads_ready = s.sem("a_heads_ready")
        out_done = s.sem("a_out_done")
        x_updated = s.sem("a_x_updated")

        turn = Turns(BODY1, STEPS1, GROUPS + 2)
        exists = turn.exists
        src_tile = ctx_in.rearrange("(t b) d n -> (b d) t n", b=2)

        def is_v(j):
            return j % GROUPS == 1

        def rope_steps(i, j):
            return 3 * (2 * i + j // GROUPS) + (0, 1, 1, 2)[j % GROUPS]

        with nc.Block() as block:

            @block.sync
            def _(sp):
                for k in range(2):
                    sp.dma_start(rows[:, k, 1, :], src_tile[:, k, :]).then_inc(ctx_loaded[k], 16)
                with sp.Fori(1, TILES // 2) as i:
                    for k in range(2):
                        sp.wait_ge(rows_turned, 2 * i + k - 1)
                        sp.dma_start(rows[:, k, 1, :], src_tile[:, 2 * i + k, :]).then_inc(ctx_loaded[k], 16)

            @block.gpsimd
            def _(pool):
                nc.gpsimd.memset(eps[:], RMS_EPS)
                nc.gpsimd.tensor_copy(ident_b[:], ident[:]).then_inc(ident_cast, 1)

                def rope(i, j, n):
                    r = rope_steps(i, j)
                    pool.wait_ge(rotated[n], r + 1)
                    nc.gpsimd.tensor_tensor(turned_cos[:, n], turned_cos[:, n], turned_sin[:, n], ALU.add).then_inc(summed_up, 1)
                    pool.wait_ge(summed_up, 2 * r + n + 1)
                    pool.wait_ge(inv_ready[n], r + 1)
                    nc.gpsimd.tensor_tensor(turned_cos[:, n], turned_cos[:, n],
                                            inv_rms[:, 2 * (j % 2) + n, :].unsqueeze(2).to_broadcast([P, HG, DH]),
                                            ALU.mult).then_inc(roped[n], 1)

                def normalise(i, j):
                    u, m = BODY1 * i + j, j % 2
                    pool.wait_ge(rden_ready, u + 1)
                    nc.gpsimd.tensor_tensor(probs[:, m], probs[:, m], rden[:, m, :].unsqueeze(2).to_broadcast([P, 4, KEYS]),
                                            ALU.mult).then_inc(probs_ready, 1)

                def step(i, j):
                    if exists(i, j - 4):
                        normalise(i, j - 4)
                    if exists(i, j) and not is_v(j):
                        for n in range(2):
                            rope(i, j, n)

                turn.run(pool, step)

            @block.tensor
            def _(pe):
                def turn_rows(i, j):
                    t, k = 2 * i + j // GROUPS, j // GROUPS % 2
                    pe.wait_ge(xn_ready, t + 1)
                    pe.wait_ge(ctx_loaded[k], 16 * (i + j // BODY1 + 1))
                    wait(pe, rowsT_ready, t)
                    for a in range(2):
                        for c in range(2):
                            last = nc.tensor.transpose(ps_x[:, (2 * a + c) * P:(2 * a + c + 1) * P],
                                                       rows[:, k, a, c * P:(c + 1) * P], ident[:])
                    last.then_inc(rows_turned, 1)

                def project(i, j, n):
                    t, k = 2 * i + j // GROUPS, j // GROUPS
                    u = BODY1 * i + j
                    if n == 0:
                        pe.wait_ge(rowsT_ready, t + 1)
                    wait(pe, v_kept[n], 2 * (2 * i + (j + 2) // GROUPS))
                    wait(pe, rotated[n], rope_steps(i, j))
                    if j % GROUPS < 2:
                        source, weights = 1 - n, [w[:, 2 * (j % GROUPS) + n] for w in kv_parts]
                    else:
                        g = 2 * (j % GROUPS - 2) + n
                        source, weights = 0, [w[:, :, g * 512:(g + 1) * 512] for w in q_parts]
                    products = [(c, *parts) for c in range(2) for parts in ((0, 0), (0, 1), (1, 0))]
                    for m, (c, r, w) in enumerate(products):
                        last = nc.tensor.matmul(ps_p[n][:], rowsT[r][:, k, source, c, :], weights[w][:, c, :],
                                                start=(m == 0), stop=(m == 5))
                    last.then_inc(projected[n], 1)

                def turn_rope(i, j, n):
                    r = rope_steps(i, j)
                    pe.wait_ge(roped[n], r + 1)
                    wait(pe, rope_kept[1 - n], r + n)
                    for h in range(HG):
                        last = nc.tensor.transpose(ps_r[:, h * P:(h + 1) * P], turned_cos[:, n, h, :], ident[:])
                    last.then_inc(rope_turned[n], 1)

                def score(i, j):
                    u, k, g = BODY1 * i + j, j // GROUPS % 2, j % GROUPS
                    pe.wait_ge(rope_kept[g % 2], 3 * (2 * i + j // GROUPS) + 2 + g // 2)
                    for n in range(2):
                        pe.wait_ge(rope_kept[n], 3 * (2 * i + j // GROUPS) + 1)
                    wait(pe, exp_ready, u)
                    nc.tensor.matmul(ps_s[:].rearrange("p a b -> p (a b)"), ident_b[:], mask[:].rearrange("p a b -> p (a b)"),
                                     start=True, stop=False)
                    for b in range(2):
                        for m in range(2):
                            last = nc.tensor.matmul(ps_s[:, 2 * b + m, :],
                                                    qT[:, k, g, b, 2 * m:2 * m + 2, :].rearrange("p h s -> p (h s)"),
                                                    kT[:, k, b, g, :], start=False, stop=(b == 1 and m == 1))
                    last.then_inc(scores_done, 1)

                def turn_probs(i, j):
                    u, m = BODY1 * i + j, j % 2
                    pe.wait_ge(probs_ready, u + 1)
                    wait(pe, probsT_ready, u)
                    for a in range(4):
                        last = nc.tensor.transpose(ps_pT[:, a, :], probs[:, m, a, :], ident[:])
                    last.then_inc(probs_turned, 1)

                def values(i, j):
                    u, k, g = BODY1 * i + j, j // GROUPS % 2, j % GROUPS
                    pe.wait_ge(probsT_ready, u + 1)
                    for n in range(2):
                        pe.wait_ge(v_kept[n], 2 * (2 * i + j // GROUPS + 1))
                    wait(pe, heads_ready, u)
                    for b in range(2):
                        last = nc.tensor.matmul(ps_o[:, b].rearrange("p h s -> p (h s)"), v[:, k, b, g * DH:(g + 1) * DH],
                                                probs_T[:, j % 2, 2 * b:2 * b + 2, :].rearrange("p a n -> p (a n)"),
                                                start=True, stop=True)
                    last.then_inc(pv_done, 1)

                def output(i, j):
                    u, g = BODY1 * i + j, j % GROUPS
                    pe.wait_ge(heads_ready, u + 1)
                    if g == 0:
                        wait(pe, x_updated, 2 * i + j // GROUPS)
                    for h in range(HG):
                        last = nc.tensor.matmul(ps_y[:, 0:D], heads[:, j % 2, h].rearrange("p b s -> p (b s)"),
                                                o_w[:, HG * g + h, :], start=(g == 0 and h == 0),
                                                stop=(g == GROUPS - 1 and h == HG - 1))
                    last.then_inc(out_done, 1)

                def step(i, j):
                    if exists(i, j - 4):
                        score(i, j - 4)
                    if exists(i, j - 5):
                        turn_probs(i, j - 5)
                    if exists(i, j):
                        project(i, j, 0)
                    if exists(i, j - 5):
                        values(i, j - 5)
                    if exists(i, j - 1) and not is_v(j - 1):
                        turn_rope(i, j - 1, 0)
                    if j % GROUPS == 3 and exists(i, j + 1):
                        turn_rows(i, j + 1)
                    if exists(i, j):
                        project(i, j, 1)
                    if exists(i, j - 5):
                        output(i, j - 5)
                    if exists(i, j - 1) and not is_v(j - 1):
                        turn_rope(i, j - 1, 1)

                pe.wait_ge(ident_cast, 1)
                turn_rows(0, 0)
                turn.run(pe, step)

            @block.scalar
            def _(act):
                def copy_rows(i, j):
                    t, k = 2 * i + j // GROUPS, j // GROUPS % 2
                    act.wait_ge(rows_turned, t + 1)
                    wait(act, projected[1], GROUPS * (t - 1))
                    nc.scalar.copy(rowsT[0][:, k].rearrange("p a c n -> p (a c n)"), ps_x[:]).then_inc(rows_high, 1)

                def keep_values(i, j, n):
                    u, k = BODY1 * i + j, j // GROUPS
                    act.wait_ge(projected[n], u + 1)
                    wait(act, pv_done, u - 1 - GROUPS)
                    for b in range(2):
                        nc.scalar.copy(v[n * S:(n + 1) * S, k, b, :], ps_p[n][b * S:(b + 1) * S, :]).then_inc(v_kept[n], 1)

                def squares(i, j, n):
                    r = rope_steps(i, j)
                    act.wait_ge(projected[n], BODY1 * i + j + 1)
                    wait(act, summed[n], r)
                    nc.scalar.activation(square[:, n, :], ps_p[n][:], ACT.Square).then_inc(squared[n], 1)

                def inverse(i, j, n):
                    r, c = rope_steps(i, j), 2 * (j % 2) + n
                    act.wait_ge(summed[n], r + 1)
                    nc.scalar.activation(log_sq[:, c, :], mean_sq[:, c, :], ACT.Ln, bias=eps[:, 0:1],
                                         scale=1.0 / DH).then_inc(log_done, 1)
                    act.wait_ge(log_done, 2 * r + n + 1)
                    wait(act, roped[n], r - 1)
                    nc.scalar.activation(inv_rms[:, c, :], log_sq[:, c, :], ACT.Exp, scale=-0.5).then_inc(inv_ready[n], 1)

                def keep_rope(i, j, n):
                    k, r = j // GROUPS % 2, rope_steps(i, j)
                    act.wait_ge(rope_turned[n], r + 1)
                    if j % GROUPS == 0:
                        nc.scalar.copy(kT[:, k, :, :, n * S:(n + 1) * S],
                                       ps_r[:].rearrange("p (g b s) -> p b g s", g=GROUPS, b=2)).then_inc(rope_kept[n], 1)
                    else:
                        g = 2 * (j % GROUPS - 2) + n
                        nc.scalar.copy(qT[:, k, g].rearrange("p b h s -> p h b s"),
                                       ps_r[:].rearrange("p (h b s) -> p h b s", h=HG, b=2)).then_inc(rope_kept[n], 1)

                def exponents(i, j):
                    u, m = BODY1 * i + j, j % 2
                    act.wait_ge(max_ready, u + 1)
                    wait(act, probs_turned, u - 1)
                    for a in range(4):
                        last = nc.scalar.activation(probs[:, m, a, :], ps_s[:, a, :], ACT.Exp, bias=neg_max[:, m, a:a + 1],
                                                    scale=1.0, accum_out=den[:, m, a:a + 1])
                    last.then_inc(exp_ready, 1)

                def keep_heads(i, j):
                    u, m = BODY1 * i + j, j % 2
                    act.wait_ge(pv_done, u + 1)
                    wait(act, out_done, u - 1)
                    nc.scalar.copy(heads[:, m].rearrange("p h b s -> p b h s"), ps_o[:]).then_inc(heads_ready, 1)

                def step(i, j):
                    if exists(i, j - 4):
                        exponents(i, j - 4)
                    rope = exists(i, j) and not is_v(j)
                    if rope:
                        squares(i, j, 0)
                    elif exists(i, j):
                        keep_values(i, j, 0)
                    if exists(i, j - 5):
                        keep_heads(i, j - 5)
                    if exists(i, j - 1) and not is_v(j - 1):
                        keep_rope(i, j - 1, 0)
                    if rope:
                        inverse(i, j, 0)
                    if j % GROUPS == 3 and exists(i, j + 1):
                        copy_rows(i, j + 1)
                    if rope:
                        squares(i, j, 1)
                    elif exists(i, j):
                        keep_values(i, j, 1)
                    if exists(i, j - 1) and not is_v(j - 1):
                        keep_rope(i, j - 1, 1)
                    if rope:
                        inverse(i, j, 1)

                nc.scalar.preload_act_table_set("natural_log_exp_and_others")
                act.wait_ge(ident_cast, 1)
                copy_rows(0, 0)
                turn.run(act, step)

            @block.vector
            def _(dve):
                def normalise_rows(i, j):
                    t, k = 2 * i + j // GROUPS, j // GROUPS % 2
                    wait(dve, rows_turned, t - 1)
                    nc.vector.tensor_scalar(rows[:, k, 0, :], x_all[:, t, :], mean_var[:, t, 0:1], column(rstd, t),
                                            ALU.subtract, ALU.mult).then_inc(xn_ready, 1)

                def part_rows(i, j):
                    t, k = 2 * i + j // GROUPS, j // GROUPS % 2
                    dve.wait_ge(rows_high, t + 1)
                    nc.vector.tensor_tensor(rowsT[1][:, k].rearrange("p a c n -> p (a c n)"), ps_x[:],
                                            rowsT[0][:, k].rearrange("p a c n -> p (a c n)"), ALU.subtract).then_inc(rowsT_ready, 1)

                def rotate(i, j, n):
                    r, c = rope_steps(i, j), 2 * (j % 2) + n
                    row = 1 + n if j % GROUPS == 0 else 0
                    half = DH // 2
                    dve.wait_ge(squared[n], r + 1)
                    nc.vector.tensor_reduce(mean_sq[:, c, :], square[:, n, :].rearrange("p (h d) -> p h d", h=HG),
                                            AX.X, ALU.add).then_inc(summed[n], 1)
                    wait(dve, rope_turned[n], r)
                    job = ps_p[n][:].rearrange("p (h d) -> p h d", h=HG)

                    def table(which, lo, hi):
                        return tables[:, row, which, lo:hi].unsqueeze(1).to_broadcast([P, HG, hi - lo])

                    nc.vector.tensor_tensor(turned_cos[:, n], job, table(0, 0, DH), ALU.mult)
                    nc.vector.tensor_tensor(turned_sin[:, n, :, 0:half], job[:, :, half:DH], table(1, 0, half), ALU.mult)
                    nc.vector.tensor_tensor(turned_sin[:, n, :, half:DH], job[:, :, 0:half], table(1, half, DH),
                                            ALU.mult).then_inc(rotated[n], 1)

                def maxima(i, j):
                    u, m = BODY1 * i + j, j % 2
                    dve.wait_ge(scores_done, u + 1)
                    wait(dve, exp_ready, u - 1)
                    nc.vector.tensor_reduce(neg_max[:, m, :], ps_s[:], AX.X, ALU.max, negate=True).then_inc(max_ready, 1)

                def denominators(i, j):
                    u, m = BODY1 * i + j, j % 2
                    dve.wait_ge(exp_ready, u + 1)
                    wait(dve, probs_ready, u - 1)
                    nc.vector.reciprocal(rden[:, m, :], den[:, m, :]).then_inc(rden_ready, 1)

                def copy_probs(i, j):
                    u, m = BODY1 * i + j, j % 2
                    dve.wait_ge(probs_turned, u + 1)
                    wait(dve, pv_done, u - 1)
                    nc.vector.tensor_copy(probs_T[:, m], ps_pT[:]).then_inc(probsT_ready, 1)

                def update(i, j):
                    t = 2 * i + j // GROUPS
                    dve.wait_ge(out_done, BODY1 * i + j + 1)
                    nc.vector.tensor_tensor(x_all[:, t, :], x_all[:, t, :], ps_y[:, 0:D], ALU.add).then_inc(x_updated, 1)

                def step(i, j):
                    if exists(i, j - 4):
                        maxima(i, j - 4)
                    if exists(i, j - 5):
                        copy_probs(i, j - 5)
                    if exists(i, j - 4):
                        denominators(i, j - 4)
                    if exists(i, j) and not is_v(j):
                        rotate(i, j, 0)
                    if j % GROUPS == 2 and exists(i, j + 2):
                        normalise_rows(i, j + 2)
                    if j % GROUPS == 3 and exists(i, j + 1):
                        part_rows(i, j + 1)
                    if exists(i, j) and not is_v(j):
                        rotate(i, j, 1)
                    if (j - 5) % GROUPS == GROUPS - 1 and exists(i, j - 5):
                        update(i, j - 5)

                normalise_rows(0, 0)
                part_rows(0, 0)
                turn.run(dve, step)
HID1 = 176
BLOCKS1 = E * HID1 // P
GROUP_BLOCKS = [(0, 4), (4, 8), (8, 11)]
GROUP_LAST = [-(-hi * P // HID1) - 1 for _, hi in GROUP_BLOCKS]
BODY2 = 2 * E


def load_second_experts(eng, w_gate, w_up, w_down, w_gu, w_d, loaded):
    for k in range(2):
        for h, w in enumerate((w_gate, w_up)):
            eng.dma_start(w_gu[:, k, :, h * HID1:(h + 1) * HID1],
                          w[:, k * P:(k + 1) * P, :].rearrange("e p f -> p e f")).then_inc(loaded, 16)
    eng.dma_start(w_d[:], w_down.rearrange("e f d -> (e f) d").rearrange("(c p) d -> p c d", p=P)).then_inc(loaded, 16)


SECOND_EXPERTS_LOADED = 16 * 5


def second_routing(nc, logits, combine):
    with ExitStack() as ctx:
        s = Scope(nc, ctx)
        from_eight = s.sb("t_from_eight", [P, E])
        best = [s.sb(f"t_best{n}", [P, TILES]) for n in range(2)]
        hot = [s.sb(f"t_hot{n}", [P, TILES, E]) for n in range(2)]
        ranked = s.sb("t_ranked", [P, TILES, E])
        rank = s.sb("t_rank", [P, TILES])
        rest = s.sb("t_rest", [P, TILES, E])
        ratio = s.sb("t_ratio", [P, TILES])
        total = s.sb("t_total", [P, TILES])
        weight = [s.sb(f"t_weight{n}", [P, TILES]) for n in range(2)]
        consts = s.sem("t_consts")
        chain = s.sem("t_chain")
        diff_ready = s.sem("t_diff_ready")
        exp_done = s.sem("t_exp_done")
        wide = lambda a: a.unsqueeze(2).to_broadcast([P, TILES, E])
        with nc.Block() as block:

            @block.gpsimd
            def _(pool):
                nc.gpsimd.iota(from_eight[:], [[1, E]], base=-E, channel_multiplier=0,
                               allow_small_or_imprecise_dtypes=True).then_inc(consts, 1)

            @block.vector
            def _(dve):
                link = Chain(dve, chain)
                dve.wait_ge(consts, 1)
                pick_first(link, nc, from_eight, logits, best[0], ranked, rank, hot[0])
                link(nc.vector.tensor_scalar(ranked[:], hot[0][:], -3e38, None, ALU.mult))
                link(nc.vector.tensor_tensor(rest[:], logits[:], ranked[:], ALU.add))
                pick_first(link, nc, from_eight, rest, best[1], ranked, rank, hot[1])
                nc.vector.tensor_tensor(ratio[:], best[1][:], best[0][:], ALU.subtract).then_inc(diff_ready, 1)
                dve.wait_ge(exp_done, 1)
                link(nc.vector.tensor_scalar(total[:], ratio[:], 1.0, None, ALU.add))
                link(nc.vector.reciprocal(weight[0][:], total[:]))
                link(nc.vector.tensor_tensor(weight[1][:], weight[0][:], ratio[:], ALU.mult))
                link(nc.vector.tensor_tensor(hot[0][:], hot[0][:], wide(weight[0][:]), ALU.mult))
                link(nc.vector.tensor_tensor(hot[1][:], hot[1][:], wide(weight[1][:]), ALU.mult))
                link(nc.vector.tensor_tensor(combine[:], hot[0][:], hot[1][:], ALU.add))

            @block.scalar
            def _(act):
                act.wait_ge(diff_ready, 1)
                nc.scalar.activation(ratio[:], ratio[:], ACT.Exp).then_inc(exp_done, 1)


def second_ffn(nc, x_all, xn_all, ident, w_gu, w_d, loaded, combine, out):
    with ExitStack() as ctx:
        s = Scope(nc, ctx)
        rows = s.sb("e_rows", [P, 2, D])
        xT = s.sb("e_xT", [P, 2, 2, P])
        act_g = s.sb("e_act_g", [P, 4, HID1])
        hid = s.sb("e_hid", [P, 2, E * HID1])
        hT = s.sb("e_hT", [P, 2, BLOCKS1, P])
        ps_h = [s.ps(f"e_ps_h{n}", [P, 512]) for n in range(4)]
        ps_t = [s.ps(f"e_ps_t{n}", [P, 4, P]) for n in range(2)]
        ps_x = s.ps("e_ps_x", [P, 512])
        ps_y = s.ps("e_ps_y", [P, 512])
        rows_ready = s.sem("e_rows_ready")
        rows_turned = s.sem("e_rows_turned")
        xT_ready = s.sem("e_xT_ready")
        h_done = s.sem("e_h_done")
        silu_ready = s.sem("e_silu_ready")
        hid_ready = s.sem("e_hid_ready")
        turned = s.sem("e_turned")
        hT_ready = s.sem("e_hT_ready")
        y_done = s.sem("e_y_done")
        x_ready = s.sem("e_x_ready")
        stored = s.sem("e_stored")
        turn = Turns(BODY2, TILES * E, E + 3)
        exists = turn.exists
        out_tile = out.rearrange("(t b) d n -> (b d) t n", b=2)
        turn_at = [last + 2 for last in GROUP_LAST]
        down_at = turn_at[2] + 1

        def tile_of(i, j):
            return 2 * i + j // E

        def groups_due(j):
            return [(n, j - at) for n, at in enumerate(turn_at) if (j - at) % E == 0]

        with nc.Block() as block:

            @block.sync
            def _(sp):
                for t in range(TILES):
                    sp.wait_ge(x_ready, t + 1)
                    sp.dma_start(out_tile[:, t, :], x_all[:, t, :]).then_inc(stored, 16)
                sp.wait_ge(stored, 16 * TILES)

            @block.tensor
            def _(pe):
                def turn_rows(i, j):
                    t, k = tile_of(i, j), j // E % 2
                    pe.wait_ge(rows_ready, t + 1)
                    wait(pe, xT_ready, t)
                    for c in range(2):
                        last = nc.tensor.transpose(ps_x[:, c * P:(c + 1) * P], rows[:, k, c * P:(c + 1) * P], ident[:])
                    last.then_inc(rows_turned, 1)

                def hidden(i, j):
                    u, k = BODY2 * i + j, j // E
                    pe.wait_ge(xT_ready, tile_of(i, j) + 1)
                    wait(pe, hid_ready, u - 3)
                    for c in range(2):
                        last = nc.tensor.matmul(ps_h[j % 4][:, 0:2 * HID1], xT[:, k, c, :], w_gu[:, c, j % E, :],
                                                start=(c == 0), stop=(c == 1))
                    last.then_inc(h_done, 1)

                def turn_group(i, j, n):
                    t, k = tile_of(i, j), j // E % 2
                    c = 3 * t + n
                    b = (3 * (j // E) + n) % 2
                    lo, hi = GROUP_BLOCKS[n]
                    pe.wait_ge(hid_ready, BODY2 * i + j + GROUP_LAST[n] + 1)
                    wait(pe, hT_ready, c - 1)
                    for m in range(lo, hi):
                        last = nc.tensor.transpose(ps_t[b][:, m - lo, :], hid[:, k, m * P:(m + 1) * P], ident[:])
                    last.then_inc(turned, 1)

                def down(i, j):
                    t, k = tile_of(i, j), j // E % 2
                    pe.wait_ge(hT_ready, 3 * t + 3)
                    wait(pe, x_ready, t)
                    for m in range(BLOCKS1):
                        last = nc.tensor.matmul(ps_y[:, 0:D], hT[:, k, m, :], w_d[:, m, :],
                                                start=(m == 0), stop=(m == BLOCKS1 - 1))
                    last.then_inc(y_done, 1)

                def step(i, j):
                    if exists(i, j):
                        hidden(i, j)
                    if j % E == 4 and exists(i, j + 4):
                        turn_rows(i, j + 4)
                    for n, j0 in groups_due(j):
                        if exists(i, j0):
                            turn_group(i, j0, n)
                    if (j - down_at) % E == 0 and exists(i, j - down_at):
                        down(i, j - down_at)

                pe.wait_ge(loaded, SECOND_EXPERTS_LOADED)
                turn_rows(0, 0)
                turn.run(pe, step)

            @block.scalar
            def _(act):
                def copy_rows(i, j):
                    t, k = tile_of(i, j), j // E % 2
                    act.wait_ge(rows_turned, t + 1)
                    wait(act, h_done, E * (t - 1))
                    nc.scalar.copy(xT[:, k].rearrange("p c n -> p (c n)"), ps_x[:, 0:D]).then_inc(xT_ready, 1)

                def silu(i, j):
                    u = BODY2 * i + j
                    act.wait_ge(h_done, u + 1)
                    wait(act, hid_ready, u - 3)
                    nc.scalar.activation(act_g[:, j % 4, :], ps_h[j % 4][:, 0:HID1], ACT.Silu).then_inc(silu_ready, 1)

                def copy_group(i, j, n):
                    t, k = tile_of(i, j), j // E % 2
                    lo, hi = GROUP_BLOCKS[n]
                    act.wait_ge(turned, 3 * t + n + 1)
                    wait(act, y_done, t - 1)
                    nc.scalar.copy(hT[:, k, lo:hi, :], ps_t[(3 * (j // E) + n) % 2][:, 0:hi - lo, :]).then_inc(hT_ready, 1)

                def step(i, j):
                    if j % E == 4 and exists(i, j + 4):
                        copy_rows(i, j + 4)
                    if exists(i, j):
                        silu(i, j)
                    for n, j0 in groups_due(j):
                        if exists(i, j0):
                            copy_group(i, j0, n)

                copy_rows(0, 0)
                turn.run(act, step)

            @block.vector
            def _(dve):
                def stage_rows(i, j):
                    t = tile_of(i, j)
                    wait(dve, rows_turned, t - 1)
                    nc.vector.tensor_copy(rows[:, j // E % 2, :], xn_all[:, t, :]).then_inc(rows_ready, 1)

                def gated(i, j):
                    u, t, k, e = BODY2 * i + j, tile_of(i, j), j // E, j % E
                    dve.wait_ge(silu_ready, u + 1)
                    wait(dve, turned, 3 * (t - 1))
                    w = combine[:].rearrange("p t e -> p (t e)")
                    w = w[:, E * t + e:E * t + e + 1] if isinstance(t, int) else w[:, bass.ds(E * t + e, 1)]
                    nc.vector.scalar_tensor_tensor(hid[:, k, e * HID1:(e + 1) * HID1], act_g[:, j % 4, :], w,
                                                   ps_h[j % 4][:, HID1:2 * HID1], ALU.mult, ALU.mult).then_inc(hid_ready, 1)

                def update(i, j):
                    t = tile_of(i, j)
                    dve.wait_ge(y_done, t + 1)
                    nc.vector.tensor_tensor(x_all[:, t, :], x_all[:, t, :], ps_y[:, 0:D], ALU.add).then_inc(x_ready, 1)

                def step(i, j):
                    if exists(i, j):
                        gated(i, j)
                    if j % E == 2 and exists(i, j + 6):
                        stage_rows(i, j + 6)
                    if (j - down_at) % E == 0 and exists(i, j - down_at):
                        update(i, j - down_at)

                stage_rows(0, 0)
                turn.run(dve, step)


def second_experts(nc, x_all, mean_var, rstd, ident, gate_w_in, w_gu, w_d, loaded, out):
    with ExitStack() as ctx:
        s = Scope(nc, ctx)
        xn_all = s.sb("xn_all_e", [P, TILES, D])
        logits = s.sb("logits_e", [P, TILES, E])
        gate_w = s.sb("gate_w_e", [P, 2, E])
        combine = s.sb("combine", [P, TILES, E])
        gate_loaded = s.sem("gate_loaded_e")
        with nc.Block() as block:

            @block.sync
            def _(sp):
                sp.dma_start(gate_w[:], gate_w_in.rearrange("(k p) e -> p k e", p=P)).then_inc(gate_loaded, 16)

        logits_stage(nc, "e", x_all, mean_var, rstd, ident, gate_w, gate_loaded, xn_all, logits)
        second_routing(nc, logits, combine)
        second_ffn(nc, x_all, xn_all, ident, w_gu, w_d, loaded, combine, out)


def build(nc, a, out):
    SPENT.clear()
    table = nc.dram_tensor("expert_rows", [SLOTS, D], F32, kind="Internal").ap()
    results = nc.dram_tensor("expert_results", [SLOTS, D], F32, kind="Internal").ap()
    with ExitStack() as ctx:
        s = Scope(nc, ctx)
        x_all = s.sb("x_all", [P, TILES, D])
        ident = s.sb("ident", [P, P])
        mean_var = s.sb("mean_var", [P, TILES, 2])
        rstd = s.sb("rstd", [P, TILES])
        o_w = s.sb("o_w", [P, H1, D])
        x_loaded = s.sem("x_loaded")
        second_loaded = s.sem("second_attention_loaded")
        gather_at = s.sb("gather_at", [P, TILES], I32)
        gate = s.sb("gate_f", [P, TILES])
        q_w = s.sb("q_w", [P, 2, H1 * DH])
        kv_w = s.sb("kv_w", [P, 4, 2, GROUPS * DH])
        with ExitStack() as first:
            f = Scope(nc, first)
            w13 = f.sb("w13", [P, 2, E, 2 * HID0])
            w2 = f.sb("w2", [P, 3, E, D])
            first_loaded = f.sem("first_experts_loaded")
            table_zeroed = f.sem("table_zeroed")
            with ExitStack() as attention:
                t = Scope(nc, attention)
                score_w = t.sb("score_w", [P, H0 // 2, 2, P], F32R)
                out_w = t.sb("out_w", [P, H0 // 2, E0])
                bias0 = t.sb("bias0", [P, 1])
                zero = t.sb("zero", [P, D])
                zero_made = t.sem("zero_made")
                with nc.Block() as block:

                    @block.gpsimd
                    def _(pool):
                        nc.gpsimd.memset(zero[:], 0.0).then_inc(zero_made, 1)

                first_weights(nc, a["L0_xattn_W_q"], a["L0_xattn_W_kv"], a["L0_xattn_W_out"], a["L0_xattn_b_out"],
                              a["x"], x_all, x_loaded, ident, score_w, out_w, bias0)
                rows_rstd_stage(nc, x_all, x_loaded, mean_var, rstd, "a")

                def prefetch_experts(sp):
                    load_first_experts(sp, a["L0_ffn_W1"], a["L0_ffn_W3"], a["L0_ffn_W2"], w13, w2, first_loaded)
                    load_second_projections(sp, a["L1_xattn_wq"], a["L1_xattn_wk"], a["L1_xattn_wv"], a["L1_xattn_wk_ctx"],
                                            a["L1_xattn_wv_ctx"], q_w, kv_w, second_loaded)
                    sp.wait_ge(zero_made, 1)
                    for n in range(TILES):
                        sp.dma_start(table[n * P:(n + 1) * P, :], zero[:]).then_inc(table_zeroed, 16)
                    sp.wait_ge(table_zeroed, 16 * TILES)

                first_attention(nc, a["ctx_2048"], x_all, mean_var, rstd, ident, score_w, out_w, bias0, o_w,
                                prefetch_experts)
            rows_rstd_stage(nc, x_all, None, mean_var, rstd, "b")
            first_experts(nc, x_all, mean_var, rstd, ident, a["L0_ffn_Wg"],
                          (a["L0_ffn_sw1"], a["L0_ffn_sw3"], a["L0_ffn_sw2"]), w13, w2, first_loaded,
                          table, results, table_zeroed, gather_at, gate,
                          lambda sp: load_second_output(sp, a["L1_xattn_wo"], o_w, second_loaded))
        clear_spent(nc, (x_loaded, second_loaded))
        with ExitStack() as attention:
            t = Scope(nc, attention)
            tables = t.sb("rope_tables", [P, 3, 2, DH])
            mask = t.sb("mask", [P, 4, KEYS], mybir.dt.bfloat16)
            q_parts = [t.sb(f"q_{n}", [P, 2, H1 * DH], F32R) for n in ("high", "low")]
            kv_parts = [t.sb(f"kv_{n}", [P, 4, 2, GROUPS * DH], F32R) for n in ("high", "low")]
            between_layers(nc, x_all, mean_var, rstd, results, gather_at, gate, a["rope"], a["L1_xattn_q_norm_w"],
                           a["L1_xattn_k_norm_w"], tables, mask, q_w, kv_w, second_loaded, q_parts, kv_parts)
            second_attention(nc, a["ctx_2048"], x_all, mean_var, rstd, ident, q_parts, kv_parts,
                             q_w, kv_w, o_w, tables, mask)
        w_gu = s.sb("w_gu", [P, 2, E, 2 * HID1])
        w_d = s.sb("w_d", [P, BLOCKS1, D])
        experts_loaded = s.sem("second_experts_loaded")
        rows_rstd_stage(nc, x_all, None, mean_var, rstd, "d",
                        lambda sp: load_second_experts(sp, a["L1_ffn_w_gate"], a["L1_ffn_w_up"], a["L1_ffn_w_down"],
                                                       w_gu, w_d, experts_loaded))
        second_experts(nc, x_all, mean_var, rstd, ident, a["L1_ffn_gate_w"], w_gu, w_d, experts_loaded, out)


def rope_angles():
    half = np.arange(0, DH, 2, dtype=np.float64) / DH
    angle = np.outer(np.arange(S, dtype=np.float64), 1.0 / 10000.0 ** half)
    cos, sin = np.cos(angle), np.sin(angle)
    return np.stack([np.concatenate([cos, cos], -1), np.concatenate([-sin, sin], -1)]).astype(np.float32)


def kernel(**inputs):
    import concourse.bacc as bacc
    from concourse.bass_utils import run_bass_kernel_spmd

    nc = bacc.Bacc("TRN2", target_bir_lowering=False, num_devices=1)
    arrays = {name: np.ascontiguousarray(a) for name, a in inputs.items()}
    arrays["rope"] = rope_angles()
    args = {name: nc.dram_tensor(name, a.shape, mybir.dt.from_np(a.dtype), kind="ExternalInput").ap()
            for name, a in arrays.items()}
    out = nc.dram_tensor("out", (NB, S, D), F32, kind="ExternalOutput").ap()
    build(nc, args, out)
    r = run_bass_kernel_spmd(nc, [arrays], core_ids=[0])
    return r.results[0]["out"]
```

```python
from contextlib import ExitStack

import numpy as np
import concourse.bass as bass
from concourse import mybir

F32 = mybir.dt.float32
F32R = mybir.dt.float32r
I32 = mybir.dt.int32
ALU = mybir.AluOpType
ACT = mybir.ActivationFunctionType
AX = mybir.AxisListType

P = 128
NB = 32
S = 64
D = 256
TILES = NB * S // P
LN_EPS = 1e-5


class Scope:

    def __init__(self, nc, ctx, sems=None):
        self.nc, self.ctx, self.sems = nc, ctx, sems or ctx

    def sb(self, name, shape, dt=F32):
        return self.ctx.enter_context(self.nc.sbuf_tensor(name, shape, dt))

    def ps(self, name, shape, dt=F32):
        return self.ctx.enter_context(self.nc.psum_tensor(name, shape, dt))

    def sem(self, name):
        sem = self.sems.enter_context(self.nc.semaphore(name))
        SPENT.append(sem)
        return sem


SPENT = []


def clear_spent(pool, count, live):
    spent = SPENT[:count]
    SPENT[:count] = [sem for sem in spent if any(sem is other for other in live)]
    for sem in spent:
        if not any(sem is other for other in live):
            pool.sem_clear(sem)


def wait(eng, sem, value):
    if isinstance(value, int) and value <= 0:
        return
    eng.wait_ge(sem, value)


class Turns:

    def __init__(self, body, steps, lag, peeled=1):
        self.body, self.steps, self.lag, self.peeled = body, steps, lag, peeled

    def exists(self, i, j):
        return not isinstance(i, int) or 0 <= self.body * i + j < self.steps

    def at_most(self, value, limit):
        return min(value, limit) if isinstance(value, int) else value

    def run(self, eng, step):
        turns = self.steps // self.body
        for i in range(self.peeled):
            for j in range(self.body):
                step(i, j)
        with eng.Fori(self.peeled, turns - 1) as i:
            for j in range(self.body):
                step(i, j)
        for j in range(self.body):
            step(turns - 1, j)
        for j in range(self.lag):
            step(turns + j // self.body, j % self.body)


def tile_stats(stats, t):
    return stats[:, t, :] if isinstance(t, int) else stats[:, bass.ds(t, 1), :].rearrange("p a n -> p (a n)")


H0 = 8
E0 = 64


def first_weights(nc, W_q, W_kv, W_out, b_out, x, x_all, stats, ident, score_w, out_w, bias0, gates, gates_loaded, load_ahead):
    scale = float(E0) ** -0.5
    with ExitStack() as ctx:
        s = Scope(nc, ctx)
        w_in = s.sb("w_in", [E0, 3 * H0 * E0])
        wo_in = s.sb("wo_in", [P, H0 // 2, E0])
        wT = s.sb("wT", [P, 12, E0])
        a_w = s.sb("a_w", [P, H0 // 2, P])
        ps_t = s.ps("ps_t", [P, 16, E0])
        ps_a = s.ps("ps_a", [P, 2, 8, E0])
        ps_b = s.ps("ps_b", [P, 2, 8, E0])
        w_loaded = s.sem("w_loaded")
        x_loaded = [s.sem(f"x_loaded{c}") for c in range(4)]
        zeroed = s.sem("zeroed")
        ident_ready = s.sem("ident_ready")
        turned = s.sem("turned")
        wT_ready = s.sem("wT_ready")
        products = s.sem("products")
        stored = s.sem("stored")
        with nc.Block() as block:

            @block.sync
            def _(sp):
                sp.dma_start(w_in[:, 0:512], W_q).then_inc(w_loaded, 16)
                sp.dma_start(w_in[:, 512:1536], W_kv).then_inc(w_loaded, 16)
                sp.dma_start(wo_in[:], W_out.rearrange("(p k) n -> k p n", k=P)).then_inc(w_loaded, 16)
                for b in range(2):
                    sp.dma_start(bias0[b * S:(b + 1) * S, :],
                                 b_out.rearrange("(d o) -> d o", o=1)).then_inc(w_loaded, 16)
                xt = x.rearrange("(t b) d n -> (b d) t n", b=2)
                for c in range(4):
                    sp.dma_start(x_all[:, 4 * c:4 * c + 4, :], xt[:, 4 * c:4 * c + 4, :]).then_inc(x_loaded[c], 16)
                for gate_w, source in gates:
                    sp.dma_start(gate_w[:], source.rearrange("(k p) e -> p k e", p=P)).then_inc(gates_loaded, 16)
                load_ahead(sp)

            @block.gpsimd
            def _(pool):
                nc.gpsimd.memset(ident[:], 0.0).then_inc(zeroed, 1)
                pool.wait_ge(zeroed, 1)
                nc.gpsimd.affine_select(out=ident[:], in_=ident[:], compare_op=ALU.not_equal, fill=1.0,
                                        base=0, pattern=[[-1, P]], channel_multiplier=1).then_inc(ident_ready, 1)

            @block.tensor
            def _(pe):
                pe.wait_ge(w_loaded, 80)
                pe.wait_ge(ident_ready, 1)
                for c in range(12):
                    last = nc.tensor.transpose(ps_t[:, c, :], w_in[:, c * P:(c + 1) * P], ident[0:E0, 0:E0])
                last.then_inc(turned, 1)
                pe.wait_ge(wT_ready, 1)
                for h in range(H0):
                    r, pair = E0 * (h % 2), h // 2
                    for b in range(2):
                        nc.tensor.matmul(ps_a[b * E0:(b + 1) * E0, h % 2, pair, :], wT[r:r + E0, pair, :],
                                         wT[r:r + E0, 4 + pair, :], start=True, stop=True)
                for h in range(H0):
                    r, pair = E0 * (h % 2), h // 2
                    last = nc.tensor.matmul(ps_b[r:r + E0, h % 2, pair, :], wT[r:r + E0, 8 + pair, :],
                                            wo_in[r:r + E0, pair, :], start=True, stop=True)
                last.then_inc(products, 1)

            @block.vector
            def _(dve):
                def take_stats(c):
                    dve.wait_ge(x_loaded[c], 16)
                    for t in range(4 * c, 4 * c + 4):
                        nc.vector.bn_stats(stats[:, t, :], x_all[:, t, :])

                dve.wait_ge(turned, 1)
                nc.vector.tensor_copy(wT[:], ps_t[:, 0:12, :]).then_inc(wT_ready, 1)
                for c in range(2):
                    take_stats(c)
                dve.wait_ge(products, 1)
                for odd in range(2):
                    nc.vector.tensor_scalar(a_w[:, :, odd * E0:(odd + 1) * E0], ps_a[:, odd, 0:4, :], scale, None,
                                            ALU.mult).then_inc(stored, 1)
                dve.wait_ge(stored, 2)
                nc.vector.tensor_copy(score_w[:, :, 0, :], a_w[:]).then_inc(stored, 1)
                dve.wait_ge(stored, 3)
                nc.vector.tensor_tensor(score_w[:, :, 1, :], a_w[:], score_w[:, :, 0, :], ALU.subtract).then_inc(stored, 1)
                for odd in range(2):
                    r = slice(odd * E0, (odd + 1) * E0)
                    nc.vector.tensor_copy(out_w[r, :, :], ps_b[r, odd, 0:4, :]).then_inc(stored, 1)
                for c in range(2, 4):
                    take_stats(c)


def rows_rstd_stage(nc, stats, mean_var, rstd, label, loads=None):
    with ExitStack() as ctx:
        s = Scope(nc, ctx)
        std = s.sb(f"std_{label}", [P, TILES])
        var_done = s.sem(f"var_done_{label}")
        eps_done = s.sem(f"eps_done_{label}")
        sqrt_done = s.sem(f"sqrt_done_{label}")
        with nc.Block() as block:
            if loads is not None:
                block.sync(loads)

            @block.vector
            def _(dve):
                for t in range(TILES):
                    nc.vector.bn_aggr(mean_var[:, t, :], stats[:, t, :]).then_inc(var_done, 1)
                dve.wait_ge(var_done, TILES)
                nc.vector.tensor_scalar(std[:], mean_var[:, :, 1], LN_EPS, None, ALU.add).then_inc(eps_done, 1)
                dve.wait_ge(sqrt_done, 1)
                nc.vector.reciprocal(rstd[:], rstd[:])

            @block.scalar
            def _(act):
                act.wait_ge(eps_done, 1)
                nc.scalar.activation(rstd[:], std[:], ACT.Sqrt).then_inc(sqrt_done, 1)


UNITS = H0 // 2 * 2
BODY0 = 2 * UNITS
STEPS0 = TILES * UNITS
CTX_AT = 4


def load_context(eng, ctx_in, t, k, ctx_tile, ctx_twice, ctx_loaded):
    eng.dma_start(ctx_tile[:, k, :], ctx_in.rearrange("(t b) d n -> (b d) t n", b=2)[:, t, :]).then_inc(ctx_loaded[k], 16)
    for half in range(2):
        eng.dma_start(ctx_twice[half * S:(half + 1) * S, k],
                      ctx_in.rearrange("(t b) d n -> d t b n", b=2)[:, t]).then_inc(ctx_loaded[k], 16)


def first_attention(nc, ctx_in, ctx_tile, ctx_twice, ctx_loaded, x_all, stats, mean_var, rstd, ident, score_w, out_w, bias0, room, prefetch):
    with ExitStack() as ctx:
        s = Scope(nc, ctx)
        ctx_split = s.sb("ctx_split", [P, 2, 2, 2, D], F32R)
        one = s.sb("one", [P, 1])
        ctx_T = s.sb("ctx_T", [P, 2, 2, P])
        xn = s.sb("xn", [P, 2, D])
        x_split = s.sb("x_split", [P, 2, 2, D], F32R)
        q_split = s.sb("q_split", [P, 4, 2, D], F32R)
        neg_max = s.sb("neg_max", [P, 4, 4])
        den = s.sb("den", [P, 4, 4])
        rden = s.sb("rden", [P, 4, 4])
        probs = s.sb("probs", [P, 4, 4, D])
        probs_T = room[:, 0:8, :].rearrange("p (u r k) n -> p u r k n", u=2, r=2)
        heads = [room[:, 8:16, :].rearrange("p (b q) n -> p b q n", b=2), s.sb("heads", [P, 2, H0 // 2, D])]
        ps_s = s.ps("ps_s", [P, 2, 4, D])
        ps_pT = s.ps("ps_pT", [P, 2, 2, D])
        ps_q = s.ps("ps_q", [P, 2, D])
        ps_o = s.ps("ps_o", [P, D])

        one_made = s.sem("one_made")
        ctx_high = s.sem("ctx_high")
        ctx_parted = s.sem("ctx_parted")
        xn_ready = s.sem("xn_ready")
        x_high = s.sem("x_high")
        x_parted = s.sem("x_parted")
        q_done = s.sem("q_done")
        q_high_a = s.sem("q_high_by_act")
        q_high_d = s.sem("q_high_by_dve")
        q_ready = s.sem("q_ready")
        ctxT_done = s.sem("ctxT_done")
        ctxT_ready = s.sem("ctxT_ready")
        scores_done = s.sem("scores_done")
        max_ready = s.sem("max_ready")
        exp_ready = s.sem("exp_ready")
        rden_ready = s.sem("rden_ready")
        probs_ready = s.sem("probs_ready")
        turned = s.sem("probs_turned")
        turned_a = s.sem("turned_copied_by_act")
        turned_d = s.sem("turned_copied_by_dve")
        pv_done = s.sem("pv_done")
        heads_ready = s.sem("heads_ready")
        out_done = s.sem("out_done")
        x_updated = s.sem("x_updated")

        turn = Turns(BODY0, STEPS0, 7)
        exists = turn.exists

        def tile_of(i, j):
            return 2 * i + j // UNITS

        with nc.Block() as block:

            @block.sync
            def _(sp):
                prefetch(sp)
                with sp.Fori(1, TILES // 2) as i:
                    for k in range(2):
                        sp.wait_ge(scores_done, UNITS * (2 * i + k - 1))
                        load_context(sp, ctx_in, 2 * i + k, k, ctx_tile, ctx_twice, ctx_loaded)

            @block.gpsimd
            def _(pool):
                def part_context(i, j, b):
                    t, k = tile_of(i, j), j // UNITS % 2
                    pool.wait_ge(ctx_loaded[k], 48 * (i + j // BODY0 + 1))
                    wait(pool, scores_done, UNITS * (t - 1))
                    nc.gpsimd.tensor_tensor(ctx_split[:, k, b, 0, :], ctx_twice[:, k, b, :], one[:].to_broadcast([P, D]),
                                            ALU.mult).then_inc(ctx_high, 1)
                    pool.wait_ge(ctx_high, 2 * t + b + 1)
                    nc.gpsimd.tensor_tensor(ctx_split[:, k, b, 1, :], ctx_twice[:, k, b, :], ctx_split[:, k, b, 0, :],
                                            ALU.subtract).then_inc(ctx_parted, 1)

                def normalise(i, j):
                    pool.wait_ge(rden_ready, BODY0 * i + j + 1)
                    p3 = probs[:, j % 4]
                    nc.gpsimd.tensor_tensor(p3, p3, rden[:, j % 4, :].unsqueeze(2).to_broadcast([P, 4, D]),
                                            ALU.mult).then_inc(probs_ready, 1)

                def step(i, j):
                    if exists(i, j):
                        normalise(i, j)
                    b = j % UNITS - CTX_AT
                    if b in (0, 1) and exists(i, j - b + UNITS - CTX_AT):
                        part_context(i, j - b + UNITS - CTX_AT, b)

                nc.gpsimd.memset(one[:], 1.0).then_inc(one_made, 1)
                pool.wait_ge(one_made, 1)
                for b in range(2):
                    part_context(0, 0, b)
                turn.run(pool, step)

            @block.tensor
            def _(pe):
                def project(i, j):
                    t, g, k, b = tile_of(i, j), BODY0 * i + j, j // UNITS % 2, j % 2
                    pe.wait_ge(x_parted, 2 * t + b + 1)
                    wait(pe, q_ready, 2 * g)
                    if (j - 3) % UNITS == 7:
                        wait(pe, ctxT_ready, turn.at_most(tile_of(i, j - 3) + 2, TILES))
                    if (j - 9) % UNITS == UNITS - 1:
                        wait(pe, x_updated, tile_of(i, j - 9) + 1)
                    for part in range(2):
                        last = nc.tensor.matmul(ps_q[:, 0, :], score_w[:, j // 2 % 4, part, :], x_split[:, k, b, :],
                                                start=(part == 0), stop=(part == 1))
                    last.then_inc(q_done, 1)

                def turn_context(i, j):
                    t, k = tile_of(i, j), j // UNITS % 2
                    pe.wait_ge(ctx_loaded[k], 48 * (i + (j // BODY0) + 1))
                    wait(pe, q_ready, 2 * (BODY0 * i + j - UNITS + 3))
                    wait(pe, x_updated, t - 1)
                    for c in range(2):
                        last = nc.tensor.transpose(ps_q[:, 1, c * P:(c + 1) * P],
                                                   ctx_tile[:, k, c * P:(c + 1) * P], ident[:])
                    last.then_inc(ctxT_done, 1)

                def score(i, j):
                    g, k, b = BODY0 * i + j, j // UNITS, j % 2
                    pe.wait_ge(q_ready, 2 * (g + 1))
                    pe.wait_ge(ctx_parted, 2 * tile_of(i, j) + b + 1)
                    wait(pe, exp_ready, g - 1)
                    for r in range(2):
                        for qb in range(2):
                            for part in range(2):
                                last = nc.tensor.matmul(ps_s[:, j % 2, 2 * r + qb, :],
                                                        q_split[:, j % 4, r, qb * P:(qb + 1) * P],
                                                        ctx_split[:, k, b, part, :], start=(part == 0), stop=(part == 1))
                    last.then_inc(scores_done, 1)

                def turn_probs(i, j):
                    g = BODY0 * i + j
                    pe.wait_ge(probs_ready, g + 1)
                    wait(pe, turned_a, g)
                    wait(pe, turned_d, g)
                    for r in range(2):
                        for kb in range(2):
                            for qb in range(2):
                                last = nc.tensor.transpose(ps_pT[:, r, kb, qb * P:(qb + 1) * P],
                                                           probs[:, j % 4, 2 * r + qb, kb * P:(kb + 1) * P], ident[:])
                    last.then_inc(turned, 1)

                def values(i, j):
                    g, k, b = BODY0 * i + j, j // UNITS % 2, j % 2
                    pe.wait_ge(turned_a, g + 1)
                    pe.wait_ge(turned_d, g + 1)
                    pe.wait_ge(ctxT_ready, tile_of(i, j) + 1)
                    wait(pe, heads_ready, g)
                    for kb in range(2):
                        for r in range(2):
                            last = nc.tensor.matmul(ps_o[r * E0:(r + 1) * E0, :],
                                                    ctx_T[:, k, kb, b * E0:(b + 1) * E0],
                                                    probs_T[:, j % 2, r, kb, :], start=(kb == 0), stop=(kb == 1),
                                                    skip_group_check=True)
                    last.then_inc(pv_done, 1)

                def output(i, j):
                    t = tile_of(i, j)
                    pe.wait_ge(heads_ready, BODY0 * i + j + 1)
                    wait(pe, x_updated, t)
                    pe.wait_ge(q_ready, turn.at_most(2 * (BODY0 * i + j + 8), 2 * STEPS0))
                    for pr in range(4):
                        for b in range(2):
                            last = nc.tensor.matmul(ps_q[b * E0:(b + 1) * E0, 1, :], out_w[:, pr, :],
                                                    heads[j // UNITS % 2][:, b, pr, :], start=(pr == 0), stop=(pr == 3),
                                                    skip_group_check=True)
                    last.then_inc(out_done, 1)

                def step(i, j):
                    if exists(i, j):
                        score(i, j)
                    if exists(i, j - 3):
                        turn_probs(i, j - 3)
                    if exists(i, j - 4):
                        values(i, j - 4)
                    if (j - 5) % UNITS == UNITS - 1 and exists(i, j - 5):
                        output(i, j - 5)
                    if j % UNITS == 6 and exists(i, j + UNITS):
                        turn_context(i, j + UNITS)
                    if exists(i, j + 3):
                        project(i, j + 3)

                turn_context(0, 0)
                for j in range(3):
                    project(0, j)
                turn.run(pe, step)

            @block.scalar
            def _(act):
                def copy_context(i, j):
                    t = tile_of(i, j)
                    act.wait_ge(ctxT_done, t + 1)
                    act.wait_ge(q_done, 1 if isinstance(t, int) and t == 0 else BODY0 * i + j - UNITS + 3)
                    wait(act, pv_done, UNITS * (t - 1))
                    nc.scalar.copy(ctx_T[:, j // UNITS % 2].rearrange("p k c -> p (k c)"), ps_q[:, 1, :]).then_inc(ctxT_ready, 1)

                def keep_x_high(i, j):
                    t, k = tile_of(i, j), j // UNITS % 2
                    act.wait_ge(xn_ready, t + 1)
                    wait(act, q_done, UNITS * (t - 1))
                    for b in range(2):
                        r = slice(b * S, (b + 1) * S)
                        nc.scalar.copy(x_split[r, k, b, :], xn[r, k, :]).then_inc(x_high, 1)

                def keep_q_high(i, j):
                    g = BODY0 * i + j
                    act.wait_ge(q_done, g + 1)
                    wait(act, scores_done, g - 3)
                    nc.scalar.copy(q_split[0:E0, j % 4, 0, :], ps_q[0:E0, 0, :]).then_inc(q_high_a, 1)

                def exponents(i, j):
                    g = BODY0 * i + j
                    act.wait_ge(max_ready, g + 1)
                    wait(act, turned, g - 3)
                    for c in range(4):
                        last = nc.scalar.activation(probs[:, j % 4, c, :], ps_s[:, j % 2, c, :], ACT.Exp,
                                                    bias=neg_max[:, j % 4, c:c + 1], scale=1.0,
                                                    accum_out=den[:, j % 4, c:c + 1])
                    last.then_inc(exp_ready, 1)

                def copy_turned(i, j):
                    g = BODY0 * i + j
                    act.wait_ge(turned, g + 1)
                    wait(act, pv_done, g - 1)
                    nc.scalar.copy(probs_T[:, j % 2, 0], ps_pT[:, 0]).then_inc(turned_a, 1)

                def copy_heads(i, j):
                    t, b = tile_of(i, j), j % 2
                    act.wait_ge(pv_done, BODY0 * i + j + 1)
                    wait(act, out_done, t - 1)
                    nc.scalar.copy(heads[j // UNITS % 2][:, b, j // 2 % 4, :], ps_o[:]).then_inc(heads_ready, 1)

                def step(i, j):
                    if j % UNITS == 7 and exists(i, j + UNITS):
                        copy_context(i, j + UNITS)
                    if exists(i, j + 2):
                        keep_q_high(i, j + 2)
                    if exists(i, j - 1):
                        exponents(i, j - 1)
                    if exists(i, j - 3):
                        copy_turned(i, j - 3)
                    if exists(i, j - 4):
                        copy_heads(i, j - 4)
                    if j % UNITS == 1 and exists(i, j + UNITS):
                        keep_x_high(i, j + UNITS)

                keep_x_high(0, 0)
                copy_context(0, 0)
                for j in range(2):
                    keep_q_high(0, j)
                turn.run(act, step)

            @block.vector
            def _(dve):
                def normalise_rows(i, j):
                    t = tile_of(i, j)
                    wait(dve, x_parted, 2 * (t - 1))
                    nc.vector.tensor_scalar(xn[:, j // UNITS % 2, :], x_all[:, t, :], mean_var[:, t, 0:1],
                                            rstd[:, t:t + 1] if isinstance(t, int) else rstd[:, bass.ds(t, 1)],
                                            ALU.subtract, ALU.mult).then_inc(xn_ready, 1)

                def part_rows(i, j):
                    t, k = tile_of(i, j), j // UNITS % 2
                    dve.wait_ge(x_high, 2 * t + 2)
                    wait(dve, q_done, UNITS * (t - 1))
                    for b in range(2):
                        own, other = slice(b * S, (b + 1) * S), slice((1 - b) * S, (2 - b) * S)
                        nc.vector.tensor_tensor(x_split[other, k, b, :], xn[own, k, :], x_split[own, k, b, :],
                                                ALU.subtract).then_inc(x_parted, 1)

                def part_q(i, j):
                    g = BODY0 * i + j
                    dve.wait_ge(q_high_a, g + 1)
                    wait(dve, scores_done, g - 3)
                    nc.vector.tensor_copy(q_split[E0:P, j % 4, 1, :], ps_q[E0:P, 0, :]).then_inc(q_high_d, 1)
                    nc.vector.tensor_tensor(q_split[E0:P, j % 4, 0, :], ps_q[0:E0, 0, :], q_split[0:E0, j % 4, 0, :],
                                            ALU.subtract).then_inc(q_ready, 1)
                    dve.wait_ge(q_high_d, g + 1)
                    nc.vector.tensor_tensor(q_split[0:E0, j % 4, 1, :], ps_q[E0:P, 0, :], q_split[E0:P, j % 4, 1, :],
                                            ALU.subtract).then_inc(q_ready, 1)

                def maxima(i, j):
                    g = BODY0 * i + j
                    dve.wait_ge(scores_done, g + 1)
                    wait(dve, exp_ready, g - 3)
                    nc.vector.tensor_reduce(neg_max[:, j % 4, :], ps_s[:, j % 2], AX.X, ALU.max,
                                            negate=True).then_inc(max_ready, 1)

                def copy_turned(i, j):
                    g = BODY0 * i + j
                    dve.wait_ge(turned, g + 1)
                    wait(dve, pv_done, g - 1)
                    nc.vector.tensor_copy(probs_T[:, j % 2, 1], ps_pT[:, 1]).then_inc(turned_d, 1)

                def denominators(i, j):
                    g = BODY0 * i + j
                    dve.wait_ge(exp_ready, g + 1)
                    wait(dve, probs_ready, g - 3)
                    nc.vector.reciprocal(rden[:, j % 4, :], den[:, j % 4, :]).then_inc(rden_ready, 1)

                def update(i, j):
                    t = tile_of(i, j)
                    dve.wait_ge(out_done, t + 1)
                    dve.wait_ge(q_high_a, turn.at_most(BODY0 * i + j + 9, STEPS0))
                    nc.vector.scalar_tensor_tensor(x_all[:, t, :], ps_q[:, 1, :], bias0[:, 0:1], x_all[:, t, :],
                                                   ALU.add, ALU.add).then_inc(x_updated, 1)

                def take_stats(i, j):
                    t = tile_of(i, j)
                    dve.wait_ge(x_updated, t + 1)
                    nc.vector.bn_stats(tile_stats(stats, t), x_all[:, t, :])

                def step(i, j):
                    if (j - 6) % UNITS == UNITS - 1 and exists(i, j - 6):
                        update(i, j - 6)
                    if exists(i, j + 2):
                        part_q(i, j + 2)
                    if (j - 7) % UNITS == UNITS - 1 and exists(i, j - 7):
                        take_stats(i, j - 7)
                    if exists(i, j):
                        maxima(i, j)
                    if exists(i, j - 1):
                        denominators(i, j - 1)
                    if exists(i, j - 3):
                        copy_turned(i, j - 3)
                    if j % UNITS == 0 and exists(i, j + UNITS):
                        normalise_rows(i, j + UNITS)
                    if j % UNITS == 2 and exists(i, j + UNITS):
                        part_rows(i, j + UNITS)

                normalise_rows(0, 0)
                part_rows(0, 0)
                for j in range(2):
                    part_q(0, j)
                turn.run(dve, step)
E = 8
HID0 = 352
CHUNKS0 = [(0, 128), (128, 128), (256, 96)]
CAP = NB * S // E
SLOTS = E * CAP
FAR = 2 * SLOTS


def load_first_experts(eng, W1, W3, W2, w13, w2, loaded):
    for k in range(2):
        rows = slice(k * P, (k + 1) * P)
        for h, w in enumerate((W1, W3)):
            eng.dma_start(w13[:, k, :, h * HID0:(h + 1) * HID0],
                          w[:, rows, :].rearrange("e p h -> p e h")).then_inc(loaded, 16)
    for c, (r0, n) in enumerate(CHUNKS0):
        eng.dma_start(w2[0:n, c, :, :], W2[:, r0:r0 + n, :].rearrange("e p d -> p e d")).then_inc(loaded, 16)


FIRST_EXPERTS_LOADED = 16 * 7


def load_shared_expert(eng, sw1, sw3, sw2, s13, s2, loaded):
    for k in range(2):
        for h, w in enumerate((sw1, sw3)):
            eng.dma_start(s13[:, k, h * HID0:(h + 1) * HID0], w[k * P:(k + 1) * P, :]).then_inc(loaded, 16)
    for c, (r0, n) in enumerate(CHUNKS0):
        eng.dma_start(s2[0:n, c, :], sw2[r0:r0 + n, :]).then_inc(loaded, 16)


SHARED_EXPERT_LOADED = 16 * 7


def logits_stage(nc, label, x_all, mean_var, rstd, ident, gate_w, gates_loaded, logits, xn_all=None, loads=None):
    with ExitStack() as ctx:
        s = Scope(nc, ctx)
        rows = s.sb(f"rows_{label}", [P, 2, D])
        xT = s.sb(f"xT_{label}", [P, 2, D])
        ps_x = s.ps(f"ps_x_{label}", [P, 2, 512])
        ps_l = s.ps(f"ps_l_{label}", [P, 512])
        rows_ready = s.sem(f"rows_ready_{label}")
        kept = s.sem(f"kept_{label}")
        turned = s.sem(f"rows_turned_{label}")
        xT_ready = s.sem(f"xT_ready_{label}")
        logits_done = s.sem(f"logits_done_{label}")
        logits_kept = s.sem(f"logits_kept_{label}")
        turn = Turns(2, TILES, 1, 2)
        exists = turn.exists
        with nc.Block() as block:
            if loads is not None:
                block.sync(loads)

            @block.vector
            def _(dve):
                def step(i, j):
                    if exists(i, j):
                        t = 2 * i + j
                        wait(dve, turned, t - 1)
                        nc.vector.tensor_scalar(rows[:, j, :], x_all[:, t, :], mean_var[:, t, 0:1],
                                                column(rstd, t), ALU.subtract, ALU.mult).then_inc(rows_ready, 1)
                        if xn_all is not None:
                            dve.wait_ge(rows_ready, t + 1)
                            nc.vector.tensor_copy(xn_all[:, t, :], rows[:, j, :]).then_inc(kept, 1)

                turn.run(dve, step)
                dve.wait_ge(logits_done, TILES)
                nc.vector.tensor_copy(logits[:].rearrange("p t e -> p (t e)"), ps_l[:, 0:TILES * E]).then_inc(logits_kept, 1)

            @block.tensor
            def _(pe):
                if gates_loaded is not None:
                    pe.wait_ge(gates_loaded, 32)

                def step(i, j):
                    if exists(i, j):
                        t = 2 * i + j
                        pe.wait_ge(rows_ready, t + 1)
                        wait(pe, xT_ready, t - 1)
                        for k in range(2):
                            last = nc.tensor.transpose(ps_x[:, j, k * P:(k + 1) * P], rows[:, j, k * P:(k + 1) * P], ident[:])
                        last.then_inc(turned, 1)
                    if exists(i, j - 1):
                        t, m = 2 * i + j - 1, (j - 1) % 2
                        pe.wait_ge(xT_ready, t + 1)
                        for k in range(2):
                            last = nc.tensor.matmul(ps_l[:, E * t:E * t + E] if isinstance(t, int) else ps_l[:, bass.ds(E * t, E)],
                                                    xT[:, m, k * P:(k + 1) * P], gate_w[:, k, :],
                                                    start=(k == 0), stop=(k == 1))
                        last.then_inc(logits_done, 1)

                turn.run(pe, step)

            @block.scalar
            def _(act):
                def step(i, j):
                    if exists(i, j):
                        t = 2 * i + j
                        act.wait_ge(turned, t + 1)
                        wait(act, logits_done, t - 1)
                        nc.scalar.copy(xT[:, j, :], ps_x[:, j, 0:D]).then_inc(xT_ready, 1)

                turn.run(act, step)


def column(a, t):
    return a[:, t:t + 1] if isinstance(t, int) else a[:, bass.ds(t, 1)]


class Chain:

    def __init__(self, eng, sem):
        self.eng, self.sem, self.n = eng, sem, 0

    def __call__(self, instruction):
        self.n += 1
        instruction.then_inc(self.sem, 1)
        self.eng.wait_ge(self.sem, self.n)


def pick_first(link, nc, from_eight, values, best, ranked, rank, one_hot):
    wide = lambda a: a.unsqueeze(2).to_broadcast([P, TILES, E])
    per_expert = from_eight[:].unsqueeze(1).to_broadcast([P, TILES, E])
    link(nc.vector.tensor_reduce(best[:], values[:], AX.X, ALU.max))
    link(nc.vector.tensor_tensor(ranked[:], values[:], wide(best[:]), ALU.is_equal))
    link(nc.vector.tensor_tensor(ranked[:], ranked[:], per_expert, ALU.mult))
    link(nc.vector.tensor_reduce(rank[:], ranked[:], AX.X, ALU.min))
    link(nc.vector.tensor_tensor(one_hot[:], per_expert, wide(rank[:]), ALU.is_equal))


def first_routing(nc, logits, scatter_at, gather_at, gate, whole, parts, whole_loaded):
    with ExitStack() as ctx:
        s = Scope(nc, ctx)
        BF = mybir.dt.bfloat16
        wide = lambda a: a.unsqueeze(2).to_broadcast([P, TILES, E])
        from_eight = s.sb("r_from_eight", [P, E])
        best = s.sb("r_best", [P, TILES])
        ranked = s.sb("r_ranked", [P, TILES, E])
        rank = s.sb("r_rank", [P, TILES])
        one_hot = s.sb("r_one_hot", [P, TILES, E])
        one_hot_b = s.sb("r_one_hot_b", [P, TILES, E], BF)
        shifted = s.sb("r_shifted", [P, TILES, E])
        total = s.sb("r_total", [P, TILES])
        pos = s.sb("r_pos", [P, TILES])
        keep = s.sb("r_keep", [P, TILES])
        slot = s.sb("r_slot", [P, TILES])
        far = s.sb("r_far", [P, TILES])
        idx = s.sb("r_idx", [P, 2, TILES])
        ones = s.sb("r_ones", [P, P], BF)
        upto = s.sb("r_upto", [P, P], BF)
        ps_c = s.ps("r_ps_c", [P, 512])
        made = s.sem("r_made")
        consts = s.sem("r_consts")
        chain = s.sem("r_chain")
        hot_ready = s.sem("r_hot_ready")
        shift_ready = s.sem("r_shift_ready")
        exp_done = s.sem("r_exp_done")
        counted = s.sem("r_counted")
        high_made = s.sem("r_shared_high")
        low_made = s.sem("r_shared_low")
        tail = CHUNKS0[2][1]
        (s13, s2), high, rest = whole, *parts
        pieces = [(s13[:], high[0][:], rest[0][:]), (s2[:, 0:2], high[1][:, 0:2], rest[1][:, 0:2]),
                  (s2[0:tail, 2], high[1][0:tail, 2], rest[1][0:tail, 2])]
        with nc.Block() as block:

            @block.gpsimd
            def _(pool):
                nc.gpsimd.iota(from_eight[:], [[1, E]], base=-E, channel_multiplier=0,
                               allow_small_or_imprecise_dtypes=True).then_inc(consts, 1)
                nc.gpsimd.iota(far[:], [[P, TILES]], base=FAR, channel_multiplier=1,
                               allow_small_or_imprecise_dtypes=True).then_inc(consts, 1)
                nc.gpsimd.memset(ones[:], 1.0).then_inc(made, 1)
                pool.wait_ge(made, 1)
                nc.gpsimd.affine_select(out=upto[:], in_=ones[:], compare_op=ALU.is_ge, fill=0.0, base=0,
                                        pattern=[[1, P]], channel_multiplier=-1).then_inc(consts, 1)
                for n, (w, h, r) in enumerate(pieces):
                    pool.wait_ge(high_made, n + 1)
                    nc.gpsimd.tensor_tensor(r, w, h, ALU.subtract).then_inc(low_made, 1)

            @block.vector
            def _(dve):
                link = Chain(dve, chain)
                dve.wait_ge(consts, 3)
                pick_first(link, nc, from_eight, logits, best, ranked, rank, one_hot)
                nc.vector.tensor_copy(one_hot_b[:], one_hot[:]).then_inc(hot_ready, 1)
                nc.vector.tensor_tensor(shifted[:], logits[:], wide(best[:]), ALU.subtract).then_inc(shift_ready, 1)
                dve.wait_ge(exp_done, 1)
                link(nc.vector.tensor_reduce(total[:], shifted[:], AX.X, ALU.add))
                link(nc.vector.reciprocal(gate[:], total[:]))
                dve.wait_ge(counted, 1)
                link(nc.vector.tensor_tensor(ranked[:], one_hot[:], ps_c[:, 0:TILES * E].rearrange("p (t e) -> p t e", e=E),
                                             ALU.mult))
                link(nc.vector.tensor_reduce(pos[:], ranked[:], AX.X, ALU.add))
                link(nc.vector.tensor_scalar(keep[:], pos[:], float(CAP), None, ALU.is_le))
                link(nc.vector.tensor_tensor(gate[:], gate[:], keep[:], ALU.mult))
                link(nc.vector.tensor_scalar(slot[:], rank[:], float(CAP), float(E * CAP - 1), ALU.mult, ALU.add))
                link(nc.vector.tensor_tensor(slot[:], slot[:], pos[:], ALU.add))
                link(nc.vector.tensor_tensor(idx[:, 0, :], slot[:], far[:], ALU.subtract))
                link(nc.vector.tensor_tensor(idx[:, 0, :], idx[:, 0, :], keep[:], ALU.mult))
                link(nc.vector.tensor_tensor(idx[:, 0, :], idx[:, 0, :], far[:], ALU.add))
                link(nc.vector.tensor_scalar(idx[:, 1, :], slot[:], float(-(SLOTS - 1)), None, ALU.add))
                link(nc.vector.tensor_tensor(idx[:, 1, :], idx[:, 1, :], keep[:], ALU.mult))
                link(nc.vector.tensor_scalar(idx[:, 1, :], idx[:, 1, :], float(SLOTS - 1), None, ALU.add))
                link(nc.vector.tensor_copy(scatter_at[:], idx[:, 0, :]))
                link(nc.vector.tensor_copy(gather_at[:], idx[:, 1, :]))

            @block.scalar
            def _(act):
                act.wait_ge(whole_loaded, SHARED_EXPERT_LOADED)
                for w, h, _ in pieces:
                    nc.scalar.copy(h, w).then_inc(high_made, 1)
                act.wait_ge(shift_ready, 1)
                nc.scalar.activation(shifted[:], shifted[:], ACT.Exp).then_inc(exp_done, 1)

            @block.tensor
            def _(pe):
                pe.wait_ge(hot_ready, 1)
                pe.wait_ge(consts, 3)
                hot = one_hot_b[:].rearrange("p t e -> p (t e)")
                last = nc.tensor.matmul(ps_c[:, 0:TILES * E], upto[:], hot, start=True, stop=False)
                for back in range(1, TILES):
                    last = nc.tensor.matmul(ps_c[:, back * E:TILES * E], ones[:], hot[:, 0:(TILES - back) * E],
                                            start=False, stop=(back == TILES - 1))
                last.then_inc(counted, 1)


def first_ffn(nc, label, ident, weights, weights_loaded=None, x_all=None, mean_var=None, rstd=None, table=None,
              results=None, loads=None, extra_pool=None, sems=None):
    split = table is None
    passes = ((0, 0), (0, 1), (1, 0)) if split else ((0, 0),)
    parts = ("high", "low") if split else ("whole",)
    dt = F32R if split else F32
    w13_of, w2_of = weights
    with ExitStack() as ctx:
        s = Scope(nc, ctx, sems)
        rows = s.sb(f"rows_{label}", [P, 2, D])
        xT = [s.sb(f"xT_{part}_{label}", [P, 2, D], dt) for part in parts]
        hid = s.sb(f"hid_{label}", [P, 2, HID0])
        hT = [s.sb(f"hT_{part}_{label}", [P, 2, 3, P], dt) for part in parts]
        y = s.sb(f"y_{label}", [P, 2, D])
        ps_x = s.ps(f"ps_x_{label}", [P, 512])
        ps_h = s.ps(f"ps_h_{label}", [P, 2, 2, 512])
        ps_hT = s.ps(f"ps_hT_{label}", [P, 512])
        ps_y = s.ps(f"ps_y_{label}", [P, 512])
        rows_ready = [s.sem(f"rows_ready{k}_{label}") for k in range(2)]
        rows_turned = s.sem(f"rows_turned_{label}")
        xT_ready = s.sem(f"xT_ready_{label}")
        xT_high = s.sem(f"xT_high_{label}") if split else None
        hT_high = s.sem(f"hT_high_{label}") if split else None
        h_done = s.sem(f"h_done_{label}")
        silu_ready = s.sem(f"silu_ready_{label}")
        hid_ready = s.sem(f"hid_ready_{label}")
        hid_turned = s.sem(f"hid_turned_{label}")
        hT_ready = s.sem(f"hT_ready_{label}")
        y_done = s.sem(f"y_done_{label}")
        y_used = s.sem(f"y_used_{label}")
        stored = [s.sem(f"stored{k}_{label}") for k in range(2)]
        each = 16 if table is not None else 1
        turn = Turns(2, TILES, 4, 2)
        exists = turn.exists
        with nc.Block() as block:
            block.gpsimd(extra_pool)

            @block.sync
            def _(sp):
                if table is None:
                    loads(sp)
                    return

                def step(i, j):
                    if exists(i, j):
                        n = 2 * i + j
                        wait(sp, rows_turned, n - 1)
                        sp.dma_start(rows[:, j, :], table[n]).then_inc(rows_ready[j], 16)
                    if exists(i, j - 3):
                        n = 2 * i + j - 3
                        sp.wait_ge(y_used, n + 1)
                        sp.dma_start(results[n], y[:, (j - 3) % 2, :]).then_inc(stored[(j - 3) % 2], 16)

                for j in range(2):
                    step(0, j)
                for i in range(1, TILES // 2 + 2):
                    for j in range(2):
                        step(i, j)
                for k in range(2):
                    sp.wait_ge(stored[k], 16 * TILES // 2)

            @block.tensor
            def _(pe):
                def turn_rows(i, j):
                    n = 2 * i + j
                    pe.wait_ge(rows_ready[j % 2], each * (i + 1))
                    wait(pe, xT_ready, n)
                    for k in range(2):
                        last = nc.tensor.transpose(ps_x[:, k * P:(k + 1) * P], rows[:, j % 2, k * P:(k + 1) * P], ident[:])
                    last.then_inc(rows_turned, 1)

                def hidden(i, j):
                    n, m = 2 * i + j, j % 2
                    pe.wait_ge(xT_ready, n + 1)
                    wait(pe, hid_ready, n - 1)
                    products = [(k, *p) for k in range(2) for p in passes]
                    for h in range(2):
                        for q, (k, r, w) in enumerate(products):
                            last = nc.tensor.matmul(ps_h[:, m, h, 0:HID0], xT[r][:, m, k * P:(k + 1) * P],
                                                    w13_of(i + j // 2, k, w)[:, h * HID0:(h + 1) * HID0],
                                                    start=(q == 0), stop=(q == len(products) - 1))
                    last.then_inc(h_done, 1)

                def turn_hidden(i, j):
                    n, m = 2 * i + j, j % 2
                    pe.wait_ge(hid_ready, n + 1)
                    wait(pe, hT_ready, n)
                    for c, (r0, w) in enumerate(CHUNKS0):
                        last = nc.tensor.transpose(ps_hT[0:w, c * P:(c + 1) * P], hid[:, m, r0:r0 + w], ident[:])
                    last.then_inc(hid_turned, 1)

                def down(i, j):
                    n, m = 2 * i + j, j % 2
                    pe.wait_ge(hT_ready, n + 1)
                    wait(pe, y_used, n)
                    products = [(c, *p) for c in range(3) for p in passes]
                    for q, (c, r, w) in enumerate(products):
                        n_rows = CHUNKS0[c][1]
                        last = nc.tensor.matmul(ps_y[:, 0:D], hT[r][0:n_rows, m, c, :], w2_of(i + j // 2, c, w)[0:n_rows, :],
                                                start=(q == 0), stop=(q == len(products) - 1))
                    last.then_inc(y_done, 1)

                def step(i, j):
                    if exists(i, j):
                        turn_rows(i, j)
                    if exists(i, j - 2):
                        turn_hidden(i, j - 2)
                    if exists(i, j - 1):
                        hidden(i, j - 1)
                    if exists(i, j - 2):
                        down(i, j - 2)

                if weights_loaded is not None:
                    pe.wait_ge(*weights_loaded)
                turn.run(pe, step)

            @block.scalar
            def _(act):
                def step(i, j):
                    if exists(i, j):
                        n = 2 * i + j
                        act.wait_ge(rows_turned, n + 1)
                        wait(act, h_done, n - 1)
                        nc.scalar.copy(xT[0][:, j, :], ps_x[:, 0:D]).then_inc(xT_high if split else xT_ready, 1)
                    if exists(i, j - 2):
                        n = 2 * i + j - 2
                        act.wait_ge(hid_turned, n + 1)
                        wait(act, y_done, n - 1)
                        w = CHUNKS0[2][1]
                        nc.scalar.copy(hT[0][0:w, j, 2, :], ps_hT[0:w, 2 * P:3 * P])
                        nc.scalar.copy(hT[0][:, j, 0:2, :], ps_hT[:, 0:2 * P].rearrange("p (c n) -> p c n", c=2)
                                       ).then_inc(hT_high if split else hT_ready, 1)
                    if exists(i, j - 1):
                        n = 2 * i + j - 1
                        act.wait_ge(h_done, n + 1)
                        wait(act, hid_turned, n - 1)
                        nc.scalar.activation(hid[:, (j - 1) % 2, :], ps_h[:, (j - 1) % 2, 0, 0:HID0],
                                             ACT.Silu).then_inc(silu_ready, 1)

                turn.run(act, step)

            @block.vector
            def _(dve):
                def stage_rows(i, j):
                    n = 2 * i + j
                    wait(dve, rows_turned, n - 1)
                    nc.vector.tensor_scalar(rows[:, j % 2, :], x_all[:, n, :], mean_var[:, n, 0:1], column(rstd, n),
                                            ALU.subtract, ALU.mult).then_inc(rows_ready[j % 2], 1)

                def part_rows(i, j):
                    dve.wait_ge(xT_high, 2 * i + j + 1)
                    nc.vector.tensor_tensor(xT[1][:, j % 2, :], ps_x[:, 0:D], xT[0][:, j % 2, :],
                                            ALU.subtract).then_inc(xT_ready, 1)

                def part_hidden(i, j):
                    w, m = CHUNKS0[2][1], j % 2
                    dve.wait_ge(hT_high, 2 * i + j + 1)
                    nc.vector.tensor_tensor(hT[1][0:w, m, 2, :], ps_hT[0:w, 2 * P:3 * P], hT[0][0:w, m, 2, :], ALU.subtract)
                    nc.vector.tensor_tensor(hT[1][:, m, 0:2, :], ps_hT[:, 0:2 * P].rearrange("p (c n) -> p c n", c=2),
                                            hT[0][:, m, 0:2, :], ALU.subtract).then_inc(hT_ready, 1)

                def step(i, j):
                    if split and exists(i, j):
                        part_rows(i, j)
                    if split and exists(i, j - 2):
                        part_hidden(i, j - 2)
                    if split and exists(i, j + 1):
                        stage_rows(i, j + 1)
                    if exists(i, j - 1):
                        n, m = 2 * i + j - 1, (j - 1) % 2
                        dve.wait_ge(silu_ready, n + 1)
                        nc.vector.tensor_tensor(hid[:, m, :], hid[:, m, :], ps_h[:, m, 1, 0:HID0], ALU.mult).then_inc(hid_ready, 1)
                    if exists(i, j - 2):
                        n = 2 * i + j - 2
                        dve.wait_ge(y_done, n + 1)
                        if table is None:
                            nc.vector.tensor_tensor(x_all[:, n, :], x_all[:, n, :], ps_y[:, 0:D], ALU.add).then_inc(y_used, 1)
                        else:
                            wait(dve, stored[j], 16 * (i - 1))
                            nc.vector.tensor_copy(y[:, j, :], ps_y[:, 0:D]).then_inc(y_used, 1)

                if split:
                    stage_rows(0, 0)
                turn.run(dve, step)


def first_experts(nc, x_all, mean_var, rstd, ident, gate_w, gates_loaded, shared_weights, w13, w2, loaded, q_w, kv_w,
                  load_projections, table, results, table_zeroed,
                  gather_at, gate, sems, prefetch, live):
    with ExitStack() as ctx:
        s = Scope(nc, ctx, sems)
        xn_all = q_w[:].rearrange("p k n -> p (k n)").rearrange("p (t n) -> p t n", t=TILES)
        room = kv_w[:].rearrange("p w k n -> p (w k n)")
        s13 = room[:, 0:4 * HID0].rearrange("p (k n) -> p k n", k=2)
        s2 = room[:, 4 * HID0:4 * HID0 + 3 * D].rearrange("p (c n) -> p c n", c=3)
        shared_parts = [(s.sb(f"s13_{part}", [P, 2, 2 * HID0], F32R), s.sb(f"s2_{part}", [P, 3, D], F32R))
                        for part in ("high", "low")]
        logits = s.sb("logits_f", [P, TILES, E])
        scatter_at = s.sb("scatter_at", [P, TILES], I32)
        shared_loaded = s.sem("shared_loaded")
        scattered = s.sem("scattered")

        def loads(sp):
            load_shared_expert(sp, *shared_weights, s13, s2, shared_loaded)
            prefetch(sp)

        logits_stage(nc, "f", x_all, mean_var, rstd, ident, gate_w, gates_loaded, logits, xn_all, loads)
        first_routing(nc, logits, scatter_at, gather_at, gate, (s13, s2), shared_parts, shared_loaded)

        def scatter(pool):
            pool.wait_ge(table_zeroed, 16 * TILES)
            for t in range(TILES):
                nc.gpsimd.indirect_dma_start(out=table, out_offset=bass.IndirectOffsetOnAxis(ap=scatter_at[:, t:t + 1], axis=0),
                                             in_=xn_all[:, t, :], in_offset=None,
                                             bounds_check=SLOTS - 1, oob_is_err=False).then_inc(scattered, 16)
            pool.wait_ge(scattered, 16 * TILES)

        def load_next(sp):
            sp.wait_ge(scattered, 16 * TILES)
            load_projections(sp)

        first_ffn(nc, "shared", ident,
                  (lambda e, k, w: shared_parts[w][0][:, k, :], lambda e, c, w: shared_parts[w][1][:, c, :]),
                  x_all=x_all, mean_var=mean_var, rstd=rstd, loads=load_next, extra_pool=scatter, sems=sems)
        before = len(SPENT)
        first_ffn(nc, "experts", ident, (lambda e, k, _: w13[:, k, e, :], lambda e, c, _: w2[:, c, e, :]),
                  (loaded, FIRST_EXPERTS_LOADED), table=table.rearrange("(n p) d -> n p d", p=P),
                  results=results.rearrange("(n p) d -> n p d", p=P),
                  extra_pool=lambda pool: clear_spent(pool, before, (loaded, *live)), sems=sems)
H1 = 16
GROUPS = 4
DH = 128
HG = H1 // GROUPS
KEYS = 2 * S
BODY1 = 2 * GROUPS
STEPS1 = TILES * GROUPS
RMS_EPS = 1e-6
MASKED = -1e30


def load_second_projections(eng, wq, wk, wv, wk_ctx, wv_ctx, q_w, kv_w, loaded):
    eng.dma_start(q_w[:], wq.rearrange("(k p) n -> p k n", p=P)).then_inc(loaded, 16)
    for n, w in enumerate((wk_ctx, wk, wv_ctx, wv)):
        eng.dma_start(kv_w[:, n], w.rearrange("(k p) n -> p k n", p=P)).then_inc(loaded, 16)


def load_second_output(eng, wo, o_w, loaded):
    for n in range(2):
        eng.dma_start(o_w[:, 8 * n:8 * n + 8], wo[n * 1024:(n + 1) * 1024].rearrange("(h p) n -> p h n", p=P)).then_inc(loaded, 16)


SECOND_ATTENTION_LOADED = 16 * 7


def between_layers(nc, x_all, stats, mean_var, rstd, results, gather_at, gate, rope, q_norm, k_norm, tables, mask,
                   q_w, kv_w, loaded, q_parts, kv_parts, load_ahead, live):
    before = len(SPENT)
    with ExitStack() as ctx:
        s = Scope(nc, ctx)
        results_got = s.sb("results_got", [P, TILES, D])
        std = s.sb("std_c", [P, TILES])
        angle = s.sb("rope_angle", [P, 2, DH])
        w = s.sb("rope_w", [P, 2, DH])
        gathered = [s.sem(f"gathered{t}") for t in range(TILES)]
        added = s.sem("experts_added")
        stats_done = s.sem("stats_done_c")
        var_done = s.sem("var_done_c")
        eps_done = s.sem("eps_done_c")
        sqrt_done = s.sem("sqrt_done_c")
        angle_loaded = s.sem("angle_loaded")
        zeros = s.sem("mask_zero")
        steps = s.sem("rope_steps")
        masked = s.sem("mask_made")
        high_made = s.sem("weights_high")
        low_made = s.sem("weights_low")
        pieces = [[a[:, 1024 * n:1024 * (n + 1)] for a in group]
                  for group in ([a[:].rearrange("p k n -> p (k n)") for a in (q_w, *q_parts)],
                                [a[:].rearrange("p w k n -> p (w k n)") for a in (kv_w, *kv_parts)])
                  for n in range(4)]
        POOL_PIECES = (7,)

        def low(eng, n):
            whole, high, rest = pieces[n]
            eng.wait_ge(high_made, n + 1)
            eng.tensor_tensor(rest, whole, high, ALU.subtract).then_inc(low_made, 1)

        with nc.Block() as block:

            @block.sync
            def _(sp):
                for b in range(2):
                    sp.dma_start(angle[b * S:(b + 1) * S], rope.rearrange("c s d -> s c d")).then_inc(angle_loaded, 16)
                for n, v in enumerate((q_norm, k_norm)):
                    sp.dma_start(w[:, n, :], v.rearrange("(o d) -> o d", o=1).to_broadcast([P, DH])).then_inc(angle_loaded, 16)
                load_ahead(sp)

            @block.gpsimd
            def _(pool):
                nc.gpsimd.memset(mask[:], 0.0).then_inc(zeros, 1)
                pool.wait_ge(zeros, 1)
                for h in range(2):
                    own = mask[h * S:(h + 1) * S]
                    nc.gpsimd.affine_select(out=own, in_=own, compare_op=ALU.is_ge, fill=MASKED, base=0,
                                            pattern=[[0, 4], [-1, S]], channel_multiplier=1).then_inc(masked, 1)
                pool.wait_ge(masked, 2)
                for t in range(TILES):
                    nc.gpsimd.indirect_dma_start(out=results_got[:, t, :], out_offset=None, in_=results,
                                                 in_offset=bass.IndirectOffsetOnAxis(ap=gather_at[:, t:t + 1], axis=0),
                                                 bounds_check=SLOTS - 1, oob_is_err=False).then_inc(gathered[t], 16)
                for t in range(TILES):
                    pool.wait_ge(gathered[t], 16)
                for n in POOL_PIECES:
                    low(pool, n)
                clear_spent(pool, before, live)

            @block.scalar
            def _(act):
                act.wait_ge(loaded, SECOND_ATTENTION_LOADED)
                for whole, high, _ in pieces:
                    nc.scalar.copy(high, whole).then_inc(high_made, 1)
                act.wait_ge(eps_done, 1)
                nc.scalar.activation(rstd[:], std[:], ACT.Sqrt).then_inc(sqrt_done, 1)

            @block.vector
            def _(dve):
                for n in range(2):
                    low(dve, n)
                dve.wait_ge(angle_loaded, 64)
                half = DH // 2
                link = Chain(dve, steps)
                link(nc.vector.tensor_scalar(w[:, 0, :], w[:, 0, :], float(DH) ** -0.5, None, ALU.mult))
                for n, row in ((0, 0), (1, 2)):
                    nc.vector.tensor_tensor(tables[:, row, 0, :], w[:, n, :], angle[:, 0, :], ALU.mult)
                    for a in range(2):
                        o = 1 - a
                        nc.vector.tensor_tensor(tables[:, row, 1, a * half:(a + 1) * half], w[:, n, o * half:(o + 1) * half],
                                                angle[:, 1, a * half:(a + 1) * half], ALU.mult)
                nc.vector.tensor_copy(tables[:, 1, 0, :], w[:, 1, :])
                nc.vector.memset(tables[:, 1, 1, :], 0.0)
                for n in range(2, 8):
                    if n not in POOL_PIECES:
                        low(dve, n)
                for t in range(TILES):
                    dve.wait_ge(gathered[t], 16)
                    nc.vector.scalar_tensor_tensor(x_all[:, t, :], results_got[:, t, :], gate[:, t:t + 1], x_all[:, t, :],
                                                   ALU.mult, ALU.add).then_inc(added, 1)
                    if t > 0:
                        dve.wait_ge(added, t)
                        nc.vector.bn_stats(stats[:, t - 1, :], x_all[:, t - 1, :]).then_inc(stats_done, 1)
                dve.wait_ge(added, TILES)
                nc.vector.bn_stats(stats[:, TILES - 1, :], x_all[:, TILES - 1, :]).then_inc(stats_done, 1)
                for t in range(TILES):
                    dve.wait_ge(stats_done, t + 1)
                    nc.vector.bn_aggr(mean_var[:, t, :], stats[:, t, :]).then_inc(var_done, 1)
                dve.wait_ge(var_done, TILES)
                nc.vector.tensor_scalar(std[:], mean_var[:, :, 1], LN_EPS, None, ALU.add).then_inc(eps_done, 1)
                dve.wait_ge(sqrt_done, 1)
                nc.vector.reciprocal(rstd[:], rstd[:])


def second_attention(nc, ctx_in, rows, ctx_loaded, x_all, stats, mean_var, rstd, ident, q_parts, kv_parts, q_w, kv_w, o_w, tables, mask):
    with ExitStack() as ctx:
        s = Scope(nc, ctx)
        BF = mybir.dt.bfloat16
        ident_b = s.sb("ident_b", [P, P], BF)
        eps = s.sb("rms_eps", [P, 1])
        rowsT = [s.sb(f"a_rowsT_{n}", [P, 2, 2, 2, P], F32R) for n in ("high", "low")]
        square = s.sb("a_square", [P, 2, 512])
        mean_sq = s.sb("a_mean_sq", [P, 4, 4])
        log_sq = s.sb("a_log_sq", [P, 4, 4])
        inv_rms = s.sb("a_inv_rms", [P, 4, 4])
        turned_cos = s.sb("a_cos", [P, 2, HG, DH])
        turned_sin = s.sb("a_sin", [P, 2, HG, DH])
        qT = q_w[:].rearrange("p k n -> p (k n)").rearrange("p (t g b h s) -> p t g b h s", t=2, g=GROUPS, b=2, h=HG)
        kT = kv_w[:, 0:2].rearrange("p w k n -> p (w k n)").rearrange("p (t b g n) -> p t b g n", t=2, b=2, g=GROUPS)
        v = kv_w[:, 2:4]
        neg_max = s.sb("a_neg_max", [P, 2, 4])
        den = s.sb("a_den", [P, 2, 4])
        rden = s.sb("a_rden", [P, 2, 4])
        probs = s.sb("a_probs", [P, 2, 4, KEYS])
        probs_T = s.sb("a_probs_T", [P, 2, 4, P])
        heads = s.sb("a_heads", [P, 2, HG, 2, S])
        ps_p = [s.ps(f"a_ps_p{n}", [P, 512]) for n in range(2)]
        ps_r = s.ps("a_ps_r", [P, 512])
        ps_s = s.ps("a_ps_s", [P, 4, KEYS])
        ps_pT = s.ps("a_ps_pT", [P, 4, P])
        ps_o = s.ps("a_ps_o", [P, 2, HG, S])
        ps_y = s.ps("a_ps_y", [P, 512])
        ps_x = s.ps("a_ps_x", [P, 512])

        ident_cast = s.sem("ident_cast")
        xn_ready = s.sem("a_xn_ready")
        rows_turned = s.sem("a_rows_turned")
        rows_high = s.sem("a_rows_high")
        rowsT_ready = s.sem("a_rowsT_ready")
        projected = [s.sem(f"a_projected{n}") for n in range(2)]
        v_kept = [s.sem(f"a_v_kept{n}") for n in range(2)]
        squared = [s.sem(f"a_squared{n}") for n in range(2)]
        summed = [s.sem(f"a_summed{n}") for n in range(2)]
        log_done = s.sem("a_log_done")
        inv_ready = [s.sem(f"a_inv_ready{n}") for n in range(2)]
        rotated = [s.sem(f"a_rotated{n}") for n in range(2)]
        summed_up = s.sem("a_summed_up")
        roped = [s.sem(f"a_roped{n}") for n in range(2)]
        rope_turned = [s.sem(f"a_rope_turned{n}") for n in range(2)]
        rope_kept = [s.sem(f"a_rope_kept{n}") for n in range(2)]
        scores_done = s.sem("a_scores_done")
        max_ready = s.sem("a_max_ready")
        exp_ready = s.sem("a_exp_ready")
        rden_ready = s.sem("a_rden_ready")
        probs_ready = s.sem("a_probs_ready")
        probs_turned = s.sem("a_probs_turned")
        probsT_ready = s.sem("a_probsT_ready")
        pv_done = s.sem("a_pv_done")
        heads_ready = s.sem("a_heads_ready")
        out_done = s.sem("a_out_done")
        x_updated = s.sem("a_x_updated")

        turn = Turns(BODY1, STEPS1, GROUPS + 3)
        exists = turn.exists
        src_tile = ctx_in.rearrange("(t b) d n -> (b d) t n", b=2)

        def is_v(j):
            return j % GROUPS == 1

        def rope_steps(i, j):
            return 3 * (2 * i + j // GROUPS) + (0, 1, 1, 2)[j % GROUPS]

        with nc.Block() as block:

            @block.sync
            def _(sp):
                with sp.Fori(1, TILES // 2) as i:
                    for k in range(2):
                        sp.wait_ge(rows_turned, 2 * i + k - 1)
                        sp.dma_start(rows[:, k, 1, :], src_tile[:, 2 * i + k, :]).then_inc(ctx_loaded[k], 16)

            @block.gpsimd
            def _(pool):
                nc.gpsimd.memset(eps[:], RMS_EPS)
                nc.gpsimd.tensor_copy(ident_b[:], ident[:]).then_inc(ident_cast, 1)

                def rope(i, j, n):
                    r = rope_steps(i, j)
                    pool.wait_ge(rotated[n], r + 1)
                    nc.gpsimd.tensor_tensor(turned_cos[:, n], turned_cos[:, n], turned_sin[:, n], ALU.add).then_inc(summed_up, 1)
                    pool.wait_ge(summed_up, 2 * r + n + 1)
                    pool.wait_ge(inv_ready[n], r + 1)
                    nc.gpsimd.tensor_tensor(turned_cos[:, n], turned_cos[:, n],
                                            inv_rms[:, 2 * (j % 2) + n, :].unsqueeze(2).to_broadcast([P, HG, DH]),
                                            ALU.mult).then_inc(roped[n], 1)

                def normalise(i, j):
                    u, m = BODY1 * i + j, j % 2
                    pool.wait_ge(rden_ready, u + 1)
                    nc.gpsimd.tensor_tensor(probs[:, m], probs[:, m], rden[:, m, :].unsqueeze(2).to_broadcast([P, 4, KEYS]),
                                            ALU.mult).then_inc(probs_ready, 1)

                def step(i, j):
                    if exists(i, j - 4):
                        normalise(i, j - 4)
                    if exists(i, j) and not is_v(j):
                        for n in range(2):
                            rope(i, j, n)

                turn.run(pool, step)

            @block.tensor
            def _(pe):
                def turn_rows(i, j):
                    t, k = 2 * i + j // GROUPS, j // GROUPS % 2
                    pe.wait_ge(xn_ready, t + 1)
                    pe.wait_ge(ctx_loaded[k], 16 * (i + j // BODY1 + 1))
                    wait(pe, rowsT_ready, t)
                    for a in range(2):
                        for c in range(2):
                            last = nc.tensor.transpose(ps_x[:, (2 * a + c) * P:(2 * a + c + 1) * P],
                                                       rows[:, k, a, c * P:(c + 1) * P], ident[:])
                    last.then_inc(rows_turned, 1)

                def project(i, j, n):
                    t, k = 2 * i + j // GROUPS, j // GROUPS
                    if n == 0:
                        pe.wait_ge(rowsT_ready, t + 1)
                    wait(pe, v_kept[n], 2 * (2 * i + (j + 2) // GROUPS))
                    wait(pe, rotated[n], rope_steps(i, j))
                    if j % GROUPS < 2:
                        source, weights = 1 - n, [w[:, 2 * (j % GROUPS) + n] for w in kv_parts]
                    else:
                        g = 2 * (j % GROUPS - 2) + n
                        source, weights = 0, [w[:, :, g * 512:(g + 1) * 512] for w in q_parts]
                    products = [(c, *parts) for c in range(2) for parts in ((0, 0), (0, 1), (1, 0))]
                    for m, (c, r, w) in enumerate(products):
                        last = nc.tensor.matmul(ps_p[n][:], rowsT[r][:, k, source, c, :], weights[w][:, c, :],
                                                start=(m == 0), stop=(m == 5))
                    last.then_inc(projected[n], 1)

                def turn_rope(i, j, n):
                    r = rope_steps(i, j)
                    pe.wait_ge(roped[n], r + 1)
                    wait(pe, rope_kept[1 - n], r + n)
                    for h in range(HG):
                        last = nc.tensor.transpose(ps_r[:, h * P:(h + 1) * P], turned_cos[:, n, h, :], ident[:])
                    last.then_inc(rope_turned[n], 1)

                def score(i, j):
                    u, k, g = BODY1 * i + j, j // GROUPS % 2, j % GROUPS
                    pe.wait_ge(rope_kept[g % 2], 3 * (2 * i + j // GROUPS) + 2 + g // 2)
                    for n in range(2):
                        pe.wait_ge(rope_kept[n], 3 * (2 * i + j // GROUPS) + 1)
                    wait(pe, exp_ready, u)
                    for b in range(2):
                        for m in range(2):
                            nc.tensor.matmul(ps_s[:, 2 * b + m, :],
                                             qT[:, k, g, b, 2 * m:2 * m + 2, :].rearrange("p h s -> p (h s)"),
                                             kT[:, k, b, g, :], start=(b == 0 and m == 0), stop=False,
                                             skip_group_check=True)
                    last = nc.tensor.matmul(ps_s[:, :, S:KEYS], ident_b[:], mask[:], start=False, stop=True,
                                            skip_group_check=True)
                    last.then_inc(scores_done, 1)

                def turn_probs(i, j):
                    u, m = BODY1 * i + j, j % 2
                    pe.wait_ge(probs_ready, u + 1)
                    wait(pe, probsT_ready, u)
                    for a in range(4):
                        last = nc.tensor.transpose(ps_pT[:, a, :], probs[:, m, a, :], ident[:])
                    last.then_inc(probs_turned, 1)

                def values(i, j):
                    u, k, g = BODY1 * i + j, j // GROUPS % 2, j % GROUPS
                    pe.wait_ge(probsT_ready, u + 1)
                    for n in range(2):
                        pe.wait_ge(v_kept[n], 2 * (2 * i + j // GROUPS + 1))
                    wait(pe, heads_ready, u)
                    for b in range(2):
                        last = nc.tensor.matmul(ps_o[:, b].rearrange("p h s -> p (h s)"), v[:, k, b, g * DH:(g + 1) * DH],
                                                probs_T[:, j % 2, 2 * b:2 * b + 2, :].rearrange("p a n -> p (a n)"),
                                                start=True, stop=True)
                    last.then_inc(pv_done, 1)

                def output(i, j):
                    u, g = BODY1 * i + j, j % GROUPS
                    pe.wait_ge(heads_ready, u + 1)
                    if g == 0:
                        wait(pe, x_updated, 2 * i + j // GROUPS)
                    for h in range(HG):
                        last = nc.tensor.matmul(ps_y[:, 0:D], heads[:, j % 2, h].rearrange("p b s -> p (b s)"),
                                                o_w[:, HG * g + h, :], start=(g == 0 and h == 0),
                                                stop=(g == GROUPS - 1 and h == HG - 1))
                    last.then_inc(out_done, 1)

                def step(i, j):
                    if exists(i, j - 4):
                        score(i, j - 4)
                    if exists(i, j - 5):
                        turn_probs(i, j - 5)
                    if exists(i, j):
                        project(i, j, 0)
                    if exists(i, j - 5):
                        values(i, j - 5)
                    if exists(i, j - 1) and not is_v(j - 1):
                        turn_rope(i, j - 1, 0)
                    if j % GROUPS == 3 and exists(i, j + 1):
                        turn_rows(i, j + 1)
                    if exists(i, j):
                        project(i, j, 1)
                    if exists(i, j - 5):
                        output(i, j - 5)
                    if exists(i, j - 1) and not is_v(j - 1):
                        turn_rope(i, j - 1, 1)

                pe.wait_ge(ident_cast, 1)
                turn_rows(0, 0)
                turn.run(pe, step)

            @block.scalar
            def _(act):
                def copy_rows(i, j):
                    t, k = 2 * i + j // GROUPS, j // GROUPS % 2
                    act.wait_ge(rows_turned, t + 1)
                    wait(act, projected[1], GROUPS * (t - 1))
                    nc.scalar.copy(rowsT[0][:, k].rearrange("p a c n -> p (a c n)"), ps_x[:]).then_inc(rows_high, 1)

                def keep_values(i, j, n):
                    u, k = BODY1 * i + j, j // GROUPS
                    act.wait_ge(projected[n], u + 1)
                    wait(act, pv_done, u - 1 - GROUPS)
                    for b in range(2):
                        nc.scalar.copy(v[n * S:(n + 1) * S, k, b, :], ps_p[n][b * S:(b + 1) * S, :]).then_inc(v_kept[n], 1)

                def squares(i, j, n):
                    r = rope_steps(i, j)
                    act.wait_ge(projected[n], BODY1 * i + j + 1)
                    wait(act, summed[n], r)
                    nc.scalar.activation(square[:, n, :], ps_p[n][:], ACT.Square).then_inc(squared[n], 1)

                def inverse(i, j, n):
                    r, c = rope_steps(i, j), 2 * (j % 2) + n
                    act.wait_ge(summed[n], r + 1)
                    nc.scalar.activation(log_sq[:, c, :], mean_sq[:, c, :], ACT.Ln, bias=eps[:, 0:1],
                                         scale=1.0 / DH).then_inc(log_done, 1)
                    act.wait_ge(log_done, 2 * r + n + 1)
                    wait(act, roped[n], r - 1)
                    nc.scalar.activation(inv_rms[:, c, :], log_sq[:, c, :], ACT.Exp, scale=-0.5).then_inc(inv_ready[n], 1)

                def keep_rope(i, j, n):
                    k, r = j // GROUPS % 2, rope_steps(i, j)
                    act.wait_ge(rope_turned[n], r + 1)
                    if j % GROUPS == 0:
                        nc.scalar.copy(kT[:, k, :, :, n * S:(n + 1) * S],
                                       ps_r[:].rearrange("p (g b s) -> p b g s", g=GROUPS, b=2)).then_inc(rope_kept[n], 1)
                    else:
                        g = 2 * (j % GROUPS - 2) + n
                        nc.scalar.copy(qT[:, k, g].rearrange("p b h s -> p h b s"),
                                       ps_r[:].rearrange("p (h b s) -> p h b s", h=HG, b=2)).then_inc(rope_kept[n], 1)

                def exponents(i, j):
                    u, m = BODY1 * i + j, j % 2
                    act.wait_ge(max_ready, u + 1)
                    wait(act, probs_turned, u - 1)
                    for a in range(4):
                        last = nc.scalar.activation(probs[:, m, a, :], ps_s[:, a, :], ACT.Exp, bias=neg_max[:, m, a:a + 1],
                                                    scale=1.0, accum_out=den[:, m, a:a + 1])
                    last.then_inc(exp_ready, 1)

                def keep_heads(i, j):
                    u, m = BODY1 * i + j, j % 2
                    act.wait_ge(pv_done, u + 1)
                    wait(act, out_done, u - 1)
                    nc.scalar.copy(heads[:, m].rearrange("p h b s -> p b h s"), ps_o[:]).then_inc(heads_ready, 1)

                def step(i, j):
                    if exists(i, j - 4):
                        exponents(i, j - 4)
                    rope = exists(i, j) and not is_v(j)
                    if rope:
                        squares(i, j, 0)
                    elif exists(i, j):
                        keep_values(i, j, 0)
                    if exists(i, j - 5):
                        keep_heads(i, j - 5)
                    if exists(i, j - 1) and not is_v(j - 1):
                        keep_rope(i, j - 1, 0)
                    if rope:
                        inverse(i, j, 0)
                    if j % GROUPS == 3 and exists(i, j + 1):
                        copy_rows(i, j + 1)
                    if rope:
                        squares(i, j, 1)
                    elif exists(i, j):
                        keep_values(i, j, 1)
                    if exists(i, j - 1) and not is_v(j - 1):
                        keep_rope(i, j - 1, 1)
                    if rope:
                        inverse(i, j, 1)

                nc.scalar.preload_act_table_set("natural_log_exp_and_others")
                act.wait_ge(ident_cast, 1)
                copy_rows(0, 0)
                turn.run(act, step)

            @block.vector
            def _(dve):
                def normalise_rows(i, j):
                    t, k = 2 * i + j // GROUPS, j // GROUPS % 2
                    wait(dve, rows_turned, t - 1)
                    nc.vector.tensor_scalar(rows[:, k, 0, :], x_all[:, t, :], mean_var[:, t, 0:1], column(rstd, t),
                                            ALU.subtract, ALU.mult).then_inc(xn_ready, 1)

                def part_rows(i, j):
                    t, k = 2 * i + j // GROUPS, j // GROUPS % 2
                    dve.wait_ge(rows_high, t + 1)
                    nc.vector.tensor_tensor(rowsT[1][:, k].rearrange("p a c n -> p (a c n)"), ps_x[:],
                                            rowsT[0][:, k].rearrange("p a c n -> p (a c n)"), ALU.subtract).then_inc(rowsT_ready, 1)

                def rotate(i, j, n):
                    r, c = rope_steps(i, j), 2 * (j % 2) + n
                    row = 1 + n if j % GROUPS == 0 else 0
                    half = DH // 2
                    dve.wait_ge(squared[n], r + 1)
                    nc.vector.tensor_reduce(mean_sq[:, c, :], square[:, n, :].rearrange("p (h d) -> p h d", h=HG),
                                            AX.X, ALU.add).then_inc(summed[n], 1)
                    wait(dve, rope_turned[n], r)
                    job = ps_p[n][:].rearrange("p (h d) -> p h d", h=HG)

                    def table(which, lo, hi):
                        return tables[:, row, which, lo:hi].unsqueeze(1).to_broadcast([P, HG, hi - lo])

                    nc.vector.tensor_tensor(turned_cos[:, n], job, table(0, 0, DH), ALU.mult)
                    nc.vector.tensor_tensor(turned_sin[:, n, :, 0:half], job[:, :, half:DH], table(1, 0, half), ALU.mult)
                    nc.vector.tensor_tensor(turned_sin[:, n, :, half:DH], job[:, :, 0:half], table(1, half, DH),
                                            ALU.mult).then_inc(rotated[n], 1)

                def maxima(i, j):
                    u, m = BODY1 * i + j, j % 2
                    dve.wait_ge(scores_done, u + 1)
                    wait(dve, exp_ready, u - 1)
                    nc.vector.tensor_reduce(neg_max[:, m, :], ps_s[:], AX.X, ALU.max, negate=True).then_inc(max_ready, 1)

                def denominators(i, j):
                    u, m = BODY1 * i + j, j % 2
                    dve.wait_ge(exp_ready, u + 1)
                    wait(dve, probs_ready, u - 1)
                    nc.vector.reciprocal(rden[:, m, :], den[:, m, :]).then_inc(rden_ready, 1)

                def copy_probs(i, j):
                    u, m = BODY1 * i + j, j % 2
                    dve.wait_ge(probs_turned, u + 1)
                    wait(dve, pv_done, u - 1)
                    nc.vector.tensor_copy(probs_T[:, m], ps_pT[:]).then_inc(probsT_ready, 1)

                def update(i, j):
                    t = 2 * i + j // GROUPS
                    dve.wait_ge(out_done, BODY1 * i + j + 1)
                    nc.vector.tensor_tensor(x_all[:, t, :], x_all[:, t, :], ps_y[:, 0:D], ALU.add).then_inc(x_updated, 1)

                def take_stats(i, j):
                    t = 2 * i + j // GROUPS
                    dve.wait_ge(x_updated, t + 1)
                    nc.vector.bn_stats(tile_stats(stats, t), x_all[:, t, :])

                def step(i, j):
                    if exists(i, j - 4):
                        maxima(i, j - 4)
                    if exists(i, j - 5):
                        copy_probs(i, j - 5)
                    if exists(i, j - 4):
                        denominators(i, j - 4)
                    if exists(i, j) and not is_v(j):
                        rotate(i, j, 0)
                    if j % GROUPS == 2 and exists(i, j + 2):
                        normalise_rows(i, j + 2)
                    if j % GROUPS == 3 and exists(i, j + 1):
                        part_rows(i, j + 1)
                    if exists(i, j) and not is_v(j):
                        rotate(i, j, 1)
                    if (j - 5) % GROUPS == GROUPS - 1 and exists(i, j - 5):
                        update(i, j - 5)
                    if (j - 6) % GROUPS == GROUPS - 1 and exists(i, j - 6):
                        take_stats(i, j - 6)

                normalise_rows(0, 0)
                part_rows(0, 0)
                turn.run(dve, step)
HID1 = 176
BLOCKS1 = E * HID1 // P
GROUP_BLOCKS = [(0, 4), (4, 8), (8, 11)]
GROUP_LAST = [-(-hi * P // HID1) - 1 for _, hi in GROUP_BLOCKS]
BODY2 = 2 * E


def load_second_experts(eng, w_gate, w_up, w_down, w_gu, w_d, gu_loaded, d_loaded):
    for k in range(2):
        for h, w in enumerate((w_gate, w_up)):
            eng.dma_start(w_gu[k][:, :, h * HID1:(h + 1) * HID1],
                          w[:, k * P:(k + 1) * P, :].rearrange("e p f -> p e f")).then_inc(gu_loaded, 16)
    eng.dma_start(w_d, w_down.rearrange("e f d -> (e f) d").rearrange("(c p) d -> p c d", p=P)).then_inc(d_loaded, 16)


def gate_up_low(pool, experts, w_gu, gu_parts, high_made, low_made):
    for e in experts:
        pool.wait_ge(high_made, 2 * (e + 1))
        for k in range(2):
            pool.tensor_tensor(gu_parts[1][:, k, e, :], w_gu[k][:, e, :], gu_parts[0][:, k, e, :],
                               ALU.subtract).then_inc(low_made, 1)


def second_routing(nc, logits, combine, w_gu, gu_parts, gu_loaded, high_made, low_made):
    with ExitStack() as ctx:
        s = Scope(nc, ctx)
        from_eight = s.sb("t_from_eight", [P, E])
        best = [s.sb(f"t_best{n}", [P, TILES]) for n in range(2)]
        hot = [s.sb(f"t_hot{n}", [P, TILES, E]) for n in range(2)]
        ranked = s.sb("t_ranked", [P, TILES, E])
        rank = s.sb("t_rank", [P, TILES])
        rest = s.sb("t_rest", [P, TILES, E])
        ratio = s.sb("t_ratio", [P, TILES])
        total = s.sb("t_total", [P, TILES])
        weight = [s.sb(f"t_weight{n}", [P, TILES]) for n in range(2)]
        consts = s.sem("t_consts")
        chain = s.sem("t_chain")
        diff_ready = s.sem("t_diff_ready")
        exp_done = s.sem("t_exp_done")
        wide = lambda a: a.unsqueeze(2).to_broadcast([P, TILES, E])
        with nc.Block() as block:

            @block.gpsimd
            def _(pool):
                nc.gpsimd.iota(from_eight[:], [[1, E]], base=-E, channel_multiplier=0,
                               allow_small_or_imprecise_dtypes=True).then_inc(consts, 1)
                gate_up_low(nc.gpsimd, range(E // 2), w_gu, gu_parts, high_made, low_made)

            @block.vector
            def _(dve):
                link = Chain(dve, chain)
                dve.wait_ge(consts, 1)
                pick_first(link, nc, from_eight, logits, best[0], ranked, rank, hot[0])
                link(nc.vector.tensor_scalar(ranked[:], hot[0][:], -3e38, None, ALU.mult))
                link(nc.vector.tensor_tensor(rest[:], logits[:], ranked[:], ALU.add))
                pick_first(link, nc, from_eight, rest, best[1], ranked, rank, hot[1])
                nc.vector.tensor_tensor(ratio[:], best[1][:], best[0][:], ALU.subtract).then_inc(diff_ready, 1)
                dve.wait_ge(exp_done, 1)
                link(nc.vector.tensor_scalar(total[:], ratio[:], 1.0, None, ALU.add))
                link(nc.vector.reciprocal(weight[0][:], total[:]))
                link(nc.vector.tensor_tensor(weight[1][:], weight[0][:], ratio[:], ALU.mult))
                link(nc.vector.tensor_tensor(hot[0][:], hot[0][:], wide(weight[0][:]), ALU.mult))
                link(nc.vector.tensor_tensor(hot[1][:], hot[1][:], wide(weight[1][:]), ALU.mult))
                link(nc.vector.tensor_tensor(combine[:], hot[0][:], hot[1][:], ALU.add))

            @block.scalar
            def _(act):
                act.wait_ge(gu_loaded, 64)

                def high(experts):
                    for e in experts:
                        for k in range(2):
                            nc.scalar.copy(gu_parts[0][:, k, e, :], w_gu[k][:, e, :]).then_inc(high_made, 1)

                high(range(E // 2))
                act.wait_ge(diff_ready, 1)
                nc.scalar.activation(ratio[:], ratio[:], ACT.Exp).then_inc(exp_done, 1)
                high(range(E // 2, E))


def second_ffn(nc, x_all, mean_var, rstd, ident, w_gu, gu_parts, high_made, low_made, w_d, d_loaded, combine, out):
    with ExitStack() as ctx:
        s = Scope(nc, ctx)
        rows = s.sb("e_rows", [P, 2, D])
        xT = [s.sb(f"e_xT_{n}", [P, 2, 2, P], F32R) for n in ("high", "low")]
        act_g = s.sb("e_act_g", [P, 4, HID1])
        hid = s.sb("e_hid", [P, 2, E * HID1])
        hT = [s.sb(f"e_hT_{n}", [P, 2, BLOCKS1, P], F32R) for n in ("high", "low")]
        d_parts = [s.sb(f"e_w_d_{n}", [P, BLOCKS1, D], F32R) for n in ("high", "low")]
        ps_h = [s.ps(f"e_ps_h{n}", [P, 512]) for n in range(4)]
        ps_t = [s.ps(f"e_ps_t{n}", [P, 4, P]) for n in range(2)]
        ps_x = s.ps("e_ps_x", [P, 512])
        ps_y = s.ps("e_ps_y", [P, 512])
        rows_ready = s.sem("e_rows_ready")
        rows_turned = s.sem("e_rows_turned")
        xT_high = s.sem("e_xT_high")
        xT_ready = s.sem("e_xT_ready")
        h_done = s.sem("e_h_done")
        silu_ready = s.sem("e_silu_ready")
        hid_ready = s.sem("e_hid_ready")
        turned = s.sem("e_turned")
        hT_high = s.sem("e_hT_high")
        hT_ready = s.sem("e_hT_ready")
        d_high = s.sem("e_down_high")
        d_low = s.sem("e_down_low")
        y_done = s.sem("e_y_done")
        x_ready = s.sem("e_x_ready")
        stored = s.sem("e_stored")
        turn = Turns(BODY2, TILES * E, E + 4)
        exists = turn.exists
        out_tile = out.rearrange("(t b) d n -> (b d) t n", b=2)
        turn_at = [last + 2 for last in GROUP_LAST]
        down_at = turn_at[2] + 2

        def tile_of(i, j):
            return 2 * i + j // E

        def groups_due(j):
            return [(n, j - at) for n, at in enumerate(turn_at) if (j - at) % E == 0]

        with nc.Block() as block:

            @block.sync
            def _(sp):
                for t in range(TILES):
                    sp.wait_ge(x_ready, t + 1)
                    sp.dma_start(out_tile[:, t, :], x_all[:, t, :]).then_inc(stored, 16)
                sp.wait_ge(stored, 16 * TILES)

            @block.gpsimd
            def _(pool):
                gate_up_low(nc.gpsimd, range(E // 2, E), w_gu, gu_parts, high_made, low_made)
                for n, (lo, hi) in enumerate(GROUP_BLOCKS):
                    pool.wait_ge(d_high, n + 1)
                    nc.gpsimd.tensor_tensor(d_parts[1][:, lo:hi, :], w_d[:, lo:hi, :], d_parts[0][:, lo:hi, :],
                                            ALU.subtract).then_inc(d_low, 1)

            @block.tensor
            def _(pe):
                def turn_rows(i, j):
                    t, k = tile_of(i, j), j // E % 2
                    pe.wait_ge(rows_ready, t + 1)
                    wait(pe, xT_ready, t)
                    for c in range(2):
                        last = nc.tensor.transpose(ps_x[:, c * P:(c + 1) * P], rows[:, k, c * P:(c + 1) * P], ident[:])
                    last.then_inc(rows_turned, 1)

                def hidden(i, j):
                    u, k = BODY2 * i + j, j // E
                    pe.wait_ge(xT_ready, tile_of(i, j) + 1)
                    wait(pe, hid_ready, u - 3)
                    if isinstance(i, int) and u < E:
                        pe.wait_ge(low_made, 2 * (u + 1))
                    products = [(c, *parts) for c in range(2) for parts in ((0, 0), (0, 1), (1, 0))]
                    for m, (c, r, w) in enumerate(products):
                        last = nc.tensor.matmul(ps_h[j % 4][:, 0:2 * HID1], xT[r][:, k, c, :], gu_parts[w][:, c, j % E, :],
                                                start=(m == 0), stop=(m == 5))
                    last.then_inc(h_done, 1)

                def turn_group(i, j, n):
                    t, k = tile_of(i, j), j // E % 2
                    c = 3 * t + n
                    b = (3 * (j // E) + n) % 2
                    lo, hi = GROUP_BLOCKS[n]
                    pe.wait_ge(hid_ready, BODY2 * i + j + GROUP_LAST[n] + 1)
                    wait(pe, hT_ready, c - 1)
                    for m in range(lo, hi):
                        last = nc.tensor.transpose(ps_t[b][:, m - lo, :], hid[:, k, m * P:(m + 1) * P], ident[:])
                    last.then_inc(turned, 1)

                def down(i, j):
                    t, k = tile_of(i, j), j // E % 2
                    pe.wait_ge(hT_ready, 3 * t + 3)
                    wait(pe, x_ready, t)
                    if isinstance(t, int) and t == 0:
                        pe.wait_ge(d_low, 3)
                    products = [(m, *parts) for m in range(BLOCKS1) for parts in ((0, 0), (0, 1), (1, 0))]
                    for n, (m, r, w) in enumerate(products):
                        last = nc.tensor.matmul(ps_y[:, 0:D], hT[r][:, k, m, :], d_parts[w][:, m, :],
                                                start=(n == 0), stop=(n == len(products) - 1))
                    last.then_inc(y_done, 1)

                def step(i, j):
                    if exists(i, j):
                        hidden(i, j)
                    if j % E == 4 and exists(i, j + 4):
                        turn_rows(i, j + 4)
                    for n, j0 in groups_due(j):
                        if exists(i, j0):
                            turn_group(i, j0, n)
                    if (j - down_at) % E == 0 and exists(i, j - down_at):
                        down(i, j - down_at)

                turn_rows(0, 0)
                turn.run(pe, step)

            @block.scalar
            def _(act):
                def copy_rows(i, j):
                    t, k = tile_of(i, j), j // E % 2
                    act.wait_ge(rows_turned, t + 1)
                    wait(act, h_done, E * (t - 1))
                    nc.scalar.copy(xT[0][:, k].rearrange("p c n -> p (c n)"), ps_x[:, 0:D]).then_inc(xT_high, 1)

                def silu(i, j):
                    u = BODY2 * i + j
                    act.wait_ge(h_done, u + 1)
                    wait(act, hid_ready, u - 3)
                    nc.scalar.activation(act_g[:, j % 4, :], ps_h[j % 4][:, 0:HID1], ACT.Silu).then_inc(silu_ready, 1)

                def copy_group(i, j, n):
                    t, k = tile_of(i, j), j // E % 2
                    lo, hi = GROUP_BLOCKS[n]
                    act.wait_ge(turned, 3 * t + n + 1)
                    wait(act, y_done, t - 1)
                    nc.scalar.copy(hT[0][:, k, lo:hi, :], ps_t[(3 * (j // E) + n) % 2][:, 0:hi - lo, :]).then_inc(hT_high, 1)

                def step(i, j):
                    if j % E == 4 and exists(i, j + 4):
                        copy_rows(i, j + 4)
                    if exists(i, j):
                        silu(i, j)
                    for n, j0 in groups_due(j):
                        if exists(i, j0):
                            copy_group(i, j0, n)

                copy_rows(0, 0)
                act.wait_ge(d_loaded, 16)
                for lo, hi in GROUP_BLOCKS:
                    nc.scalar.copy(d_parts[0][:, lo:hi, :], w_d[:, lo:hi, :]).then_inc(d_high, 1)
                turn.run(act, step)

            @block.vector
            def _(dve):
                def stage_rows(i, j):
                    t = tile_of(i, j)
                    wait(dve, rows_turned, t - 1)
                    nc.vector.tensor_scalar(rows[:, j // E % 2, :], x_all[:, t, :], mean_var[:, t, 0:1], column(rstd, t),
                                            ALU.subtract, ALU.mult).then_inc(rows_ready, 1)

                def part_rows(i, j):
                    t, k = tile_of(i, j), j // E % 2
                    dve.wait_ge(xT_high, t + 1)
                    nc.vector.tensor_tensor(xT[1][:, k].rearrange("p c n -> p (c n)"), ps_x[:, 0:D],
                                            xT[0][:, k].rearrange("p c n -> p (c n)"), ALU.subtract).then_inc(xT_ready, 1)

                def gated(i, j):
                    u, t, k, e = BODY2 * i + j, tile_of(i, j), j // E, j % E
                    dve.wait_ge(silu_ready, u + 1)
                    wait(dve, turned, 3 * (t - 1))
                    w = combine[:].rearrange("p t e -> p (t e)")
                    w = w[:, E * t + e:E * t + e + 1] if isinstance(t, int) else w[:, bass.ds(E * t + e, 1)]
                    nc.vector.scalar_tensor_tensor(hid[:, k, e * HID1:(e + 1) * HID1], act_g[:, j % 4, :], w,
                                                   ps_h[j % 4][:, HID1:2 * HID1], ALU.mult, ALU.mult).then_inc(hid_ready, 1)

                def part_group(i, j, n):
                    t, k = tile_of(i, j), j // E % 2
                    lo, hi = GROUP_BLOCKS[n]
                    dve.wait_ge(hT_high, 3 * t + n + 1)
                    nc.vector.tensor_tensor(hT[1][:, k, lo:hi, :], ps_t[(3 * (j // E) + n) % 2][:, 0:hi - lo, :],
                                            hT[0][:, k, lo:hi, :], ALU.subtract).then_inc(hT_ready, 1)

                def update(i, j):
                    t = tile_of(i, j)
                    dve.wait_ge(y_done, t + 1)
                    nc.vector.tensor_tensor(x_all[:, t, :], x_all[:, t, :], ps_y[:, 0:D], ALU.add).then_inc(x_ready, 1)

                def step(i, j):
                    if exists(i, j):
                        gated(i, j)
                    if j % E == 2 and exists(i, j + 6):
                        stage_rows(i, j + 6)
                    if j % E == 5 and exists(i, j + 3):
                        part_rows(i, j + 3)
                    for n, j0 in groups_due(j):
                        if exists(i, j0):
                            part_group(i, j0, n)
                    if (j - down_at) % E == 0 and exists(i, j - down_at):
                        update(i, j - down_at)

                stage_rows(0, 0)
                part_rows(0, 0)
                turn.run(dve, step)


def second_experts(nc, x_all, mean_var, rstd, ident, gate_w, w_gu, w_d, gu_loaded, d_loaded, out):
    with ExitStack() as ctx:
        s = Scope(nc, ctx)
        logits = s.sb("logits_e", [P, TILES, E])
        combine = s.sb("combine", [P, TILES, E])
        gu_parts = [s.sb(f"gu_{n}", [P, 2, E, 2 * HID1], F32R) for n in ("high", "low")]
        high_made = s.sem("gate_up_high")
        low_made = s.sem("gate_up_low")
        logits_stage(nc, "e", x_all, mean_var, rstd, ident, gate_w, None, logits)
        second_routing(nc, logits, combine, w_gu, gu_parts, gu_loaded, high_made, low_made)
        second_ffn(nc, x_all, mean_var, rstd, ident, w_gu, gu_parts, high_made, low_made, w_d, d_loaded, combine, out)


def build(nc, a, out):
    SPENT.clear()
    table = nc.dram_tensor("expert_rows", [SLOTS, D], F32, kind="Internal").ap()
    results = nc.dram_tensor("expert_results", [SLOTS, D], F32, kind="Internal").ap()
    with ExitStack() as ctx:
        s = Scope(nc, ctx)
        x_all = s.sb("x_all", [P, TILES, D])
        ident = s.sb("ident", [P, P])
        mean_var = s.sb("mean_var", [P, TILES, 2])
        stats = s.sb("stats", [P, TILES, 6])
        rstd = s.sb("rstd", [P, TILES])
        o_w = s.sb("o_w", [P, H1, D])
        gates = [s.sb(f"gate_w{n}", [P, 2, E]) for n in range(2)]
        gates_loaded = s.sem("gates_loaded")
        second_loaded = s.sem("second_attention_loaded")
        gather_at = s.sb("gather_at", [P, TILES], I32)
        gate = s.sb("gate_f", [P, TILES])
        q_w = s.sb("q_w", [P, 2, H1 * DH])
        kv_w = s.sb("kv_w", [P, 4, 2, GROUPS * DH])
        late = ctx.enter_context(ExitStack())

        def load_projections(sp):
            load_second_projections(sp, a["L1_xattn_wq"], a["L1_xattn_wk"], a["L1_xattn_wv"], a["L1_xattn_wk_ctx"],
                                    a["L1_xattn_wv_ctx"], q_w, kv_w, second_loaded)

        with ExitStack() as first:
            f = Scope(nc, first)
            w13 = f.sb("w13", [P, 2, E, 2 * HID0])
            w2 = f.sb("w2", [P, 3, E, D])
            first_loaded = f.sem("first_experts_loaded")
            table_zeroed = f.sem("table_zeroed")
            with ExitStack() as attention:
                t = Scope(nc, attention)
                score_w = t.sb("score_w", [P, H0 // 2, 2, P], F32R)
                out_w = t.sb("out_w", [P, H0 // 2, E0])
                bias0 = t.sb("bias0", [P, 1])
                ctx_tile = t.sb("ctx_tile", [P, 2, D])
                ctx_twice = t.sb("ctx_twice", [P, 2, 2, D])
                ctx_loaded = [t.sem(f"ctx_loaded{k}") for k in range(2)]
                zero = t.sb("zero", [P, D])
                zero_made = t.sem("zero_made")
                with nc.Block() as block:

                    @block.gpsimd
                    def _(pool):
                        nc.gpsimd.memset(zero[:], 0.0).then_inc(zero_made, 1)

                def load_first_context(sp):
                    for k in range(2):
                        load_context(sp, a["ctx_2048"], k, k, ctx_tile, ctx_twice, ctx_loaded)

                first_weights(nc, a["L0_xattn_W_q"], a["L0_xattn_W_kv"], a["L0_xattn_W_out"], a["L0_xattn_b_out"],
                              a["x"], x_all, stats, ident, score_w, out_w, bias0,
                              ((gates[0], a["L0_ffn_Wg"]), (gates[1], a["L1_ffn_gate_w"])), gates_loaded, load_first_context)
                rows_rstd_stage(nc, stats, mean_var, rstd, "a")

                def prefetch_experts(sp):
                    load_first_experts(sp, a["L0_ffn_W1"], a["L0_ffn_W3"], a["L0_ffn_W2"], w13, w2, first_loaded)
                    sp.wait_ge(zero_made, 1)
                    for n in range(TILES):
                        sp.dma_start(table[n * P:(n + 1) * P, :], zero[:]).then_inc(table_zeroed, 16)
                    sp.wait_ge(table_zeroed, 16 * TILES)

                first_attention(nc, a["ctx_2048"], ctx_tile, ctx_twice, ctx_loaded, x_all, stats, mean_var, rstd, ident, score_w, out_w, bias0, o_w,
                                prefetch_experts)
            rows_rstd_stage(nc, stats, mean_var, rstd, "b")
            first_experts(nc, x_all, mean_var, rstd, ident, gates[0], gates_loaded,
                          (a["L0_ffn_sw1"], a["L0_ffn_sw3"], a["L0_ffn_sw2"]), w13, w2, first_loaded,
                          q_w, kv_w, load_projections,
                          table, results, table_zeroed, gather_at, gate, late,
                          lambda sp: load_second_output(sp, a["L1_xattn_wo"], o_w, second_loaded),
                          (second_loaded,))
        with ExitStack() as attention:
            t = Scope(nc, attention)
            tables = t.sb("rope_tables", [P, 3, 2, DH])
            mask = t.sb("mask", [P, 4, S], mybir.dt.bfloat16)
            q_parts = [t.sb(f"q_{n}", [P, 2, H1 * DH], F32R) for n in ("high", "low")]
            kv_parts = [t.sb(f"kv_{n}", [P, 4, 2, GROUPS * DH], F32R) for n in ("high", "low")]
            rows = t.sb("a_rows", [P, 2, 2, D])
            ctx_loaded = [t.sem(f"a_ctx_loaded{k}") for k in range(2)]

            def load_second_context(sp):
                for k in range(2):
                    sp.dma_start(rows[:, k, 1, :], a["ctx_2048"].rearrange("(t b) d n -> (b d) t n", b=2)[:, k, :]
                                 ).then_inc(ctx_loaded[k], 16)

            between_layers(nc, x_all, stats, mean_var, rstd, results, gather_at, gate, a["rope"], a["L1_xattn_q_norm_w"],
                           a["L1_xattn_k_norm_w"], tables, mask, q_w, kv_w, second_loaded, q_parts, kv_parts,
                           load_second_context, (second_loaded, *ctx_loaded))
            late.close()
            second_attention(nc, a["ctx_2048"], rows, ctx_loaded, x_all, stats, mean_var, rstd, ident, q_parts, kv_parts,
                             q_w, kv_w, o_w, tables, mask)
        w_gu = [w[:, 0:E * 2 * HID1].rearrange("p (e f) -> p e f", e=E)
                for w in (q_w[:].rearrange("p k n -> p (k n)"), kv_w[:].rearrange("p w k n -> p (w k n)"))]
        w_d = o_w[:, 0:BLOCKS1, :]
        gu_loaded = s.sem("gate_up_loaded")
        d_loaded = s.sem("down_loaded")
        rows_rstd_stage(nc, stats, mean_var, rstd, "d",
                        lambda sp: load_second_experts(sp, a["L1_ffn_w_gate"], a["L1_ffn_w_up"], a["L1_ffn_w_down"],
                                                       w_gu, w_d, gu_loaded, d_loaded))
        second_experts(nc, x_all, mean_var, rstd, ident, gates[1], w_gu, w_d, gu_loaded, d_loaded, out)


def rope_angles():
    half = np.arange(0, DH, 2, dtype=np.float64) / DH
    angle = np.outer(np.arange(S, dtype=np.float64), 1.0 / 10000.0 ** half)
    cos, sin = np.cos(angle), np.sin(angle)
    return np.stack([np.concatenate([cos, cos], -1), np.concatenate([-sin, sin], -1)]).astype(np.float32)


def kernel(**inputs):
    import concourse.bacc as bacc
    from concourse.bass_utils import run_bass_kernel_spmd

    nc = bacc.Bacc("TRN2", target_bir_lowering=False, num_devices=1)
    arrays = {name: np.ascontiguousarray(a) for name, a in inputs.items()}
    arrays["rope"] = rope_angles()
    args = {name: nc.dram_tensor(name, a.shape, mybir.dt.from_np(a.dtype), kind="ExternalInput").ap()
            for name, a in arrays.items()}
    out = nc.dram_tensor("out", (NB, S, D), F32, kind="ExternalOutput").ap()
    build(nc, args, out)
    r = run_bass_kernel_spmd(nc, [arrays], core_ids=[0])
    return r.results[0]["out"]
```
